# Optimizing a Trainium2 kernel written in Bass

```python
import numpy as np
import jax
import jax.numpy as jnp

def _softmax(x, axis=-1):
    return jax.nn.softmax(x, axis=axis)

def _gelu(x):
    return jax.nn.gelu(x, approximate=True)

def _silu(x):
    return jax.nn.silu(x)

def _sigmoid(x):
    return jax.nn.sigmoid(x)

def _layernorm(x, axis=-1, eps=1e-05):
    m = jnp.mean(x, axis=axis, keepdims=True)
    v = jnp.var(x, axis=axis, keepdims=True)
    return (x - m) / jnp.sqrt(v + eps)

def _scatter_add(tgt, idx, src, axis=0):
    return tgt.at[idx].add(src)

def _segment_sum(src, seg, n):
    return jax.ops.segment_sum(src, seg, n)
kernel_name = 'mk_adaln_d2_jaxref_r4_59652e'

def setup_inputs(seed: int=0):
    np.random.seed(seed)
    _w = jnp.asarray

    def _L0_attn_setup():
        import jax, jax.numpy as jnp
        import numpy as np
        from jax import lax
        D = 256
        ORDER = 2
        FILT = 64
        EMB = 3
        INNER = D * (ORDER + 1)
        DF = D * (ORDER - 1)
        L_MAX = 512

        def _pos_emb(L):
            t = jnp.linspace(0.0, 1.0, L)[:, None]
            tr = jnp.linspace(0.0, L - 1.0, L)[:, None]
            w = 2.0 * np.pi * tr / L
            f = jnp.array([0.0001], jnp.float32)[None, :]
            z = jnp.concatenate([t, jnp.cos(f * w), -jnp.sin(f * w)], axis=-1)
            return (z, t)

        def _decay(t):
            max_d = np.log(0.01) / 0.3
            min_d = np.log(0.01) / 1.5
            deltas = jnp.linspace(min_d, max_d, DF)[None, :]
            return jnp.exp(-t * jnp.abs(deltas))
        key = jax.random.key(seed)
        ks = jax.random.split(key, 16)
        s = 0.02
        return {'u': jax.random.normal(ks[0], (4, L_MAX, D), jnp.float32), 'in_w': jax.random.normal(ks[1], (D, INNER), jnp.float32) * s, 'in_b': jnp.zeros((INNER,), jnp.float32), 'short_w': jax.random.normal(ks[2], (INNER, 3), jnp.float32) * 0.3, 'short_b': jnp.zeros((INNER,), jnp.float32), 'mlp_w1': jax.random.normal(ks[3], (EMB, FILT), jnp.float32) * 0.3, 'mlp_b1': jnp.zeros((FILT,), jnp.float32), 'mlp_w2': jax.random.normal(ks[4], (FILT, FILT), jnp.float32) * 0.1, 'mlp_b2': jnp.zeros((FILT,), jnp.float32), 'mlp_w3': jax.random.normal(ks[5], (FILT, FILT), jnp.float32) * 0.1, 'mlp_b3': jnp.zeros((FILT,), jnp.float32), 'mlp_wo': jax.random.normal(ks[6], (FILT, DF), jnp.float32) * 0.1, 'freq': jnp.ones((1, FILT), jnp.float32), 'filt_bias': jax.random.normal(ks[7], (DF,), jnp.float32), 'out_w': jax.random.normal(ks[8], (D, D), jnp.float32) * s, 'out_b': jnp.zeros((D,), jnp.float32)}
    _L0_attn_in = _L0_attn_setup()

    def _L0_ffn_setup():
        import jax, jax.numpy as jnp
        import numpy as np

        def _binarize(w):
            alpha = jax.lax.stop_gradient(jnp.mean(jnp.abs(w), axis=1, keepdims=True))
            bw = alpha * jnp.sign(w)
            return w + jax.lax.stop_gradient(bw - w)
        key = jax.random.key(seed)
        k1, k2, k3, k4, k5 = jax.random.split(key, 5)
        D, H = (256, 1024)
        x = jax.random.normal(k1, (64, 196, D), dtype=jnp.float32)
        w1 = jax.random.normal(k2, (H, D), dtype=jnp.float32) * 0.02
        b1 = jax.random.normal(k3, (H,), dtype=jnp.float32) * 0.02
        w2 = jax.random.normal(k4, (D, H), dtype=jnp.float32) * 0.02
        b2 = jax.random.normal(k5, (D,), dtype=jnp.float32) * 0.02
        return {'x': x, 'w1': w1, 'b1': b1, 'w2': w2, 'b2': b2}
    _L0_ffn_in = _L0_ffn_setup()
    _L0_c = _w((lambda *s: np.random.randn(*s).astype(np.float32) * 0.05)(4, 256))
    _L0_wmod = _w((lambda *s: np.random.randn(*s).astype(np.float32) * 0.05)(256, 6 * 256) * 256 ** (-0.5))

    def _L1_attn_setup():
        import jax, jax.numpy as jnp
        import numpy as np
        B, S, HID = (1, 512, 256)
        H, HKV, D = (16, 4, 64)
        THETA = 10000.0

        def _rope_tables(seq_len, head_dim):
            inv_freq = 1.0 / THETA ** (jnp.arange(0, head_dim, 2, dtype=jnp.float32) / head_dim)
            freqs = jnp.arange(seq_len, dtype=jnp.float32)[:, None] * inv_freq[None, :]
            emb = jnp.concatenate([freqs, freqs], axis=-1)
            return (jnp.cos(emb)[:, 0::2], jnp.sin(emb)[:, 0::2])

        def _apply_rope(x, cos, sin):
            xe, xo = (x[..., 0::2], x[..., 1::2])
            re = xe * cos - xo * sin
            ro = xe * sin + xo * cos
            return jnp.stack([re, ro], axis=-1).reshape(x.shape)
        key = jax.random.key(seed)
        k0, k1, k2, k3, k4 = jax.random.split(key, 5)
        return {'hidden_states': jax.random.normal(k0, (B, S, HID), dtype=jnp.float32), 'Wq': jax.random.normal(k1, (HID, H * D), dtype=jnp.float32) * 0.02, 'Wk': jax.random.normal(k2, (HID, HKV * D), dtype=jnp.float32) * 0.02, 'Wv': jax.random.normal(k3, (HID, HKV * D), dtype=jnp.float32) * 0.02, 'Wo': jax.random.normal(k4, (H * D, HID), dtype=jnp.float32) * 0.02}
    _L1_attn_in = _L1_attn_setup()

    def _L1_ffn_setup():
        import jax, jax.numpy as jnp
        import numpy as np
        TOP_K = 2
        key = jax.random.key(seed)
        ks = jax.random.split(key, 6)
        B, S, D, E = (8, 1024, 256, 8)
        s = 1.0 / np.sqrt(D)
        return {'x': jax.random.normal(ks[0], (B, S, D), dtype=jnp.float32), 'Wr': jax.random.normal(ks[1], (D, E), dtype=jnp.float32) * s, 'br': jnp.zeros((E,), dtype=jnp.float32), 'W1': jax.random.normal(ks[2], (E, D, D), dtype=jnp.float32) * s, 'b1': jnp.zeros((E, D), dtype=jnp.float32), 'W2': jax.random.normal(ks[3], (E, D, D), dtype=jnp.float32) * s, 'b2': jnp.zeros((E, D), dtype=jnp.float32)}
    _L1_ffn_in = _L1_ffn_setup()
    _L1_c = _w((lambda *s: np.random.randn(*s).astype(np.float32) * 0.05)(4, 256))
    _L1_wmod = _w((lambda *s: np.random.randn(*s).astype(np.float32) * 0.05)(256, 6 * 256) * 256 ** (-0.5))
    _d = {'L0_attn_u': _L0_attn_in['u'], 'L0_attn_in_w': _L0_attn_in['in_w'], 'L0_attn_in_b': _L0_attn_in['in_b'], 'L0_attn_short_w': _L0_attn_in['short_w'], 'L0_attn_short_b': _L0_attn_in['short_b'], 'L0_attn_mlp_w1': _L0_attn_in['mlp_w1'], 'L0_attn_mlp_b1': _L0_attn_in['mlp_b1'], 'L0_attn_mlp_w2': _L0_attn_in['mlp_w2'], 'L0_attn_mlp_b2': _L0_attn_in['mlp_b2'], 'L0_attn_mlp_w3': _L0_attn_in['mlp_w3'], 'L0_attn_mlp_b3': _L0_attn_in['mlp_b3'], 'L0_attn_mlp_wo': _L0_attn_in['mlp_wo'], 'L0_attn_freq': _L0_attn_in['freq'], 'L0_attn_filt_bias': _L0_attn_in['filt_bias'], 'L0_attn_out_w': _L0_attn_in['out_w'], 'L0_attn_out_b': _L0_attn_in['out_b'], 'L0_ffn_w1': _L0_ffn_in['w1'], 'L0_ffn_b1': _L0_ffn_in['b1'], 'L0_ffn_w2': _L0_ffn_in['w2'], 'L0_ffn_b2': _L0_ffn_in['b2'], 'L0_c': _L0_c, 'L0_wmod': _L0_wmod, 'L1_attn_Wq': _L1_attn_in['Wq'], 'L1_attn_Wk': _L1_attn_in['Wk'], 'L1_attn_Wv': _L1_attn_in['Wv'], 'L1_attn_Wo': _L1_attn_in['Wo'], 'L1_ffn_Wr': _L1_ffn_in['Wr'], 'L1_ffn_br': _L1_ffn_in['br'], 'L1_ffn_W1': _L1_ffn_in['W1'], 'L1_ffn_b1': _L1_ffn_in['b1'], 'L1_ffn_W2': _L1_ffn_in['W2'], 'L1_ffn_b2': _L1_ffn_in['b2'], 'L1_c': _L1_c, 'L1_wmod': _L1_wmod}
    _x0 = _d['L0_attn_u']
    _d['L0_attn_u'] = jax.random.normal(jax.random.fold_in(jax.random.key(seed), 1), (4, 1024, 256), dtype=_x0.dtype)
    del _x0
    return _d

def reference(L0_attn_u, L0_attn_in_w, L0_attn_in_b, L0_attn_short_w, L0_attn_short_b, L0_attn_mlp_w1, L0_attn_mlp_b1, L0_attn_mlp_w2, L0_attn_mlp_b2, L0_attn_mlp_w3, L0_attn_mlp_b3, L0_attn_mlp_wo, L0_attn_freq, L0_attn_filt_bias, L0_attn_out_w, L0_attn_out_b, L0_ffn_w1, L0_ffn_b1, L0_ffn_w2, L0_ffn_b2, L0_c, L0_wmod, L1_attn_Wq, L1_attn_Wk, L1_attn_Wv, L1_attn_Wo, L1_ffn_Wr, L1_ffn_br, L1_ffn_W1, L1_ffn_b1, L1_ffn_W2, L1_ffn_b2, L1_c, L1_wmod):

    def _L0_attn_ref(u, in_w, in_b, short_w, short_b, mlp_w1, mlp_b1, mlp_w2, mlp_b2, mlp_w3, mlp_b3, mlp_wo, freq, filt_bias, out_w, out_b):
        import jax, jax.numpy as jnp
        import numpy as np
        from jax import lax
        D = 256
        ORDER = 2
        FILT = 64
        EMB = 3
        INNER = D * (ORDER + 1)
        DF = D * (ORDER - 1)
        L_MAX = 512

        def _pos_emb(L):
            t = jnp.linspace(0.0, 1.0, L)[:, None]
            tr = jnp.linspace(0.0, L - 1.0, L)[:, None]
            w = 2.0 * np.pi * tr / L
            f = jnp.array([0.0001], jnp.float32)[None, :]
            z = jnp.concatenate([t, jnp.cos(f * w), -jnp.sin(f * w)], axis=-1)
            return (z, t)

        def _decay(t):
            max_d = np.log(0.01) / 0.3
            min_d = np.log(0.01) / 1.5
            deltas = jnp.linspace(min_d, max_d, DF)[None, :]
            return jnp.exp(-t * jnp.abs(deltas))
        B, L, _ = u.shape
        up = jnp.einsum('bld,de->ble', u, in_w) + in_b
        up = up.transpose(0, 2, 1)
        uc = lax.conv_general_dilated(up, short_w[:, None, :], (1,), [(2, 2)], feature_group_count=INNER, dimension_numbers=('NCH', 'OIH', 'NCH'))
        uc = uc[..., :L] + short_b[None, :, None]
        x0, x1, v = (uc[:, :D], uc[:, D:2 * D], uc[:, 2 * D:])
        z, t = _pos_emb(L)
        h = jnp.sin(freq * (z @ mlp_w1 + mlp_b1))
        h = jnp.sin(freq * (h @ mlp_w2 + mlp_b2))
        h = jnp.sin(freq * (h @ mlp_w3 + mlp_b3))
        h = h @ mlp_wo
        k = (h * _decay(t)).T
        vx = v * x1
        n = 2 * L
        y = jnp.fft.irfft(jnp.fft.rfft(vx, n=n) * jnp.fft.rfft(k, n=n), n=n)[..., :L]
        v = y + vx * filt_bias[None, :, None]
        yv = (v * x0).transpose(0, 2, 1)
        return jnp.einsum('bld,de->ble', yv, out_w) + out_b

    def _L0_ffn_ref(x, w1, b1, w2, b2):
        import jax, jax.numpy as jnp
        import numpy as np

        def _binarize(w):
            alpha = jax.lax.stop_gradient(jnp.mean(jnp.abs(w), axis=1, keepdims=True))
            bw = alpha * jnp.sign(w)
            return w + jax.lax.stop_gradient(bw - w)
        bw1 = _binarize(w1)
        h = jnp.einsum('bsd,hd->bsh', x, bw1) + b1
        h = jax.nn.gelu(h, approximate=False)
        bw2 = _binarize(w2)
        out = jnp.einsum('bsh,dh->bsd', h, bw2) + b2
        return out

    def _L1_attn_ref(hidden_states, Wq, Wk, Wv, Wo):
        import jax, jax.numpy as jnp
        import numpy as np
        B, S, HID = (1, 512, 256)
        H, HKV, D = (16, 4, 64)
        THETA = 10000.0

        def _rope_tables(seq_len, head_dim):
            inv_freq = 1.0 / THETA ** (jnp.arange(0, head_dim, 2, dtype=jnp.float32) / head_dim)
            freqs = jnp.arange(seq_len, dtype=jnp.float32)[:, None] * inv_freq[None, :]
            emb = jnp.concatenate([freqs, freqs], axis=-1)
            return (jnp.cos(emb)[:, 0::2], jnp.sin(emb)[:, 0::2])

        def _apply_rope(x, cos, sin):
            xe, xo = (x[..., 0::2], x[..., 1::2])
            re = xe * cos - xo * sin
            ro = xe * sin + xo * cos
            return jnp.stack([re, ro], axis=-1).reshape(x.shape)
        b, s, _ = hidden_states.shape
        q = (hidden_states @ Wq).reshape(b, s, H, D).transpose(0, 2, 1, 3)
        k = (hidden_states @ Wk).reshape(b, s, HKV, D).transpose(0, 2, 1, 3)
        v = (hidden_states @ Wv).reshape(b, s, HKV, D).transpose(0, 2, 1, 3)
        cos, sin = _rope_tables(s, D)
        q = _apply_rope(q, cos, sin)
        k = _apply_rope(k, cos, sin)
        G = H // HKV
        qg = q.reshape(b, HKV, G, s, D)
        scale = jnp.float32(D) ** (-0.5)
        scores = jnp.einsum('bkgqd,bkpd->bkgqp', qg, k) * scale
        causal = jnp.tril(jnp.ones((s, s), dtype=bool))
        scores = jnp.where(causal, scores, jnp.float32(-1e+30))
        probs = jax.nn.softmax(scores, axis=-1)
        out = jnp.einsum('bkgqp,bkpd->bkgqd', probs, v).reshape(b, H, s, D)
        out = out.transpose(0, 2, 1, 3).reshape(b, s, H * D)
        return out @ Wo

    def _L1_ffn_ref(x, Wr, br, W1, b1, W2, b2):
        import jax, jax.numpy as jnp
        import numpy as np
        TOP_K = 2
        k = TOP_K
        scores0 = x[:, 0, :] @ Wr + br
        _, idx = jax.lax.top_k(scores0, k)
        W1g, b1g = (W1[idx], b1[idx])
        W2g, b2g = (W2[idx], b2[idx])
        h = jnp.einsum('bsd,bkde->bkse', x, W1g) + b1g[:, :, None, :]
        h = jax.nn.gelu(h, approximate=False)
        o = jnp.einsum('bkse,bkef->bksf', h, W2g) + b2g[:, :, None, :]
        return jnp.sum(o, axis=1) / k
    x = L0_attn_u
    mod = (_silu(L0_c) @ L0_wmod).reshape(L0_c.shape[0], 6, 1, -1)
    sa, ca, ga, sb, cb, gb = (mod[:, 0], mod[:, 1], mod[:, 2], mod[:, 3], mod[:, 4], mod[:, 5])
    ga = (2 * (ga >= 0) - 1) * jnp.maximum(jnp.abs(ga), 0.25)
    gb = (2 * (gb >= 0) - 1) * jnp.maximum(jnp.abs(gb), 0.25)
    h = _layernorm(x, axis=-1) * (1 + ca) + sa
    x = x + ga * _L0_attn_ref(h, L0_attn_in_w, L0_attn_in_b, L0_attn_short_w, L0_attn_short_b, L0_attn_mlp_w1, L0_attn_mlp_b1, L0_attn_mlp_w2, L0_attn_mlp_b2, L0_attn_mlp_w3, L0_attn_mlp_b3, L0_attn_mlp_wo, L0_attn_freq, L0_attn_filt_bias, L0_attn_out_w, L0_attn_out_b)
    h = _layernorm(x, axis=-1) * (1 + cb) + sb
    x = x + gb * _L0_ffn_ref(h, L0_ffn_w1, L0_ffn_b1, L0_ffn_w2, L0_ffn_b2)
    mod = (_silu(L1_c) @ L1_wmod).reshape(L1_c.shape[0], 6, 1, -1)
    sa, ca, ga, sb, cb, gb = (mod[:, 0], mod[:, 1], mod[:, 2], mod[:, 3], mod[:, 4], mod[:, 5])
    ga = (2 * (ga >= 0) - 1) * jnp.maximum(jnp.abs(ga), 0.25)
    gb = (2 * (gb >= 0) - 1) * jnp.maximum(jnp.abs(gb), 0.25)
    h = _layernorm(x, axis=-1) * (1 + ca) + sa
    x = x + ga * _L1_attn_ref(h, L1_attn_Wq, L1_attn_Wk, L1_attn_Wv, L1_attn_Wo)
    h = _layernorm(x, axis=-1) * (1 + cb) + sb
    x = x + gb * _L1_ffn_ref(h, L1_ffn_Wr, L1_ffn_br, L1_ffn_W1, L1_ffn_b1, L1_ffn_W2, L1_ffn_b2)
    return x

_drawn_inputs = setup_inputs


def setup_inputs(seed=0):
    import zlib

    import numpy as np

    out = dict(_drawn_inputs(seed))
    spreads = {'L0_attn_in_b': (0.0, 0.1),
     'L0_attn_short_b': (0.0, 0.1),
     'L0_attn_mlp_b1': (0.0, 0.1),
     'L0_attn_mlp_b2': (0.0, 0.1),
     'L0_attn_mlp_b3': (0.0, 0.1),
     'L0_attn_freq': (1.0, 0.2),
     'L0_attn_out_b': (0.0, 0.1),
     'L1_ffn_br': (0.0, 0.1),
     'L1_ffn_b1': (0.0, 0.1),
     'L1_ffn_b2': (0.0, 0.1)}
    factors = {}
    for name, (base, spread) in spreads.items():
        noise = np.random.default_rng([zlib.crc32(name.encode()), seed]).standard_normal(out[name].shape)
        drawn = base * np.exp(spread * noise) if base else spread * noise
        out[name] = jnp.asarray(drawn.astype(out[name].dtype))
    for name, factor in factors.items():
        out[name] = (out[name] * factor).astype(out[name].dtype)
    return out
```

```python
from contextlib import ExitStack

import numpy as np

import concourse.bass as bass
from concourse import mybir

F32 = mybir.dt.float32
F32R = mybir.dt.float32r
U32 = mybir.dt.uint32
ALU = mybir.AluOpType
ACT = mybir.ActivationFunctionType
AX = mybir.AxisListType.X

P = 128
B, L, D = 4, 1024, 256
NT = L // P
ND = D // P
HALF = 512
NHALF = L // HALF
EPS = 1e-5

S = 256
NB = L // S
ST = S // P
FILT = 64
EMB = 3
INNER = 3 * D

HID = 1024
NH1 = HID // P

HEADS, KV, HD = 16, 4, 64
GQ = HEADS // KV
GW = (GQ + 2) * HD
QK = (GQ + 1) * HD
SCALE = HD ** -0.5
MASKED = -1e30
QRING = 3
PRING = 8
LEAD = 2

EXPERTS, TOPK = 8, 2

E_ORDER = (4, 5, 2, 3, 0, 1)
PAIRS_DONE = (NB - 1, NB * (NB - 1) // 2)
Y_DONE = (0, 1, 4, 6)
NLOADED = 21

PI_DOWN = 3.1415925
TWO_PI_HI = 6.28125
TWO_PI_LO = float(2 * np.pi - 6.28125)
ROUND = float(1.5 * 2 ** 23)


def shape_constants():
    n = np.arange(2 * S)[:, None]
    f = np.arange(S)[None, :] + 0.5
    ang = np.pi * ((n * (2 * f)) % (4 * S)) / (2 * S) * 1.0
    fwd = np.concatenate([np.cos(ang), np.sin(ang)], axis=1)
    fwd = fwd.reshape(2, ST, P, 2 * S).transpose(2, 0, 1, 3)
    inv = np.concatenate([np.cos(ang[S:]), np.sin(ang[S:])], axis=1).T / S
    inv = inv.reshape(2 * ST, P, S).transpose(1, 0, 2)
    t = np.linspace(0.0, 1.0, L, dtype=np.float32)[:, None]
    tr = np.linspace(0.0, L - 1.0, L, dtype=np.float32)[:, None]
    w = (2.0 * np.pi * tr / L).astype(np.float32)
    fr = np.float32(0.0001)
    z = np.concatenate([t, np.cos(fr * w), -np.sin(fr * w)], axis=-1)
    deltas = np.linspace(np.log(0.01) / 1.5, np.log(0.01) / 0.3, D, dtype=np.float32)[None, :]
    decay = np.exp(-t * np.abs(deltas)).reshape(NT, P, D).transpose(1, 0, 2)
    inv_freq = np.float32(1.0) / np.float32(10000.0) ** (np.arange(0, HD, 2, dtype=np.float32) / np.float32(HD))
    freqs = np.arange(L, dtype=np.float32)[:, None] * inv_freq[None, :]
    emb = np.concatenate([freqs, freqs], axis=-1)
    cos, sin = np.cos(emb)[:, 0::2], np.sin(emb)[:, 0::2]
    rope = np.stack([cos, sin], axis=1).reshape(NT, P, 2, HD // 2).transpose(1, 0, 2, 3)
    c = lambda a: np.ascontiguousarray(a, dtype=np.float32)
    return {"fwd": c(fwd), "inv": c(inv), "zT": c(z.T), "decay": c(decay), "rope": c(rope)}


def adaln_hyena_binffn_gqa_moe(nc, d, out, gate_scratch, kf_scratch):
    es = ExitStack()
    with es:
        def sb(name, shape, dt=F32, stack=es):
            return stack.enter_context(nc.sbuf_tensor(name, shape, dt))

        def sem(name):
            return es.enter_context(nc.semaphore(name))

        x = sb("x", [P, NT, D])
        ident = sb("ident", [P, P])
        in_w = sb("in_w", [P, ND, INNER])
        out_w = sb("out_w", [P, ND, D])
        sgn1 = sb("sgn1", [P, ND, HID])
        sgn2 = sb("sgn2", [P, NH1, D])
        fwd = sb("fwd", [P, ST, 2 * S])
        inv = sb("inv", [P, 2 * ST, S])
        wqkv = sb("wqkv", [P, ND, KV, GW])
        wo = sb("wo", [P, HEADS * HD // P, D])
        rope = sb("rope", [P, NT, 2, HD // 2])
        mrow = sb("mrow", [P, L])
        wr = sb("wr", [P, ND, EXPERTS])
        br = sb("br", [1, EXPERTS])
        in_b = sb("in_b", [P, INNER // P])
        short_w = sb("short_w", [P, INNER // P, 3])
        short_b = sb("short_b", [P, INNER // P])
        filt_b = sb("filt_b", [P, ND])
        ffn_b1 = sb("ffn_b1", [P, NH1])
        alpha1 = sb("alpha1", [P, NH1])
        rows = sb("rows", [P, 2, D])
        alpha2 = sb("alpha2", [P, D])
        modT = sb("modT", [P, 2, 4, ND, B])
        modb = sb("modb", [P, 2, 4, ND])
        gates = sb("gates", [P, 4, D])
        terms = sb("terms", [P, 3, D])
        escale = sb("escale", [P, 2, D])
        neghalf = sb("neghalf", [P, NT])
        stat = sb("stat", [P, NT, 6])
        mv = sb("mv", [P, NT, 2])
        var = sb("var", [P, NT])
        rstd = sb("rstd", [P, NT])
        hT = sb("hT", [P, ND, L])

        with ExitStack() as a:
            fwd_old = sb("fwd_old", [P, ST, 2 * S], F32, a)
            kern = sb("kern", [P, NT, D], F32, a)
            decay = sb("decay", [P, NT, D], F32, a)
            w1rows = sb("w1rows", [P, NH1, D], F32, a)
            w1T = sb("w1T", [P, ND, HID], F32, a)
            w2T = sb("w2T", [P, NH1, D], F32, a)
            zT = sb("zT", [EMB, L], F32, a)
            fw1 = sb("fw1", [EMB, FILT], F32, a)
            fw23 = sb("fw23", [FILT, 2, FILT], F32, a)
            fwo = sb("fwo", [FILT, D], F32, a)
            fb = sb("fb", [FILT, 4], F32, a)
            ang = sb("ang", [FILT, L], F32, a)
            turn = sb("turn", [FILT, L], F32, a)
            sine = sb("sine", [FILT, L], F32, a)
            wmod = sb("wmod", [P, ND, 6 * D], F32, a)
            cT = sb("cT", [P, 2, ND, B], F32, a)
            grow = sb("grow", [B, 2, 2 * D], F32, a)
            gabs = sb("gabs", [B, 2 * D], F32, a)
            gsgn = sb("gsgn", [B, 2 * D], F32, a)
            ones = sb("ones", [P, P], F32, a)
            Kf0 = sb("Kf0", [P, NB, 2, ST, D], F32, a)
        with ExitStack() as a:
            hrow = sb("hrow", [P, NT, D], F32, a)
            tmp = sb("tmp", [P, 2, 2, D], F32, a)
            with ExitStack() as a1:
                Kf = sb("Kf", [P, NB, 2, ST, D], F32, a1)
                up = sb("up", [P, 2, L + 2], F32, a1)
                tap = sb("tap", [P, 2, L], F32, a1)
                x1 = sb("x1", [P, ND, L], F32, a1)
                x0 = sb("x0", [P, ND, L], F32, a1)
                vx = sb("vx", [P, ND, L], F32, a1)
                vrow = sb("vrow", [P, NT, D], F32, a1)
                prod = sb("prod", [P, 2, 2, 2, ST, D], F32, a1)
                Yf = sb("Yf", [P, NB, 2, ST, D], F32, a1)
            with ExitStack() as a2:
                gT = sb("gT", [P, NH1, L], F32, a2)
            with ExitStack() as a3:
                qhh = sb("qhh", [P, QRING, L], F32R, a3)
                q2 = sb("q2", [HD + 1, QRING, L], F32R, a3)
                khl = sb("khl", [P, 2, L], F32R, a3)
                k2 = sb("k2", [HD + 1, 2, L], F32R, a3)
                v1 = sb("v1", [P, 2, NT, HD + 1], F32, a3)
                oT = sb("oT", [P, HEADS * HD // P, L], F32, a3)
                pT = sb("pT", [P, PRING, HALF], F32, a3)
                rot = sb("rot", [P, NT, QK], F32, a3)
                orow = sb("orow", [P, NT, P], F32, a3)
                mx = sb("mx", [P, 2, NT], F32, a3)
                nm = sb("nm", [P, 2, NT], F32, a3)
                nmr = sb("nmr", [NT, 2, P], F32R, a3)
                den = sb("den", [P, 2, 4], F32, a3)
            with ExitStack() as a4:
                w1e = sb("w1e", [P, TOPK, ND, D], F32, a4)
                w2e = sb("w2e", [P, TOPK, ND, D], F32, a4)
                b1e = sb("b1e", [P, TOPK, ND], F32, a4)
                b2e = sb("b2e", [P, TOPK, D], F32, a4)
                geT = sb("geT", [P, TOPK * ND, L], F32, a4)
                score = sb("score", [1, EXPERTS], F32, a4)
                top = sb("top", [1, 8], F32, a4)
                topi = sb("topi", [1, 8], U32, a4)
        hflat = hrow[:, :, :].rearrange("p t n -> p (t n)")

        def rot_buf(r):
            return [hflat[:, (2 * r + k) * QK:(2 * r + k + 1) * QK].rearrange("p (h e i) -> p h e i", e=2, i=HD // 2)
                    for k in range(2)]

        def rotated(t):
            return rot[:, t, :]

        ps = es.enter_context(nc.psum_tensor("ps", [P, 8, HALF], F32))

        bar = sem("bar")
        go = {e: sem("go_" + e) for e in ("tensor", "vector", "scalar", "gpsimd")}
        first_cleared = None
        names = ["loaded", "loaded_filter", "loaded_c", "loaded_mod", "const_made", "filter_angle", "filter_sine", "kern_done",
                 "kf_done", "kf_loaded", "abs_done", "silu_done", "mod_done", "gate_rows", "gate_stored", "mod_picked",
                 "x_loaded", "gates_loaded", "gates_mixed", "var_done", "rstd_done", "hrow_done", "hT_done",
                 "bias_added", "tap_done", "conv_done", "vx_done", "vrow_done", "prod_done", 
                 "y_first", "y_done", "yv_done", "gelu_done", "rot_a", "rot_done", "v_done", "q_done", "q_lo_done",
                 "k_done", "k_lo_done", "nm_done", "nmr_done", "m_loaded0", "m_loaded1", "m_loaded2", "exp_done", "masked_done", 
                 "o_done", "oT_done", "top_done", "expert_loaded0", "expert_loaded1", "eb_mixed", "egelu_done", "x_done", "stored"]
        s = {}
        for n in names:
            s[n] = sem(n)
        ready = [sem(f"ready{i}") for i in range(8)]
        freed = [sem(f"freed{i}") for i in range(8)]
        cleared = list(s.values()) + ready + freed
        nums = [q.num for q in cleared]
        assert nums == list(range(nums[0], nums[0] + len(nums)))

        def m_loaded(u):
            return s[f"m_loaded{u % QRING}"], 16 * (u // QRING + 1)

        class Banks:
            def __init__(self):
                self.reset()

            def reset(self):
                self.at, self.uses, self.frees, self.owner, self.chunk = 0, [0] * 8, [0] * 8, [None] * 8, {}

            def take(self, pe, key, n=1, until=None):
                while self.at % n:
                    self.at += 1
                b = self.at % 8
                for q in range(b, b + n):
                    if self.owner[q] is not None:
                        pe.wait_ge(*self.owner[q])
                self.uses[b] += 1
                if until is None:
                    self.frees[b] += 1
                    until = (freed[b], self.frees[b])
                for q in range(b, b + n):
                    self.owner[q] = until
                self.at += n
                self.chunk[key] = (b, self.uses[b])
                return b

            def wait(self, eng, key):
                b, use = self.chunk[key]
                eng.wait_ge(ready[b], use)
                return b

        banks = {"setup": Banks(), "batch": Banks()}

        def part_ends(eng, name):
            eng.drain().then_inc(bar, 1)
            eng.wait_ge(go[name], 1)
            eng.sem_clear(go[name])

        block = es.enter_context(nc.Block())

        @block.tensor
        def _(pe):
            mm, tr = nc.tensor.matmul, nc.tensor.transpose
            bk = banks["setup"]
            pe.wait_ge(s["loaded_filter"], 16 * 9)
            for layer in range(3):
                if layer:
                    pe.wait_ge(s["filter_sine"], layer)
                for h in range(NHALF):
                    b = bk.take(pe, ("filter", layer, h))
                    w = fw1[:, :] if layer == 0 else fw23[:, layer - 1, :]
                    src = zT if layer == 0 else sine
                    mm(ps[0:FILT, b, :], w, src[:, h * HALF:(h + 1) * HALF], start=True, stop=True)\
                        .then_inc(ready[b], 1)
            pe.wait_ge(s["filter_sine"], 3)
            for t in range(0, NT, 2):
                b = bk.take(pe, ("kern", t), until=(s["kern_done"], t // 2 + 1))
                for u in range(2):
                    i = mm(ps[:, b, u * D:(u + 1) * D], sine[:, (t + u) * P:(t + u + 1) * P], fwo[:, :],
                           start=True, stop=True)
                i.then_inc(ready[b], 1)
            pe.wait_ge(s["loaded"], 16 * NLOADED)
            pe.wait_ge(s["kern_done"], NT // 2)
            for m in range(NB):
                for c in range(2):
                    b = bk.take(pe, ("kf", m, c))
                    for ft in range(ST):
                        col = (c * ST + ft) * P
                        terms_ = [(fwd_old, ST * m + q, q) for q in range(ST)]
                        if m:
                            terms_ += [(fwd, ST * (m - 1) + q, q) for q in range(ST)]
                        for n, (tab, t, q) in enumerate(terms_):
                            i = mm(ps[:, b, ft * D:(ft + 1) * D], tab[:, q, col:col + P], kern[:, t, :],
                                   start=n == 0, stop=n == len(terms_) - 1)
                    i.then_inc(ready[b], 1)
            pe.wait_ge(s["const_made"], 1)
            pe.wait_ge(s["abs_done"], 1)
            b = bk.take(pe, ("alpha2",))
            for q in range(NH1):
                i = mm(ps[:, b, 0:D], ones[:, :], w2T[:, q, :], start=q == 0, stop=q == NH1 - 1)
            i.then_inc(ready[b], 1)
            pe.wait_ge(s["silu_done"], 1)
            for layer in range(2):
                pe.wait_ge(s["loaded_mod"], 16 * (layer + 1))
                b = bk.take(pe, ("modT", layer))
                for n, kind in enumerate((0, 1, 3, 4)):
                    for dt in range(ND):
                        o = (n * ND + dt) * B
                        for q in range(ND):
                            i = mm(ps[:, b, o:o + B], wmod[:, q, kind * D + dt * P:kind * D + (dt + 1) * P],
                                   cT[:, layer, q, :], start=q == 0, stop=q == ND - 1)
                i.then_inc(ready[b], 1)
                b = bk.take(pe, ("gate", layer))
                for n, kind in enumerate((2, 5)):
                    for q in range(ND):
                        i = mm(ps[0:B, b, n * D:(n + 1) * D], cT[:, layer, q, :],
                               wmod[:, q, kind * D:(kind + 1) * D], start=q == 0, stop=q == ND - 1)
                i.then_inc(ready[b], 1)
            part_ends(pe, "tensor")

            bk = banks["batch"]

            def normed(k):
                for h in range(NHALF):
                    for dt in range(ND):
                        b = bk.take(pe, ("ln", k, h, dt), until=(s["hT_done"], (k * NHALF + h) * ND + dt + 1))
                        for u in range(4):
                            t = 4 * h + u
                            pe.wait_ge(s["hrow_done"], k * NT + t + 1)
                            i = tr(ps[:, b, u * P:(u + 1) * P], hrow[:, t, dt * P:(dt + 1) * P], ident[:, :])
                        i.then_inc(ready[b], 1)

            def h_ready(k, h):
                pe.wait_ge(s["hT_done"], (k * NHALF + h + 1) * ND)

            def project(g):
                for t in range(NT):
                    b = bk.take(pe, ("qkv", g, t), until=(s["v_done"], g * NT + t + 1))
                    for q in range(ND):
                        i = mm(ps[:, b, 0:GW], hT[:, q, t * P:(t + 1) * P], wqkv[:, q, g, :],
                               start=q == 0, stop=q == ND - 1)
                    i.then_inc(ready[b], 1)

            def turn_rows(g, slot, key, done, n):
                pe.wait_ge(s["rot_done"], (g + 1) * NT)
                for h in range(NHALF):
                    b = bk.take(pe, key + (h,), until=(done, NHALF * n + h + 1))
                    for u in range(4):
                        i = tr(ps[0:HD, b, u * P:(u + 1) * P], rotated(4 * h + u)[:, slot * HD:(slot + 1) * HD],
                               ident[:, :])
                    i.then_inc(ready[b], 1)

            def turn_head(u):
                if u % GQ == 0:
                    turn_rows(u // GQ, GQ, ("k", u // GQ), s["k_lo_done"], u // GQ)
                turn_rows(u // GQ, u % GQ, ("q", u), s["q_lo_done"], u)

            def score_rows(u, i):
                g, r, n = u // GQ, u % QRING, (i + 1) * P
                b = bk.take(pe, ("rows", u, i), 1 if n <= HALF else 2)
                if i == 0:
                    pe.wait_ge(s["q_done"], NHALF * (u + 1))
                    pe.wait_ge(s["k_lo_done"], NHALF * (g + 1))
                for c in range(0, n, HALF):
                    e = min(n, c + HALF)
                    q = mm(ps[:, b + c // HALF, 0:e - c], qhh[:, r, i * P:(i + 1) * P], khl[:, g % 2, c:e],
                           start=True, stop=True)
                q.then_inc(ready[b], 1)

            def turn_maxima(u):
                b = bk.take(pe, ("nm", u), until=(s["nmr_done"], u + 1))
                pe.wait_ge(s["nm_done"], u + 1)
                tr(ps[0:NT, b, 0:P], nm[:, u % 2, :], ident[:, :]).then_inc(ready[b], 1)

            def score_cols(u, c, j):
                g, r = u // GQ, u % QRING
                lo, hi = max(c * HALF, j * P), (c + 1) * HALF
                b = bk.take(pe, ("cols", u, c, j), until=(s["exp_done"], 12 * u + 4 * c + j + 1))
                if c == 0 and j == 0:
                    pe.wait_ge(s["q_lo_done"], NHALF * (u + 1))
                    pe.wait_ge(*m_loaded(u))
                mm(ps[:, b, 0:hi - lo], khl[:, g % 2, j * P:(j + 1) * P], qhh[:, r, lo:hi], start=True, stop=False)
                mm(ps[:, b, 0:hi - lo], k2[:, g % 2, j * P:(j + 1) * P], q2[:, r, lo:hi], start=False, stop=True)\
                    .then_inc(ready[b], 1)

            def values(u, c, i, b):
                g = u // GQ
                if i % 4 == 0:
                    pe.wait_ge(s["v_done"], (g + 1) * NT)
                for j in range(i + 1):
                    if j == 0 or j >= 4 * c:
                        pe.wait_ge(s["exp_done"], 12 * u + 4 * c + (j if j >= 4 * c else 4 * c - 1) + 1)
                        if j >= 4 * c:
                            pe.wait_ge(s["masked_done"], NT * u + j + 1)
                    lo = max(c * HALF, j * P)
                    slot = (12 * u + 4 * c + j) % PRING
                    q = mm(ps[:, b, (i % 4) * (HD + 1):(i % 4 + 1) * (HD + 1)],
                           pT[:, slot, i * P - lo:(i + 1) * P - lo], v1[:, g % 2, j, :],
                           start=j == 0, stop=j == i)
                return q

            def turn_outputs(w):
                for h in range(NHALF):
                    b = bk.take(pe, ("o", w, h), until=(s["oT_done"], NHALF * w + h + 1))
                    pe.wait_ge(s["o_done"], 4 * w + 2 + h + 1)
                    for u in range(4):
                        i = tr(ps[:, b, u * P:(u + 1) * P], orow[:, 4 * h + u, :], ident[:, :])
                    i.then_inc(ready[b], 1)

            with pe.Fori(0, B):
                bk.reset()
                normed(0)
                for n, e in enumerate(E_ORDER):
                    for h in range(NHALF):
                        b = bk.take(pe, ("up", n, h))
                        h_ready(0, h)
                        for q in range(ND):
                            i = mm(ps[:, b, :], in_w[:, q, e * P:(e + 1) * P], hT[:, q, h * HALF:(h + 1) * HALF],
                                   start=q == 0, stop=q == ND - 1)
                        i.then_inc(ready[b], 1)
                pe.wait_ge(s["vx_done"], ND)
                for t in range(0, NT, 2):
                    b = bk.take(pe, ("vrow", t), until=(s["vrow_done"], t // 2 + 1))
                    for u in range(2):
                        for dt in range(ND):
                            i = tr(ps[:, b, (u * ND + dt) * P:(u * ND + dt + 1) * P],
                                   vx[:, dt, (t + u) * P:(t + u + 1) * P], ident[:, :])
                    i.then_inc(ready[b], 1)
                vblocks = vrow[:, :, :].rearrange("p (j q) n -> p j q n", q=ST)
                for jp in range(NB // 2):
                    pe.wait_ge(s["vrow_done"], 2 * (jp + 1))
                    b = bk.take(pe, ("vf", jp), 4, until=(s["prod_done"], PAIRS_DONE[jp]))
                    for c in range(2 * ST):
                        for q in range(ST):
                            i = mm(ps[:, b + c, :], fwd[:, q, c * P:(c + 1) * P], vblocks[:, 2 * jp:2 * jp + 2, q, :],
                                   start=q == 0, stop=q == ST - 1)
                    i.then_inc(ready[b], 1)
                for ip in range(NB // 2):
                    for dt in range(ND):
                        b = bk.take(pe, ("y", ip, dt))
                        for u in range(2):
                            blk = 2 * ip + u
                            pe.wait_ge(s["y_first"], 2 * (blk + 1))
                            if blk:
                                pe.wait_ge(s["y_done"], Y_DONE[blk])
                            for q in range(2 * ST):
                                i = mm(ps[:, b, u * S:(u + 1) * S], Yf[:, blk, q // ST, q % ST, dt * P:(dt + 1) * P],
                                       inv[:, q, :], start=q == 0, stop=q == 2 * ST - 1)
                        i.then_inc(ready[b], 1)
                for t in range(0, NT, 2):
                    b = bk.take(pe, ("out0", t))
                    pe.wait_ge(s["yv_done"], ND * (t // 4 + 1))
                    for u in range(2):
                        for q in range(ND):
                            i = mm(ps[:, b, u * D:(u + 1) * D], x0[:, q, (t + u) * P:(t + u + 1) * P], out_w[:, q, :],
                                   start=q == 0, stop=q == ND - 1)
                    i.then_inc(ready[b], 1)
                normed(1)
                for h in range(NHALF):
                    h_ready(1, h)
                    for n in range(NH1):
                        b = bk.take(pe, ("ffn1", h, n), until=(s["gelu_done"], h * NH1 + n + 1))
                        for q in range(ND):
                            i = mm(ps[:, b, :], sgn1[:, q, n * P:(n + 1) * P], hT[:, q, h * HALF:(h + 1) * HALF],
                                   start=q == 0, stop=q == ND - 1)
                        i.then_inc(ready[b], 1)
                for t in range(0, NT, 2):
                    b = bk.take(pe, ("ffn2", t))
                    for u in range(2):
                        for q in range(NH1):
                            pe.wait_ge(s["gelu_done"], NH1 * (t // 4) + q + 1)
                            i = mm(ps[:, b, u * D:(u + 1) * D], gT[:, q, (t + u) * P:(t + u + 1) * P], sgn2[:, q, :],
                                   start=q == 0, stop=q == NH1 - 1)
                    i.then_inc(ready[b], 1)
                normed(2)
                h_ready(2, NHALF - 1)
                project(0)
                for u in range(LEAD):
                    turn_head(u)
                    for i in range(NT):
                        score_rows(u, i)
                turn_maxima(0)
                for u in range(HEADS):
                    w = u + LEAD
                    if u + 1 < HEADS:
                        turn_maxima(u + 1)
                    for j in range(4):
                        score_cols(u, 0, j)
                    if w < HEADS:
                        turn_head(w)
                    if u >= 2 and u % 2 == 0:
                        turn_outputs(u // 2 - 1)
                    b = bk.take(pe, ("pv", u, 0), until=(s["o_done"], 2 * u + 1))
                    for i in range(4):
                        q = values(u, 0, i, b)
                    q.then_inc(ready[b], 1)
                    for i in range(4):
                        if w < HEADS:
                            score_rows(w, i)
                    for j in range(NT):
                        score_cols(u, 1, j)
                    if w < HEADS:
                        score_rows(w, 4)
                    b = bk.take(pe, ("pv", u, 1), until=(s["o_done"], 2 * u + 2))
                    for i in range(4, NT):
                        q = values(u, 1, i, b)
                    q.then_inc(ready[b], 1)
                    for i in range(5, NT):
                        if w < HEADS:
                            score_rows(w, i)
                    if u % GQ == 1 and u // GQ + 1 < KV:
                        project(u // GQ + 1)
                turn_outputs(HEADS // 2 - 1)
                for t in range(0, NT, 2):
                    b = bk.take(pe, ("out1", t))
                    pe.wait_ge(s["oT_done"], HEADS - 1 + t // 4)
                    for u in range(2):
                        for q in range(HEADS // 2):
                            i = mm(ps[:, b, u * D:(u + 1) * D], oT[:, q, (t + u) * P:(t + u + 1) * P], wo[:, q, :],
                                   start=q == 0, stop=q == HEADS // 2 - 1)
                    i.then_inc(ready[b], 1)
                normed(3)
                h_ready(3, 0)
                b = bk.take(pe, ("router",))
                for q in range(ND):
                    i = mm(ps[0:1, b, 0:EXPERTS], hT[:, q, 0:1], wr[:, q, :], start=q == 0, stop=q == ND - 1)
                i.then_inc(ready[b], 1)
                h_ready(3, NHALF - 1)
                for k in range(TOPK):
                    pe.wait_ge(s[f"expert_loaded{k}"], 16 * 4)
                    for h in range(NHALF):
                        for n in range(ND):
                            b = bk.take(pe, ("moe1", k, h, n), until=(s["egelu_done"], (k * NHALF + h) * ND + n + 1))
                            for q in range(ND):
                                i = mm(ps[:, b, :], w1e[:, k, q, n * P:(n + 1) * P], hT[:, q, h * HALF:(h + 1) * HALF],
                                       start=q == 0, stop=q == ND - 1)
                            i.then_inc(ready[b], 1)
                for t in range(0, NT, 2):
                    b = bk.take(pe, ("moe2", t))
                    pe.wait_ge(s["egelu_done"], ND * NHALF + ND * (t // 4 + 1))
                    for u in range(2):
                        for n in range(TOPK * ND):
                            i = mm(ps[:, b, u * D:(u + 1) * D], geT[:, n, (t + u) * P:(t + u + 1) * P],
                                   w2e[:, n // ND, n % ND, :], start=n == 0, stop=n == TOPK * ND - 1)
                    i.then_inc(ready[b], 1)
                part_ends(pe, "tensor")

        @block.scalar
        def _(act):
            A = nc.scalar.activation
            bk = banks["setup"]

            act.wait_ge(s["loaded"], 16 * NLOADED)
            A(sgn1[:, :, :], w1T[:, :, :], ACT.Sign)
            A(sgn2[:, :, :], w2T[:, :, :], ACT.Sign)
            act.drain()
            A(w2T[:, :, :], w2T[:, :, :], ACT.Abs).then_inc(s["abs_done"], 1)
            act.wait_ge(s["loaded_c"], 16)
            A(cT[:, :, :, :], cT[:, :, :, :], ACT.Silu).then_inc(s["silu_done"], 1)
            for layer in range(3):
                act.wait_ge(s["filter_angle"], layer + 1)
                A(sine[:, :], ang[:, :], ACT.Sin).then_inc(s["filter_sine"], 1)
            for m in range(NB):
                for c in range(2):
                    b = bk.wait(act, ("kf", m, c))
                    A(Kf0[:, m, c, :, :], ps[:, b, :].rearrange("p (f n) -> p f n", f=ST), ACT.Copy)\
                        .then_inc(freed[b], 1)
            act.drain().then_inc(s["kf_done"], 1)
            b = bk.wait(act, ("alpha2",))
            A(alpha2[:, :], ps[:, b, 0:D], ACT.Copy, scale=1.0 / HID).then_inc(freed[b], 1)
            part_ends(act, "scalar")

            bk = banks["batch"]

            def normed(k):
                if k == 0:
                    act.wait_ge(s["mod_picked"], 1)
                for h in range(NHALF):
                    for dt in range(ND):
                        b = bk.wait(act, ("ln", k, h, dt))
                        at = 2 * (k % 2)
                        A(hT[:, dt, h * HALF:(h + 1) * HALF], ps[:, b, :], ACT.Identity,
                          bias=modb[:, k // 2, at, dt:dt + 1], scale=modb[:, k // 2, at + 1, dt:dt + 1])\
                            .then_inc(s["hT_done"], 1)

            def turn_head(u):
                g = u // GQ
                if u >= QRING:
                    bk.wait(act, ("pv", u - QRING, 1))
                if u % GQ == 0:
                    for h in range(NHALF):
                        b = bk.wait(act, ("k", g, h))
                        cols = slice(h * HALF, (h + 1) * HALF)
                        A(khl[0:HD, g % 2, cols], ps[0:HD, b, :], ACT.Copy)
                        A(k2[0:HD, g % 2, cols], ps[0:HD, b, :], ACT.Copy).then_inc(s["k_done"], 1)
                for h in range(NHALF):
                    b = bk.wait(act, ("q", u, h))
                    for half in (HD, 0):
                        i = A(qhh[half:half + HD, u % QRING, h * HALF:(h + 1) * HALF], ps[0:HD, b, :], ACT.Copy)
                    i.then_inc(s["q_done"], 1)

            def turn_maxima(u):
                b = bk.wait(act, ("nm", u))
                if u >= 2:
                    act.wait_ge(*m_loaded(u - 2))
                A(nmr[:, u % 2, :], ps[0:NT, b, 0:P], ACT.Copy).then_inc(s["nmr_done"], 1)

            def exps(u, c, j):
                n = 12 * u + 4 * c + j
                lo = max(c * HALF, j * P)
                b = bk.wait(act, ("cols", u, c, j))
                if n >= PRING:
                    pu, pj = (n - PRING) // 12, (n - PRING) % 12
                    bk.wait(act, ("pv", pu, int(pj >= 4)))
                A(pT[:, n % PRING, 0:(c + 1) * HALF - lo], ps[:, b, 0:(c + 1) * HALF - lo], ACT.Exp, scale=SCALE)\
                    .then_inc(s["exp_done"], 1)

            def value_rows(g):
                for t in range(NT):
                    b = bk.wait(act, ("qkv", g, t))
                    act.wait_ge(s["rot_a"], g * NT + t + 1)
                    A(v1[:, g % 2, t, 0:HD], ps[:, b, QK:GW], ACT.Copy).then_inc(s["v_done"], 1)

            def turn_outputs(w):
                for h in range(NHALF):
                    b = bk.wait(act, ("o", w, h))
                    A(oT[:, w, h * HALF:(h + 1) * HALF], ps[:, b, :], ACT.Copy).then_inc(s["oT_done"], 1)

            with act.Fori(0, B):
                normed(0)
                for n, e in enumerate(E_ORDER):
                    if n >= 2:
                        act.wait_ge(s["conv_done"], n - 1)
                    for h in range(NHALF):
                        b = bk.wait(act, ("up", n, h))
                        A(up[:, n % 2, 2 + h * HALF:2 + (h + 1) * HALF], ps[:, b, :], ACT.Identity,
                          bias=in_b[:, e:e + 1]).then_inc(freed[b], 1)
                    act.drain()
                    A(tap[:, n % 2, :], up[:, n % 2, 2:L + 2], ACT.Identity, scale=short_w[:, e, 2:3],
                      bias=short_b[:, e:e + 1]).then_inc(s["tap_done"], 1)
                for t in range(0, NT, 2):
                    b = bk.wait(act, ("vrow", t))
                    A(vrow[:, t:t + 2, :], ps[:, b, :].rearrange("p (t n) -> p t n", t=2), ACT.Copy)\
                        .then_inc(s["vrow_done"], 1)
                normed(1)
                for h in range(NHALF):
                    for n in range(NH1):
                        b = bk.wait(act, ("ffn1", h, n))
                        A(gT[:, n, h * HALF:(h + 1) * HALF], ps[:, b, :], ACT.Gelu, scale=alpha1[:, n:n + 1],
                          bias=ffn_b1[:, n:n + 1]).then_inc(s["gelu_done"], 1)
                normed(2)
                value_rows(0)
                for u in range(LEAD):
                    turn_head(u)
                turn_maxima(0)
                for u in range(HEADS):
                    w = u + LEAD
                    if u + 1 < HEADS:
                        turn_maxima(u + 1)
                    for j in range(4):
                        exps(u, 0, j)
                    if w < HEADS:
                        turn_head(w)
                    if u >= 2 and u % 2 == 0:
                        turn_outputs(u // 2 - 1)
                    for j in range(NT):
                        exps(u, 1, j)
                    if u % GQ == 1 and u // GQ + 1 < KV:
                        value_rows(u // GQ + 1)
                turn_outputs(HEADS // 2 - 1)
                normed(3)
                for k in range(TOPK):
                    act.wait_ge(s[f"expert_loaded{k}"], 16 * 4)
                    for h in range(NHALF):
                        for n in range(ND):
                            b = bk.wait(act, ("moe1", k, h, n))
                            A(geT[:, k * ND + n, h * HALF:(h + 1) * HALF], ps[:, b, :], ACT.Gelu,
                              bias=b1e[:, k, n:n + 1]).then_inc(s["egelu_done"], 1)
                part_ends(act, "scalar")

        @block.vector
        def _(dve):
            V = nc.vector
            bk = banks["setup"]
            dve.wait_ge(s["loaded_filter"], 16 * 9)
            for layer in range(3):
                if layer:
                    dve.wait_ge(s["filter_sine"], layer)
                for h in range(NHALF):
                    b = bk.wait(dve, ("filter", layer, h))
                    V.tensor_scalar(ang[:, h * HALF:(h + 1) * HALF], ps[0:FILT, b, :], fb[:, layer:layer + 1],
                                    fb[:, 3:4], ALU.add, ALU.mult).then_inc(freed[b], 1)
                dve.drain()
                V.tensor_scalar(turn[:, :], ang[:, :], float(1 / (2 * np.pi)), ROUND, ALU.mult, ALU.add)
                dve.drain()
                V.tensor_scalar(turn[:, :], turn[:, :], ROUND, None, ALU.subtract)
                dve.drain()
                V.scalar_tensor_tensor(out=ang[:, :], in0=turn[:, :], scalar=-TWO_PI_HI, in1=ang[:, :],
                                       op0=ALU.mult, op1=ALU.add)
                dve.drain()
                V.scalar_tensor_tensor(out=ang[:, :], in0=turn[:, :], scalar=-TWO_PI_LO, in1=ang[:, :],
                                       op0=ALU.mult, op1=ALU.add)
                dve.drain()
                V.tensor_scalar(ang[:, :], ang[:, :], PI_DOWN, -PI_DOWN, ALU.min, ALU.max)\
                    .then_inc(s["filter_angle"], 1)
            dve.wait_ge(s["loaded"], 16 * NLOADED)
            for t in range(0, NT, 2):
                b = bk.wait(dve, ("kern", t))
                V.tensor_tensor(kern[:, t:t + 2, :], ps[:, b, :].rearrange("p (t n) -> p t n", t=2),
                                decay[:, t:t + 2, :], ALU.mult).then_inc(s["kern_done"], 1)
            V.reduce_sum(alpha1[:, :], w1rows[:, :, :], AX, apply_absolute_value=True)
            dve.drain()
            V.tensor_scalar(alpha1[:, :], alpha1[:, :], 1.0 / D, None, ALU.mult)
            for layer in range(2):
                b = bk.wait(dve, ("modT", layer))
                V.tensor_copy(modT[:, layer, :, :, :].rearrange("p k t b -> p (k t b)"), ps[:, b, 0:4 * ND * B])\
                    .then_inc(freed[b], 1)
                dve.drain()
                for k in (1, 3):
                    V.tensor_scalar(modT[:, layer, k, :, :], modT[:, layer, k, :, :], 1.0, None, ALU.add)
                b = bk.wait(dve, ("gate", layer))
                V.tensor_copy(grow[:, layer, :], ps[0:B, b, :]).then_inc(freed[b], 1)
                dve.drain()
                V.scalar_tensor_tensor(out=gabs[:, :], in0=grow[:, layer, :], scalar=-1.0, in1=grow[:, layer, :],
                                       op0=ALU.mult, op1=ALU.max)
                V.tensor_scalar(gsgn[:, :], grow[:, layer, :], 0.0, 2.0, ALU.is_ge, ALU.mult)
                dve.drain()
                V.tensor_scalar(gabs[:, :], gabs[:, :], 0.25, None, ALU.max)
                V.tensor_scalar(gsgn[:, :], gsgn[:, :], -1.0, None, ALU.add)
                dve.drain()
                V.tensor_tensor(grow[:, layer, :], gabs[:, :], gsgn[:, :], ALU.mult).then_inc(s["gate_rows"], 1)
                dve.drain()
            part_ends(dve, "vector")

            bk = banks["batch"]

            def normed(k):
                for t in range(NT):
                    V.bn_stats(stat[:, t, :], x[:, t, :])
                dve.drain()
                for t in range(NT):
                    V.bn_aggr(mv[:, t, :], stat[:, t, :])
                dve.drain()
                V.tensor_scalar(var[:, :], mv[:, :, 1], EPS, None, ALU.add).then_inc(s["var_done"], 1)
                dve.wait_ge(s["rstd_done"], k + 1)
                for t in range(NT):
                    V.tensor_scalar(hrow[:, t, :], x[:, t, :], mv[:, t, 0:1], rstd[:, t:t + 1],
                                    ALU.subtract, ALU.mult).then_inc(s["hrow_done"], 1)

            def add_to_x(name, k, gate):
                dve.wait_ge(s["bias_added"], k)
                for t in range(0, NT, 2):
                    b = bk.wait(dve, (name, t))
                    r = (t // 2) % 2
                    V.tensor_tensor(tmp[:, r, :, :], ps[:, b, :].rearrange("p (t n) -> p t n", t=2),
                                    gate.unsqueeze(1).broadcast_to([P, 2, D]), ALU.mult).then_inc(freed[b], 1)
                    dve.drain()
                    V.tensor_tensor(x[:, t:t + 2, :], x[:, t:t + 2, :], tmp[:, r, :, :], ALU.add)
                dve.drain()

            def rotate(g):
                for t in range(NT):
                    b = bk.wait(dve, ("qkv", g, t))
                    r = t % 2
                    n = g * NT + t
                    if n >= 2:
                        dve.wait_ge(s["rot_done"], n - 1)
                    v = ps[:, b, 0:QK].rearrange("p (h e i) -> p h e i", e=2, i=HD // 2)
                    cs = [rope[:, t, q, :].unsqueeze(1).broadcast_to([P, GQ + 1, HD // 2]) for q in range(2)]
                    A4, B4 = rot_buf(r)
                    for e in range(2):
                        V.tensor_tensor(A4[:, :, e, :], v[:, :, e, :], cs[0], ALU.mult)
                    V.tensor_tensor(B4[:, :, 0, :], v[:, :, 1, :], cs[1], ALU.mult)
                    V.tensor_tensor(B4[:, :, 1, :], v[:, :, 0, :], cs[1], ALU.mult).then_inc(s["rot_a"], 1)

            def turn_head(u):
                g = u // GQ
                if u % GQ == 0:
                    for h in range(NHALF):
                        b = bk.wait(dve, ("k", g, h))
                        cols = slice(h * HALF, (h + 1) * HALF)
                        dve.wait_ge(s["k_done"], NHALF * g + h + 1)
                        V.tensor_tensor(khl[HD:P, g % 2, cols], ps[0:HD, b, :], khl[0:HD, g % 2, cols].bitcast(F32),
                                        ALU.subtract).then_inc(s["k_lo_done"], 1)
                for h in range(NHALF):
                    b = bk.wait(dve, ("q", u, h))
                    cols = slice(h * HALF, (h + 1) * HALF)
                    dve.wait_ge(s["q_done"], NHALF * u + h + 1)
                    V.tensor_tensor(q2[0:HD, u % QRING, cols], ps[0:HD, b, :], qhh[0:HD, u % QRING, cols].bitcast(F32),
                                    ALU.subtract).then_inc(s["q_lo_done"], 1)

            def row_maxima(u, i):
                n = (i + 1) * P
                b = bk.wait(dve, ("rows", u, i))
                v = (ps[:, b:b + 2, :].rearrange("p a n -> p (a n)") if n > HALF else ps[:, b, :])[:, 0:n]
                V.tensor_tensor_reduce(out=v, in0=v, in1=mrow[:, L - n:L], scale=1.0, scalar=-3e38, op0=ALU.add,
                                       op1=ALU.max, accum_out=mx[:, u % 2, i:i + 1]).then_inc(freed[b], 1)

            def negate(u):
                dve.drain()
                V.tensor_scalar(nm[:, u % 2, :], mx[:, u % 2, :], -1.0, None, ALU.mult).then_inc(s["nm_done"], 1)

            def normalise(u, c):
                b = bk.wait(dve, ("pv", u, c))
                v = ps[:, b, 0:4 * (HD + 1)].rearrange("p (i n) -> p i n", n=HD + 1)
                V.reciprocal(den[:, c, :], v[:, :, HD])
                dve.drain()
                if u >= 2 and u % 2 == 0:
                    dve.wait_ge(s["oT_done"], u)
                V.tensor_tensor(orow[:, 4 * c:4 * c + 4, (u % 2) * HD:(u % 2 + 1) * HD], v[:, :, 0:HD],
                                den[:, c, :].unsqueeze(2).broadcast_to([P, 4, HD]), ALU.mult)\
                    .then_inc(s["o_done"], 1)

            with dve.Fori(0, B) as bi:
                V.tensor_copy(modb[:, :, :, :].rearrange("p l k t -> p (l k t)"),
                              modT[:, :, :, :, :].rearrange("p l k t b -> p (l k t) b")[:, :, bass.ds(bi, 1)]
                              .rearrange("p n b -> p (n b)")).then_inc(s["mod_picked"], 1)
                for r in range(2):
                    V.memset(up[:, r, 0:2], 0.0)
                dve.wait_ge(s["x_loaded"], 16)
                normed(0)
                for n, e in enumerate(E_ORDER):
                    dst = {0: x0, 1: x1, 2: vx}[e // ND]
                    dt = e % ND
                    dve.wait_ge(s["tap_done"], n + 1)
                    V.scalar_tensor_tensor(out=tap[:, n % 2, :], in0=up[:, n % 2, 1:L + 1], scalar=short_w[:, e, 1:2],
                                           in1=tap[:, n % 2, :], op0=ALU.mult, op1=ALU.add)
                    dve.drain()
                    V.scalar_tensor_tensor(out=dst[:, dt, :], in0=up[:, n % 2, 0:L], scalar=short_w[:, e, 0:1],
                                           in1=tap[:, n % 2, :], op0=ALU.mult, op1=ALU.add)\
                        .then_inc(s["conv_done"], 1)
                    if e // ND == 1:
                        dve.drain()
                        V.tensor_tensor(vx[:, dt, :], vx[:, dt, :], x1[:, dt, :], ALU.mult).then_inc(s["vx_done"], 1)
                dve.wait_ge(s["kf_loaded"], 16)
                n = 0
                for jp in range(NB // 2):
                    b = bk.wait(dve, ("vf", jp))
                    for jj in range(2):
                        j = 2 * jp + jj
                        for i in range(j, NB):
                            if j and n - 2 >= NB:
                                dve.wait_ge(s["y_done"], n - 2 - NB + 1)
                            v = ps[:, b:b + 2 * ST, jj * D:(jj + 1) * D].rearrange("p (c f) n -> p c f n", c=2)
                            for k in range(2):
                                q = V.tensor_tensor(prod[:, n % 2, k, :, :, :], v,
                                                    Kf[:, i - j, k, :, :].unsqueeze(1).broadcast_to([P, 2, ST, D]),
                                                    ALU.mult)
                            if j == 0:
                                dve.drain()
                                V.tensor_tensor(Yf[:, i, 0, :, :], prod[:, n % 2, 0, 0, :, :], prod[:, n % 2, 1, 1, :, :],
                                                ALU.subtract).then_inc(s["y_first"], 1)
                                V.tensor_tensor(Yf[:, i, 1, :, :], prod[:, n % 2, 0, 1, :, :], prod[:, n % 2, 1, 0, :, :],
                                                ALU.add).then_inc(s["y_first"], 1)
                                dve.drain()
                            else:
                                q.then_inc(s["prod_done"], 1)
                            n += 1
                for ip in range(NB // 2):
                    for dt in range(ND):
                        b = bk.wait(dve, ("y", ip, dt))
                        cols = slice(ip * HALF, (ip + 1) * HALF)
                        V.scalar_tensor_tensor(out=vx[:, dt, cols], in0=vx[:, dt, cols], scalar=filt_b[:, dt:dt + 1],
                                               in1=ps[:, b, :], op0=ALU.mult, op1=ALU.add).then_inc(freed[b], 1)
                        dve.drain()
                        V.tensor_tensor(x0[:, dt, cols], vx[:, dt, cols], x0[:, dt, cols], ALU.mult)\
                            .then_inc(s["yv_done"], 1)
                add_to_x("out0", 1, gates[:, 0, :])
                normed(1)
                dve.wait_ge(s["gates_mixed"], 1)
                add_to_x("ffn2", 2, escale[:, 0, :])
                normed(2)
                rotate(0)
                for u in range(LEAD):
                    turn_head(u)
                    for i in range(NT):
                        row_maxima(u, i)
                    negate(u)
                for u in range(HEADS):
                    w = u + LEAD
                    if w < HEADS:
                        turn_head(w)
                    normalise(u, 0)
                    for i in range(5):
                        if w < HEADS:
                            row_maxima(w, i)
                    normalise(u, 1)
                    if w < HEADS:
                        for i in range(5, NT):
                            row_maxima(w, i)
                        dve.wait_ge(s["nmr_done"], w - 1)
                        negate(w)
                    if u % GQ == 1 and u // GQ + 1 < KV:
                        rotate(u // GQ + 1)
                add_to_x("out1", 2, gates[:, 2, :])
                normed(3)
                b = bk.wait(dve, ("router",))
                V.tensor_tensor(score[:, :], ps[0:1, b, 0:EXPERTS], br[:, :], ALU.add).then_inc(freed[b], 1)
                dve.drain()
                V.max(top[:, :], score[:, :])
                dve.drain()
                V.max_index(topi[:, :], top[:, :], score[:, :]).then_inc(s["top_done"], 1)
                add_to_x("moe2", 3, escale[:, 1, :])
                dve.drain().then_inc(s["x_done"], 1)
                part_ends(dve, "vector")

        @block.gpsimd
        def _(pool):
            G = nc.gpsimd
            G.memset(ones[:, :], 1.0)
            G.memset(ident[:, :], 0.0)
            G.memset(mrow[:, :], 0.0)
            G.memset(neghalf[:, :], -0.5)
            pool.drain()
            G.affine_select(out=ident[:, :], in_=ident[:, :], compare_op=ALU.not_equal, fill=1.0, base=0,
                            pattern=[[-1, P]], channel_multiplier=1)
            G.affine_select(out=mrow[:, L - P:L], in_=mrow[:, L - P:L], compare_op=ALU.is_ge, fill=MASKED, base=0,
                            pattern=[[-1, P]], channel_multiplier=1)
            pool.drain().then_inc(s["const_made"], 1)
            part_ends(pool, "gpsimd")

            def normed(k):
                pool.wait_ge(s["var_done"], k + 1)
                G.tensor_tensor(rstd[:, :], var[:, :], neghalf[:, :], ALU.pow).then_inc(s["rstd_done"], 1)

            def add_bias(k, n):
                pool.wait_ge(s["hrow_done"], (k + 1) * NT)
                for t in range(0, NT, 2):
                    G.tensor_tensor(x[:, t:t + 2, :], x[:, t:t + 2, :],
                                    terms[:, n, :].unsqueeze(1).broadcast_to([P, 2, D]), ALU.add)
                pool.drain().then_inc(s["bias_added"], 1)

            def mask(u, c, j):
                pool.wait_ge(s["exp_done"], 12 * u + 4 * c + j + 1)
                v = pT[:, (12 * u + 4 * c + j) % PRING, 0:P]
                G.affine_select(out=v, in_=v, compare_op=ALU.is_ge, fill=0.0, base=0, pattern=[[1, P]],
                                channel_multiplier=-1).then_inc(s["masked_done"], 1)

            def rotate(g):
                for t in range(NT):
                    pool.wait_ge(s["rot_a"], g * NT + t + 1)
                    if g and t == 0:
                        pool.wait_ge(s["q_done"], NHALF * GQ * g)
                    A4, B4 = rot_buf(t % 2)
                    R4 = rotated(t).rearrange("p (h e i) -> p h e i", e=2, i=HD // 2)
                    G.tensor_tensor(R4[:, :, 0, :], A4[:, :, 0, :], B4[:, :, 0, :], ALU.subtract)
                    G.tensor_tensor(R4[:, :, 1, :], A4[:, :, 1, :], B4[:, :, 1, :], ALU.add).then_inc(s["rot_done"], 1)

            with pool.Fori(0, B):
                pool.wait_ge(s["gates_loaded"], 16)
                G.tensor_tensor(terms[:, 0, :], rows[:, 0, :], gates[:, 0, :], ALU.mult)
                G.tensor_tensor(terms[:, 1, :], rows[:, 1, :], gates[:, 1, :], ALU.mult)
                G.tensor_tensor(escale[:, 0, :], alpha2[:, :], gates[:, 1, :], ALU.mult)
                G.tensor_scalar(escale[:, 1, :], gates[:, 3, :], 1.0 / TOPK, 0.0, ALU.mult, ALU.add)
                pool.drain().then_inc(s["gates_mixed"], 1)
                normed(0)
                add_bias(0, 0)
                n = done = 0
                for j in range(NB):
                    for i in range(j, NB):
                        if j:
                            done += 1
                            pool.wait_ge(s["prod_done"], done)
                            if j == 1 and i == 1:
                                pool.wait_ge(s["y_first"], 2 * NB)
                            pr = prod[:, n % 2]
                            for c, (k, w, op) in ((0, (0, 0, ALU.add)), (1, (0, 1, ALU.add)),
                                                  (0, (1, 1, ALU.subtract)), (1, (1, 0, ALU.add))):
                                if k == 1 and c == 0:
                                    pool.drain()
                                q = G.tensor_tensor(Yf[:, i, c, :, :], Yf[:, i, c, :, :], pr[:, k, w, :, :], op)
                            q.then_inc(s["y_done"], 1)
                            pool.drain()
                        n += 1
                normed(1)
                add_bias(1, 1)
                normed(2)
                G.memset(v1[:, :, :, HD:HD + 1], 1.0)
                pool.drain()
                G.memset(k2[HD:HD + 1, :, :].bitcast(F32), 1.0)
                pool.drain()
                rotate(0)
                for u in range(HEADS):
                    for j in range(4):
                        mask(u, 0, j)
                    for j in range(4, NT):
                        mask(u, 1, j)
                    if u % GQ == 1 and u // GQ + 1 < KV:
                        rotate(u // GQ + 1)
                normed(3)
                for k in range(TOPK):
                    pool.wait_ge(s[f"expert_loaded{k}"], 16 * 4)
                G.tensor_tensor(b2e[:, 0, :], b2e[:, 0, :], b2e[:, 1, :], ALU.add)
                pool.drain()
                G.tensor_tensor(terms[:, 2, :], b2e[:, 0, :], escale[:, 1, :], ALU.mult)
                pool.drain()
                add_bias(3, 2)
                part_ends(pool, "gpsimd")

        @block.sync
        def _(sp):
            dma = nc.sync.dma_start
            for dst, src in ((zT[:, :], d["zT"]), (fw1[:, :], d["L0_attn_mlp_w1"]), (fw23[:, 0, :], d["L0_attn_mlp_w2"]),
                             (fw23[:, 1, :], d["L0_attn_mlp_w3"]), (fwo[:, :], d["L0_attn_mlp_wo"]),
                             (fb[:, 0:1], d["L0_attn_mlp_b1"]), (fb[:, 1:2], d["L0_attn_mlp_b2"]),
                             (fb[:, 2:3], d["L0_attn_mlp_b3"]), (fb[:, 3:4], d["L0_attn_freq"])):
                dma(dst, src, allow_slow_non_contiguous=True).then_inc(s["loaded_filter"], 16)
            dma(cT[:, :, :, :], d["cT"], allow_slow_non_contiguous=True).then_inc(s["loaded_c"], 16)
            loads = [(w1rows[:, :, :], d["L0_ffn_w1"]), (w1T[:, :, :], d["w1T"]), (w2T[:, :, :], d["w2T"]),
                     (decay[:, :, :], d["decay"]), (fwd[:, :, :], d["fwd"][:, 0]), (fwd_old[:, :, :], d["fwd"][:, 1]),
                     (inv[:, :, :], d["inv"]), (in_w[:, :, :], d["in_w"]), (out_w[:, :, :], d["out_w"]),
                     (wqkv[:, :, :, :], d["wqkv"]), (wo[:, :, :], d["wo"]), (rope[:, :, :, :], d["rope"]),
                     (wr[:, :, :], d["wr"]), (br[:, :], d["L1_ffn_br"]), (in_b[:, :], d["in_b"]),
                     (short_w[:, :, :], d["short_w"]), (short_b[:, :], d["short_b"]), (filt_b[:, :], d["filt_b"]),
                     (ffn_b1[:, :], d["ffn_b1"]), (rows[:, 0, :], d["L0_attn_out_b"].partition_broadcast(P)),
                     (rows[:, 1, :], d["L0_ffn_b2"].partition_broadcast(P))]
            assert len(loads) == NLOADED
            for dst, src in loads:
                dma(dst, src, allow_slow_non_contiguous=True).then_inc(s["loaded"], 16)
            for layer in range(2):
                if layer:
                    sp.wait_ge(s["gate_rows"], 1)
                dma(wmod[:, :, :], d[f"wmod{layer}"]).then_inc(s["loaded_mod"], 16)
            sp.wait_ge(s["gate_rows"], 2)
            dma(gate_scratch, grow[:, :, :].rearrange("b l n -> b (l n)")).then_inc(s["gate_stored"], 16)
            sp.wait_ge(s["kf_done"], 1)
            dma(kf_scratch, Kf0[:, :, :, :, :].rearrange("p m c f n -> p (m c f n)")).then_inc(s["gate_stored"], 16)
            sp.wait_ge(s["gate_stored"], 32)

            def clear():
                sp.wait_ge(bar, 4)
                sp.sem_clear(range(nums[0], nums[-1] + 1))
                sp.sem_clear(bar)
                for e in go:
                    sp.sem_inc(go[e], 1)

            clear()
            with sp.Fori(0, B) as bi:
                dma(x[:, :, :], d["x"][bass.ds(bi, 1), :, :].rearrange("a (t p) n -> p (a t) n", p=P))\
                    .then_inc(s["x_loaded"], 16)
                dma(gates[:, :, :].rearrange("p k n -> p (k n)"),
                    gate_scratch[bass.ds(bi, 1), :].broadcast_to([P, 4 * D])).then_inc(s["gates_loaded"], 16)
                dma(Kf[:, :, :, :, :].rearrange("p m c f n -> p (m c f n)"), kf_scratch).then_inc(s["kf_loaded"], 16)
                for u in range(HEADS):
                    sp.wait_ge(s["nmr_done"], u + 1)
                    if u >= QRING:
                        banks["batch"].wait(sp, ("pv", u - QRING, 1))
                    dma(q2[HD:HD + 1, u % QRING, :].bitcast(F32), nmr[:, u % 2, :].bitcast(F32)).then_inc(m_loaded(u)[0], 16)
                sp.wait_ge(s["top_done"], 1)
                for k in range(TOPK):
                    e = nc.sync.value_load(topi[0:1, k:k + 1], min_val=0, max_val=EXPERTS - 1)
                    one = bass.ds(e, 1)
                    for dst, src in ((w1e[:, k, :, :], d["W1"][one].rearrange("e p q n -> p (e q) n")),
                                     (w2e[:, k, :, :], d["W2"][one].rearrange("e p q n -> p (e q) n")),
                                     (b1e[:, k, :], d["b1"][one].rearrange("e p q -> p (e q)")),
                                     (b2e[:, k, :], d["b2"][one, :].broadcast_to([P, D]))):
                        dma(dst, src, allow_slow_non_contiguous=True).then_inc(s[f"expert_loaded{k}"], 16)
                sp.wait_ge(s["x_done"], 1)
                dma(out[bass.ds(bi, 1), :, :].rearrange("a (t p) n -> p (a t) n", p=P), x[:, :, :])\
                    .then_inc(s["stored"], 16)
                sp.wait_ge(s["stored"], 16)
                clear()


INPUTS = ["L0_attn_mlp_w1", "L0_attn_mlp_w2", "L0_attn_mlp_w3", "L0_attn_mlp_wo"]


def layouts(v):
    g = {n: np.ascontiguousarray(v[n]) for n in v}
    tiles = lambda a, n: np.ascontiguousarray(a.reshape(n, P, -1).transpose(1, 0, 2))
    cols = lambda a: np.ascontiguousarray(a.reshape(-1, P).T)
    o = {"x": g["L0_attn_u"]}
    for n in INPUTS:
        o[n] = g[n]
    for n in ("L0_attn_mlp_b1", "L0_attn_mlp_b2", "L0_attn_mlp_b3", "L0_attn_freq"):
        o[n] = g[n].reshape(FILT, 1)
    o["L0_ffn_w1"] = tiles(g["L0_ffn_w1"], NH1)
    o["w1T"] = tiles(np.ascontiguousarray(g["L0_ffn_w1"].T), ND)
    o["w2T"] = tiles(np.ascontiguousarray(g["L0_ffn_w2"].T), NH1)
    o["in_w"] = tiles(g["L0_attn_in_w"], ND)
    o["out_w"] = tiles(g["L0_attn_out_w"], ND)
    o["wo"] = tiles(g["L1_attn_Wo"], HEADS * HD // P)
    o["wr"] = tiles(g["L1_ffn_Wr"], ND)
    o["L1_ffn_br"] = g["L1_ffn_br"].reshape(1, EXPERTS)
    o["in_b"] = cols(g["L0_attn_in_b"])
    o["short_w"] = tiles(g["L0_attn_short_w"], INNER // P)
    o["short_b"] = cols(g["L0_attn_short_b"])
    o["filt_b"] = cols(g["L0_attn_filt_bias"])
    o["ffn_b1"] = cols(g["L0_ffn_b1"])
    o["L0_attn_out_b"] = g["L0_attn_out_b"]
    o["L0_ffn_b2"] = g["L0_ffn_b2"]
    halves = lambda w, n: w.reshape(D, n, HD // 2, 2).transpose(0, 1, 3, 2).reshape(D, n, HD)
    q = halves(g["L1_attn_Wq"], HEADS).reshape(D, KV, GQ, HD)
    k = halves(g["L1_attn_Wk"], KV)[:, :, None]
    val = g["L1_attn_Wv"].reshape(D, KV, 1, HD)
    o["wqkv"] = np.ascontiguousarray(np.concatenate([q, k, val], axis=2).reshape(ND, P, KV, GW).transpose(1, 0, 2, 3))
    o["W1"] = np.ascontiguousarray(g["L1_ffn_W1"].reshape(EXPERTS, ND, P, D).transpose(0, 2, 1, 3))
    o["W2"] = np.ascontiguousarray(g["L1_ffn_W2"].reshape(EXPERTS, ND, P, D).transpose(0, 2, 1, 3))
    o["b1"] = np.ascontiguousarray(g["L1_ffn_b1"].reshape(EXPERTS, ND, P).transpose(0, 2, 1))
    o["b2"] = g["L1_ffn_b2"]
    o["cT"] = np.ascontiguousarray(np.stack([g["L0_c"].T, g["L1_c"].T]).reshape(2, ND, P, B).transpose(2, 0, 1, 3))
    o["wmod0"] = tiles(g["L0_wmod"], ND)
    o["wmod1"] = tiles(g["L1_wmod"], ND)
    return o


def kernel(**inputs):
    import concourse.bacc as bacc
    from concourse.bass_utils import run_bass_kernel_spmd

    arrays = layouts({n: np.asarray(a) for n, a in inputs.items()})
    arrays.update(shape_constants())
    nc = bacc.Bacc("TRN2", target_bir_lowering=False, num_devices=1)
    d = {n: nc.dram_tensor(f"in_{n}", a.shape, mybir.dt.from_np(a.dtype), kind="ExternalInput").ap()
         for n, a in arrays.items()}
    out = nc.dram_tensor("out", (B, L, D), F32, kind="ExternalOutput").ap()
    gate_scratch = nc.dram_tensor("gate_scratch", (B, 4 * D), F32, kind="Internal").ap()
    kf_scratch = nc.dram_tensor("kf_scratch", (P, NB * 2 * ST * D), F32, kind="Internal").ap()
    adaln_hyena_binffn_gqa_moe(nc, d, out, gate_scratch, kf_scratch)
    r = run_bass_kernel_spmd(nc, [{f"in_{n}": a for n, a in arrays.items()}], core_ids=[0])
    return r.results[0]["out"]
```

```python
from contextlib import ExitStack

import numpy as np

import concourse.bass as bass
from concourse import mybir

F32 = mybir.dt.float32
F32R = mybir.dt.float32r
U32 = mybir.dt.uint32
ALU = mybir.AluOpType
ACT = mybir.ActivationFunctionType
AX = mybir.AxisListType.X

P = 128
B, L, D = 4, 1024, 256
NT = L // P
ND = D // P
HALF = 512
NHALF = L // HALF
EPS = 1e-5

S = 256
NB = L // S
ST = S // P
FILT = 64
EMB = 3
INNER = 3 * D

HID = 1024
NH1 = HID // P

HEADS, KV, HD = 16, 4, 64
GQ = HEADS // KV
GW = (GQ + 2) * HD
QK = (GQ + 1) * HD
SCALE = HD ** -0.5
MASKED = -1e30
QRING = 2
PRING = 8

EXPERTS, TOPK = 8, 2

E_ORDER = (4, 5, 2, 3, 0, 1)
PAIRS = ((0, 0), (0, 1), (1, 1), (0, 2), (1, 2), (0, 3), (1, 3), (2, 2), (2, 3), (3, 3))
POOL_PAIRS = ((1, 1), (1, 2), (1, 3), (2, 2))
DVE_PAIRS = tuple(p for p in PAIRS if p not in POOL_PAIRS)
LN_FFN, LN_ATT, LN_MOE, LN_NEXT = range(4)
NLOADED = 19

PI_DOWN = 3.1415925
TWO_PI_HI = 6.28125
TWO_PI_LO = float(2 * np.pi - 6.28125)
ROUND = float(1.5 * 2 ** 23)


def shape_constants():
    n = np.arange(2 * S)[:, None]
    f = np.arange(S)[None, :] + 0.5
    ang = np.pi * ((n * (2 * f)) % (4 * S)) / (2 * S) * 1.0
    fwd = np.concatenate([np.cos(ang), np.sin(ang)], axis=1)
    fwd = fwd.reshape(2, ST, P, 2 * S).transpose(2, 0, 1, 3)
    inv = np.concatenate([np.cos(ang[S:]), np.sin(ang[S:])], axis=1).T / S
    inv = inv.reshape(2 * ST, P, S).transpose(1, 0, 2)
    t = np.linspace(0.0, 1.0, L, dtype=np.float32)[:, None]
    tr = np.linspace(0.0, L - 1.0, L, dtype=np.float32)[:, None]
    w = (2.0 * np.pi * tr / L).astype(np.float32)
    fr = np.float32(0.0001)
    z = np.concatenate([t, np.cos(fr * w), -np.sin(fr * w)], axis=-1)
    deltas = np.linspace(np.log(0.01) / 1.5, np.log(0.01) / 0.3, D, dtype=np.float32)[None, :]
    decay = np.exp(-t * np.abs(deltas)).reshape(NT, P, D).transpose(1, 0, 2)
    inv_freq = np.float32(1.0) / np.float32(10000.0) ** (np.arange(0, HD, 2, dtype=np.float32) / np.float32(HD))
    freqs = np.arange(L, dtype=np.float32)[:, None] * inv_freq[None, :]
    emb = np.concatenate([freqs, freqs], axis=-1)
    cos, sin = np.cos(emb)[:, 0::2], np.sin(emb)[:, 0::2]
    rope = np.stack([cos, sin], axis=1).reshape(NT, P, 2, HD // 2).transpose(1, 0, 2, 3)
    c = lambda a: np.ascontiguousarray(a, dtype=np.float32)
    return {"fwd": c(fwd), "inv": c(inv), "zT": c(z.T), "decay": c(decay), "rope": c(rope)}


def adaln_hyena_binffn_gqa_moe(nc, d, out, gate_scratch, kf_scratch, scratch):
    es = ExitStack()
    with es:
        def sb(name, shape, dt=F32, stack=es):
            return stack.enter_context(nc.sbuf_tensor(name, shape, dt))

        def sem(name):
            return es.enter_context(nc.semaphore(name))

        x = sb("x", [P, NT, D])
        ident = sb("ident", [P, P])
        wqkv = sb("wqkv", [P, 2, ND, KV, GW], F32R)
        wo = sb("wo", [P, HEADS * HD // P, D])
        rope = sb("rope", [P, NT, 2, HD // 2])
        mrow = sb("mrow", [P, L])
        wr = sb("wr", [P, 2, ND, EXPERTS], F32R)
        br = sb("br", [1, EXPERTS])
        in_b = sb("in_b", [P, INNER // P])
        short_w = sb("short_w", [P, INNER // P, 3])
        short_b = sb("short_b", [P, INNER // P])
        filt_b = sb("filt_b", [P, ND])
        ffn_b1 = sb("ffn_b1", [P, NH1])
        alpha1 = sb("alpha1", [P, NH1])
        rows = sb("rows", [P, 2, D])
        alpha2 = sb("alpha2", [P, D])
        modT = sb("modT", [P, 2, 4, ND, B])
        modb = sb("modb", [P, 2, 4, ND])
        modn = sb("modn", [P, 2, ND])
        gates = sb("gates", [P, 4, D])
        terms = sb("terms", [P, 3, D])
        escale = sb("escale", [P, 2, D])
        neghalf = sb("neghalf", [P, NT])
        stat = sb("stat", [P, NT, 6])
        mv = sb("mv", [P, NT, 2])
        var = sb("var", [P, NT])
        rstd = sb("rstd", [P, NT])
        hT = sb("hT", [P, 2, ND, L], F32R)
        hfull = sb("hfull", [P, 2, HALF])
        hrow = sb("hrow", [P, NT, D])
        tmp = sb("tmp", [P, 2, 2, D])

        with ExitStack() as a:
            in_w = sb("in_w", [P, 2, ND, INNER], F32R, a)
            sgn1 = sb("sgn1", [P, ND, HID], F32R, a)
            sgn2 = sb("sgn2", [P, NH1, D], F32R, a)
            out_w = sb("out_w", [P, ND, D], F32, a)
            fwd = sb("fwd", [P, ST, 2 * S], F32, a)
            inv = sb("inv", [P, 2 * ST, S], F32, a)
            with ExitStack() as ak:
                Kf = sb("Kf", [P, NB, 2, ST, D], F32, ak)
                with ExitStack() as a0:
                    fwd_old = sb("fwd_old", [P, ST, 2 * S], F32, a0)
                    kern = sb("kern", [P, NT, D], F32, a0)
                    decay = sb("decay", [P, NT, D], F32, a0)
                    w2T = sb("w2T", [P, NH1, D], F32, a0)
                    fw1 = sb("fw1", [EMB, FILT], F32, a0)
                    fw23 = sb("fw23", [FILT, 2, FILT], F32, a0)
                    fwo = sb("fwo", [FILT, D], F32, a0)
                    fb = sb("fb", [FILT, 4], F32, a0)
                    ang = sb("ang", [FILT, L], F32, a0)
                    sine = sb("sine", [FILT, L], F32, a0)
                    wraw = sb("wraw", [P, ND, 6 * D], F32, a0)
                    wr_raw = sb("wr_raw", [P, ND, EXPERTS], F32, a0)
                    cT = sb("cT", [P, 2, ND, B], F32, a0)
                    grow = sb("grow", [B, 2, 2 * D], F32, a0)
                    ones = sb("ones", [P, P], F32, a0)
                    with ExitStack() as a01:
                        zT = sb("zT", [EMB, L], F32, a01)
                    with ExitStack() as a02:
                        gabs = sb("gabs", [B, 2 * D], F32, a02)
                        gsgn = sb("gsgn", [B, 2 * D], F32, a02)
                with ExitStack() as a1:
                    x1 = sb("x1", [P, L], F32, a1)
                    x0 = sb("x0", [P, ND, L], F32, a1)
                    vx = sb("vx", [P, ND, L], F32, a1)
                    vrow = sb("vrow", [P, NT, D], F32, a1)
                    Yf = sb("Yf", [P, NB, 2, ST, D], F32, a1)
                    with ExitStack() as a11:
                        up = sb("up", [P, 2, L + 2], F32, a11)
                        tap = sb("tap", [P, 2, L], F32, a11)
                    with ExitStack() as a12:
                        prod = sb("prod", [P, 2, 2, 2, ST, D], F32, a12)
            turn, w1rows = sine, hrow
            with ExitStack() as a2:
                gfull = sb("gfull", [P, 4, HALF], F32, a2)
                gT = sb("gT", [P, 2, NH1, L], F32R, a2)
        with ExitStack() as a:
            with ExitStack() as a3:
                qhh = sb("qhh", [P, QRING, L], F32R, a3)
                q2 = sb("q2", [HD + 1, QRING, L], F32R, a3)
                khl = sb("khl", [P, 2, L], F32R, a3)
                k2 = sb("k2", [HD + 1, 2, L], F32R, a3)
                v1 = sb("v1", [P, 2, NT, HD + 1], F32, a3)
                oT = sb("oT", [P, HEADS * HD // P, L], F32, a3)
                pT = sb("pT", [P, PRING, HALF], F32, a3)
                rprod = sb("rprod", [P, 4, QK], F32, a3)
                rot = sb("rot", [P, NT, QK], F32, a3)
                orow = sb("orow", [P, NT, P], F32, a3)
                mx = sb("mx", [P, 2, NT], F32, a3)
                nm = sb("nm", [P, 2, NT], F32, a3)
                nmr = sb("nmr", [NT, 2, P], F32R, a3)
                den = sb("den", [P, 2, 4], F32, a3)
        with ExitStack() as a:
            skip = sb("skip", [P, 58 * 256], F32, a)
            assert skip.shape[1] * 4 >= 4 * (2 * ND * INNER + ND * HID + NH1 * D + ND * D + ST * 2 * S + 2 * ST * S
                                             + NB * 2 * ST * D)
            w1e = sb("w1e", [P, TOPK, ND, D], F32, a)
            w1s = sb("w1s", [P, TOPK, 2, ND, D], F32R, a)
            w2e = sb("w2e", [P, TOPK, ND, D], F32, a)
            b1e = sb("b1e", [P, TOPK, ND], F32, a)
            b2e = sb("b2e", [P, TOPK, D], F32, a)
            xn = sb("xn", [P, NT, D], F32, a)
            geT = sb("geT", [P, TOPK * ND, L], F32, a)
            score = sb("score", [1, EXPERTS], F32, a)
            top = sb("top", [1, 8], F32, a)
            topi = sb("topi", [1, 8], U32, a)

        def rot_buf(r):
            return [rprod[:, 2 * r + k, :].rearrange("p (h e i) -> p h e i", e=2, i=HD // 2)
                    for k in range(2)]

        def rotated(t):
            return rot[:, t, :]

        ps = es.enter_context(nc.psum_tensor("ps", [P, 8, HALF], F32))

        bar = sem("bar")
        go = {e: sem("go_" + e) for e in ("tensor", "vector", "scalar", "gpsimd")}
        first_cleared = None
        names = ["loaded", "loaded_filter", "loaded_c",  "const_made", "filter_angle", "filter_sine", "kern_done",
                 "kf_done",  "abs_done", "silu_done", "mod_done", "gate_rows", "gate_stored", "mod_picked",
                 "x_loaded", "x_next_loaded", "gates_loaded", "gates_mixed", "var_done", "rstd_done", "hrow_done", "hT_done",
                 "bias_added", "tap_done", "conv_done", "vx_done", "vrow_done", "prod_done", 
                 "y_dve", "y_pool", "yv_done", "g_hi_done", "g_lo_done", "h_lo_done", "w1_split", "sgn_done", "raw_used", "loaded_raw", "l0_loaded", "rot_a", "rot_done", "v_done", "q_done", "q_lo_done",
                 "k_done", "k_lo_done", "nm_done", "nmr_done", "m_loaded0", "m_loaded1", "exp_done", "masked_done", 
                 "o_done", "oT_done", "top_done", "expert_loaded0", "expert_loaded1", "eb_mixed", "egelu_done", "x_done", "stored"]
        s = {}
        for n in names:
            s[n] = sem(n)
        ready = [sem(f"ready{i}") for i in range(8)]
        freed = [sem(f"freed{i}") for i in range(8)]
        cleared = list(s.values()) + ready + freed
        nums = [q.num for q in cleared]
        assert nums == list(range(nums[0], nums[0] + len(nums)))

        def m_loaded(u):
            return s[f"m_loaded{u % QRING}"], 16 * (u // QRING + 1)

        class Banks:
            def __init__(self):
                self.reset()

            def reset(self):
                self.at, self.uses, self.frees, self.owner, self.chunk = 0, [0] * 8, [0] * 8, [None] * 8, {}

            def take(self, pe, key, n=1, until=None):
                while self.at % n:
                    self.at += 1
                b = self.at % 8
                for q in range(b, b + n):
                    if self.owner[q] is not None:
                        pe.wait_ge(*self.owner[q])
                self.uses[b] += 1
                if until is None:
                    self.frees[b] += 1
                    until = (freed[b], self.frees[b])
                for q in range(b, b + n):
                    self.owner[q] = until
                self.at += n
                self.chunk[key] = (b, self.uses[b])
                return b

            def wait(self, eng, key):
                b, use = self.chunk[key]
                eng.wait_ge(ready[b], use)
                return b

        banks = {"setup": Banks(), "batch": Banks()}

        def part_ends(eng, name):
            eng.drain().then_inc(bar, 1)
            eng.wait_ge(go[name], 1)
            eng.sem_clear(go[name])

        block = es.enter_context(nc.Block())

        @block.tensor
        def _(pe):
            mm, tr = nc.tensor.matmul, nc.tensor.transpose

            def split_mm(o, lhs, rhs, tiles):
                pairs = [(a, c, q) for q in range(tiles) for a, c in ((0, 0), (0, 1), (1, 0))]
                for n, (a, c, q) in enumerate(pairs):
                    i = mm(o, lhs(a, q), rhs(c, q), start=n == 0, stop=n == len(pairs) - 1)
                return i

            def sign_mm(o, lhs, rhs, pairs):
                for n, (a, q) in enumerate(pairs):
                    i = mm(o, lhs(a, q), rhs(a, q), start=n == 0, stop=n == len(pairs) - 1)
                return i
            bk = banks["setup"]
            pe.wait_ge(s["loaded_filter"], 16 * 9)
            for layer in range(3):
                if layer:
                    pe.wait_ge(s["filter_sine"], layer)
                for h in range(NHALF):
                    b = bk.take(pe, ("filter", layer, h))
                    w = fw1[:, :] if layer == 0 else fw23[:, layer - 1, :]
                    src = zT if layer == 0 else sine
                    mm(ps[0:FILT, b, :], w, src[:, h * HALF:(h + 1) * HALF], start=True, stop=True)\
                        .then_inc(ready[b], 1)
            pe.wait_ge(s["filter_sine"], 3)
            for t in range(0, NT, 2):
                b = bk.take(pe, ("kern", t), until=(s["kern_done"], t // 2 + 1))
                for u in range(2):
                    i = mm(ps[:, b, u * D:(u + 1) * D], sine[:, (t + u) * P:(t + u + 1) * P], fwo[:, :],
                           start=True, stop=True)
                i.then_inc(ready[b], 1)
            pe.wait_ge(s["loaded"], 16 * NLOADED)
            pe.wait_ge(s["kern_done"], NT // 2)
            for m in range(NB):
                for c in range(2):
                    b = bk.take(pe, ("kf", m, c))
                    for ft in range(ST):
                        col = (c * ST + ft) * P
                        terms_ = [(fwd_old, ST * m + q, q) for q in range(ST)]
                        if m:
                            terms_ += [(fwd, ST * (m - 1) + q, q) for q in range(ST)]
                        for n, (tab, t, q) in enumerate(terms_):
                            i = mm(ps[:, b, ft * D:(ft + 1) * D], tab[:, q, col:col + P], kern[:, t, :],
                                   start=n == 0, stop=n == len(terms_) - 1)
                    i.then_inc(ready[b], 1)
            pe.wait_ge(s["const_made"], 1)
            pe.wait_ge(s["abs_done"], 1)
            b = bk.take(pe, ("alpha2",))
            for q in range(NH1):
                i = mm(ps[:, b, 0:D], ones[:, :], w2T[:, q, :], start=q == 0, stop=q == NH1 - 1)
            i.then_inc(ready[b], 1)
            pe.wait_ge(s["silu_done"], 1)
            for layer in range(2):
                pe.wait_ge(s["loaded_raw"], 16 * (layer + 1))
                b = bk.take(pe, ("modT", layer))
                for n, kind in enumerate((0, 1, 3, 4)):
                    for dt in range(ND):
                        o = (n * ND + dt) * B
                        for q in range(ND):
                            i = mm(ps[:, b, o:o + B], wraw[:, q, kind * D + dt * P:kind * D + (dt + 1) * P],
                                   cT[:, layer, q, :], start=q == 0, stop=q == ND - 1)
                i.then_inc(ready[b], 1)
                b = bk.take(pe, ("gate", layer))
                for n, kind in enumerate((2, 5)):
                    for q in range(ND):
                        i = mm(ps[0:B, b, n * D:(n + 1) * D], cT[:, layer, q, :],
                               wraw[:, q, kind * D:(kind + 1) * D], start=q == 0, stop=q == ND - 1)
                i.then_inc(ready[b], 1)

            def normed(k, h):
                for dt in range(ND):
                    b = bk.take(pe, ("ln", k, h, dt), until=(s["hT_done"], (k * NHALF + h) * ND + dt + 1))
                    for u in range(4):
                        t = 4 * h + u
                        if dt == 0:
                            pe.wait_ge(s["hrow_done"], k * NT + t + 1)
                        i = tr(ps[:, b, u * P:(u + 1) * P], hrow[:, t, dt * P:(dt + 1) * P], ident[:, :])
                    i.then_inc(ready[b], 1)

            for h in range(NHALF):
                normed(0, h)
            part_ends(pe, "tensor")

            bk = banks["batch"]

            def h_ready(k, h):
                pe.wait_ge(s["h_lo_done"], (k * NHALF + h + 1) * ND)

            def project(g, tiles=range(NT)):
                for t in tiles:
                    b = bk.take(pe, ("qkv", g, t), until=(s["v_done"], g * NT + t + 1))
                    split_mm(ps[:, b, 0:GW], lambda a, q: hT[:, a, q, t * P:(t + 1) * P],
                             lambda a, q: wqkv[:, a, q, g, :], ND).then_inc(ready[b], 1)

            def turn_rows(g, slot, key, done, n):
                pe.wait_ge(s["rot_done"], (g + 1) * NT)
                for h in range(NHALF):
                    b = bk.take(pe, key + (h,), until=(done, NHALF * n + h + 1))
                    for u in range(4):
                        i = tr(ps[0:HD, b, u * P:(u + 1) * P], rotated(4 * h + u)[:, slot * HD:(slot + 1) * HD],
                               ident[:, :])
                    i.then_inc(ready[b], 1)

            def turn_head(u):
                if u % GQ == 0:
                    turn_rows(u // GQ, GQ, ("k", u // GQ), s["k_lo_done"], u // GQ)
                turn_rows(u // GQ, u % GQ, ("q", u), s["q_lo_done"], u)

            def score_rows(u, i):
                g, r, n = u // GQ, u % QRING, (i + 1) * P
                b = bk.take(pe, ("rows", u, i), 1 if n <= HALF else 2)
                if i == 0:
                    pe.wait_ge(s["q_done"], NHALF * (u + 1))
                    pe.wait_ge(s["k_lo_done"], NHALF * (g + 1))
                for c in range(0, n, HALF):
                    e = min(n, c + HALF)
                    q = mm(ps[:, b + c // HALF, 0:e - c], qhh[:, r, i * P:(i + 1) * P], khl[:, g % 2, c:e],
                           start=True, stop=True)
                q.then_inc(ready[b], 1)

            def turn_maxima(u):
                b = bk.take(pe, ("nm", u), until=(s["nmr_done"], u + 1))
                pe.wait_ge(s["nm_done"], u + 1)
                tr(ps[0:NT, b, 0:P], nm[:, u % 2, :], ident[:, :]).then_inc(ready[b], 1)

            def score_cols(u, c, j):
                g, r = u // GQ, u % QRING
                lo, hi = max(c * HALF, j * P), (c + 1) * HALF
                b = bk.take(pe, ("cols", u, c, j), until=(s["exp_done"], 12 * u + 4 * c + j + 1))
                if c == 0 and j == 0:
                    pe.wait_ge(s["q_lo_done"], NHALF * (u + 1))
                    pe.wait_ge(*m_loaded(u))
                mm(ps[:, b, 0:hi - lo], khl[:, g % 2, j * P:(j + 1) * P], qhh[:, r, lo:hi], start=True, stop=False)
                mm(ps[:, b, 0:hi - lo], k2[:, g % 2, j * P:(j + 1) * P], q2[:, r, lo:hi], start=False, stop=True)\
                    .then_inc(ready[b], 1)

            def values(u, c, i, b):
                g = u // GQ
                if i == 0 and u % GQ == 0:
                    pe.wait_ge(s["v_done"], (g + 1) * NT)
                pe.wait_ge(s["masked_done"], NT * u + i + 1)
                for j in range(i + 1):
                    lo = max(c * HALF, j * P)
                    slot = (12 * u + 4 * c + j) % PRING
                    q = mm(ps[:, b, (i % 4) * (HD + 1):(i % 4 + 1) * (HD + 1)],
                           pT[:, slot, i * P - lo:(i + 1) * P - lo], v1[:, g % 2, j, :],
                           start=j == 0, stop=j == i)
                return q

            def turn_outputs(w):
                for h in range(NHALF):
                    b = bk.take(pe, ("o", w, h), until=(s["oT_done"], NHALF * w + h + 1))
                    pe.wait_ge(s["o_done"], 4 * w + 2 + h + 1)
                    for u in range(4):
                        i = tr(ps[:, b, u * P:(u + 1) * P], orow[:, 4 * h + u, :], ident[:, :])
                    i.then_inc(ready[b], 1)

            with pe.Fori(0, B):
                bk.reset()
                for n, e in enumerate(E_ORDER):
                    for h in range(NHALF):
                        b = bk.take(pe, ("up", n, h))
                        split_mm(ps[:, b, :], lambda a, q: in_w[:, a, q, e * P:(e + 1) * P],
                                 lambda a, q: hT[:, a, q, h * HALF:(h + 1) * HALF], ND).then_inc(ready[b], 1)
                pe.wait_ge(s["vx_done"], ND)
                for t in range(0, NT, 2):
                    b = bk.take(pe, ("vrow", t), until=(s["vrow_done"], t // 2 + 1))
                    for u in range(2):
                        for dt in range(ND):
                            i = tr(ps[:, b, (u * ND + dt) * P:(u * ND + dt + 1) * P],
                                   vx[:, dt, (t + u) * P:(t + u + 1) * P], ident[:, :])
                    i.then_inc(ready[b], 1)
                vblocks = vrow[:, :, :].rearrange("p (j q) n -> p j q n", q=ST)
                for jp in range(NB // 2):
                    pe.wait_ge(s["vrow_done"], 2 * (jp + 1))
                    b = bk.take(pe, ("vf", jp), 4, until=(s["prod_done"], POOL_PAIRS.index((1, 3)) + 1) if jp == 0 else None)
                    for c in range(2 * ST):
                        for q in range(ST):
                            i = mm(ps[:, b + c, :], fwd[:, q, c * P:(c + 1) * P], vblocks[:, 2 * jp:2 * jp + 2, q, :],
                                   start=q == 0, stop=q == ST - 1)
                    i.then_inc(ready[b], 1)
                for ip in range(NB // 2):
                    for dt in range(ND):
                        b = bk.take(pe, ("y", ip, dt))
                        for u in range(2):
                            blk = 2 * ip + u
                            pe.wait_ge(s["y_dve"], 1 + max(n for n, p in enumerate(DVE_PAIRS) if p[1] == blk))
                            if blk:
                                pe.wait_ge(s["y_pool"], 1 + max(n for n, p in enumerate(POOL_PAIRS) if p[1] == blk))
                            for q in range(2 * ST):
                                i = mm(ps[:, b, u * S:(u + 1) * S], Yf[:, blk, q // ST, q % ST, dt * P:(dt + 1) * P],
                                       inv[:, q, :], start=q == 0, stop=q == 2 * ST - 1)
                        i.then_inc(ready[b], 1)
                for t in range(0, NT, 2):
                    b = bk.take(pe, ("out0", t))
                    pe.wait_ge(s["yv_done"], ND * (t // 4 + 1))
                    for u in range(2):
                        for q in range(ND):
                            i = mm(ps[:, b, u * D:(u + 1) * D], x0[:, q, (t + u) * P:(t + u + 1) * P], out_w[:, q, :],
                                   start=q == 0, stop=q == ND - 1)
                    i.then_inc(ready[b], 1)
                for h in range(NHALF):
                    normed(LN_FFN, h)
                    h_ready(LN_FFN, h)
                    for n in range(NH1):
                        b = bk.take(pe, ("ffn1", h, n), until=(s["g_hi_done"], h * NH1 + n + 1))
                        sign_mm(ps[:, b, :], lambda a, q: sgn1[:, q, n * P:(n + 1) * P],
                                lambda a, q: hT[:, a, q, h * HALF:(h + 1) * HALF],
                                [(a, q) for q in range(ND) for a in range(2)]).then_inc(ready[b], 1)
                for t in range(0, NT, 2):
                    b = bk.take(pe, ("ffn2", t))
                    for u in range(2):
                        if u == 0 and t % 4 == 0:
                            pe.wait_ge(s["g_lo_done"], NH1 * (t // 4 + 1))
                        i = sign_mm(ps[:, b, u * D:(u + 1) * D],
                                    lambda a, q: gT[:, a, q, (t + u) * P:(t + u + 1) * P],
                                    lambda a, q: sgn2[:, q, :], [(a, q) for q in range(NH1) for a in range(2)])
                    i.then_inc(ready[b], 1)
                for h in range(NHALF):
                    normed(LN_ATT, h)
                    h_ready(LN_ATT, h)
                    project(0, range(4 * h, 4 * h + 4))
                turn_head(0)
                for i in range(NT):
                    score_rows(0, i)
                turn_maxima(0)
                for u in range(HEADS):
                    w = u + 1
                    for j in range(4):
                        score_cols(u, 0, j)
                    if w < HEADS:
                        turn_head(w)
                    if u >= 2 and u % 2 == 0:
                        turn_outputs(u // 2 - 1)
                    if u % GQ == 2 and u // GQ + 1 < KV:
                        project(u // GQ + 1)
                    for j in range(4):
                        score_cols(u, 1, j)
                    b = bk.take(pe, ("pv", u, 0), until=(s["o_done"], 2 * u + 1))
                    for i in range(4):
                        q = values(u, 0, i, b)
                    q.then_inc(ready[b], 1)
                    if w < HEADS:
                        for i in range(4):
                            score_rows(w, i)
                    for j in range(4, NT):
                        score_cols(u, 1, j)
                        if w < HEADS:
                            score_rows(w, j)
                    b = bk.take(pe, ("pv", u, 1), until=(s["o_done"], 2 * u + 2))
                    for i in range(4, NT):
                        if i == 6 and w < HEADS:
                            turn_maxima(w)
                        q = values(u, 1, i, b)
                    q.then_inc(ready[b], 1)
                turn_outputs(HEADS // 2 - 1)
                for t in range(0, NT, 2):
                    b = bk.take(pe, ("out1", t))
                    pe.wait_ge(s["oT_done"], HEADS - 1 + t // 4)
                    for u in range(2):
                        for q in range(HEADS // 2):
                            i = mm(ps[:, b, u * D:(u + 1) * D], oT[:, q, (t + u) * P:(t + u + 1) * P], wo[:, q, :],
                                   start=q == 0, stop=q == HEADS // 2 - 1)
                    i.then_inc(ready[b], 1)
                normed(LN_MOE, 0)
                h_ready(LN_MOE, 0)
                b = bk.take(pe, ("router",))
                split_mm(ps[0:1, b, 0:EXPERTS], lambda a, q: hT[:, a, q, 0:1], lambda a, q: wr[:, a, q, :], ND)\
                    .then_inc(ready[b], 1)
                normed(LN_MOE, 1)
                h_ready(LN_MOE, 1)
                for k in range(TOPK):
                    pe.wait_ge(s["w1_split"], k + 1)
                    for h in range(NHALF):
                        for n in range(ND):
                            b = bk.take(pe, ("moe1", k, h, n), until=(s["egelu_done"], (k * NHALF + h) * ND + n + 1))
                            split_mm(ps[:, b, :], lambda a, q: w1s[:, k, a, q, n * P:(n + 1) * P],
                                     lambda a, q: hT[:, a, q, h * HALF:(h + 1) * HALF], ND).then_inc(ready[b], 1)
                for h in range(NHALF):
                    normed(LN_NEXT, h)
                for t in range(0, NT, 2):
                    b = bk.take(pe, ("moe2", t))
                    pe.wait_ge(s["egelu_done"], ND * NHALF + ND * (t // 4 + 1))
                    for u in range(2):
                        for n in range(TOPK * ND):
                            i = mm(ps[:, b, u * D:(u + 1) * D], geT[:, n, (t + u) * P:(t + u + 1) * P],
                                   w2e[:, n // ND, n % ND, :], start=n == 0, stop=n == TOPK * ND - 1)
                    i.then_inc(ready[b], 1)
                part_ends(pe, "tensor")

        @block.scalar
        def _(act):
            A = nc.scalar.activation
            bk = banks["setup"]

            act.wait_ge(s["loaded"], 16 * NLOADED)
            A(sgn1[:, :, :], x[:, :, :].rearrange("p t n -> p (t n)").rearrange("p (q n) -> p q n", q=ND), ACT.Sign)\
                .then_inc(s["sgn_done"], 1)
            A(sgn2[:, :, :], w2T[:, :, :], ACT.Sign).then_inc(s["sgn_done"], 1)
            act.drain()
            A(w2T[:, :, :], w2T[:, :, :], ACT.Abs).then_inc(s["abs_done"], 1)
            act.wait_ge(s["loaded_c"], 16)
            A(cT[:, :, :, :], cT[:, :, :, :], ACT.Silu).then_inc(s["silu_done"], 1)
            for layer in range(3):
                act.wait_ge(s["filter_angle"], layer + 1)
                A(sine[:, :], ang[:, :], ACT.Sin).then_inc(s["filter_sine"], 1)
            for m in range(NB):
                for c in range(2):
                    b = bk.wait(act, ("kf", m, c))
                    A(Kf[:, m, c, :, :], ps[:, b, :].rearrange("p (f n) -> p f n", f=ST), ACT.Copy)\
                        .then_inc(freed[b], 1)
            act.drain().then_inc(s["kf_done"], 1)
            b = bk.wait(act, ("alpha2",))
            A(alpha2[:, :], ps[:, b, 0:D], ACT.Copy, scale=1.0 / HID).then_inc(freed[b], 1)

            def normed(k, h, mod):
                for dt in range(ND):
                    n = (k * NHALF + h) * ND + dt
                    b = bk.wait(act, ("ln", k, h, dt))
                    if n >= 2:
                        act.wait_ge(s["h_lo_done"], n - 1)
                    args = {"bias": mod[:, 0, dt:dt + 1], "scale": mod[:, 1, dt:dt + 1]}
                    A(hfull[:, n % 2, :], ps[:, b, :], ACT.Identity, **args)
                    A(hT[:, 0, dt, h * HALF:(h + 1) * HALF], ps[:, b, :], ACT.Identity, **args)\
                        .then_inc(s["hT_done"], 1)

            act.wait_ge(s["mod_picked"], 1)
            for h in range(NHALF):
                normed(0, h, modn)
            part_ends(act, "scalar")

            bk = banks["batch"]

            def turn_head(u):
                g = u // GQ
                if u >= QRING:
                    bk.wait(act, ("pv", u - QRING, 1))
                if u % GQ == 0:
                    for h in range(NHALF):
                        b = bk.wait(act, ("k", g, h))
                        cols = slice(h * HALF, (h + 1) * HALF)
                        A(khl[0:HD, g % 2, cols], ps[0:HD, b, :], ACT.Copy)
                        A(k2[0:HD, g % 2, cols], ps[0:HD, b, :], ACT.Copy).then_inc(s["k_done"], 1)
                for h in range(NHALF):
                    b = bk.wait(act, ("q", u, h))
                    for half in (HD, 0):
                        i = A(qhh[half:half + HD, u % QRING, h * HALF:(h + 1) * HALF], ps[0:HD, b, :], ACT.Copy)
                    i.then_inc(s["q_done"], 1)

            def turn_maxima(u):
                b = bk.wait(act, ("nm", u))
                if u >= 2:
                    act.wait_ge(*m_loaded(u - 2))
                A(nmr[:, u % 2, :], ps[0:NT, b, 0:P], ACT.Copy).then_inc(s["nmr_done"], 1)

            def exps(u, c, j):
                n = 12 * u + 4 * c + j
                lo = max(c * HALF, j * P)
                b = bk.wait(act, ("cols", u, c, j))
                if (c, j) == (0, 0) and u:
                    bk.wait(act, ("pv", u - 1, 1))
                if (c, j) == (1, PRING - 4):
                    bk.wait(act, ("pv", u, 0))
                A(pT[:, n % PRING, 0:(c + 1) * HALF - lo], ps[:, b, 0:(c + 1) * HALF - lo], ACT.Exp, scale=SCALE)\
                    .then_inc(s["exp_done"], 1)

            def value_rows(g, tiles=range(NT)):
                for t in tiles:
                    b = bk.wait(act, ("qkv", g, t))
                    act.wait_ge(s["rot_a"], g * NT + t + 1)
                    A(v1[:, g % 2, t, 0:HD], ps[:, b, QK:GW], ACT.Copy).then_inc(s["v_done"], 1)

            def turn_outputs(w):
                for h in range(NHALF):
                    b = bk.wait(act, ("o", w, h))
                    A(oT[:, w, h * HALF:(h + 1) * HALF], ps[:, b, :], ACT.Copy).then_inc(s["oT_done"], 1)

            with act.Fori(0, B):
                for n, e in enumerate(E_ORDER):
                    if n >= 2:
                        act.wait_ge(s["conv_done"], n - 1)
                    for h in range(NHALF):
                        b = bk.wait(act, ("up", n, h))
                        A(up[:, n % 2, 2 + h * HALF:2 + (h + 1) * HALF], ps[:, b, :], ACT.Identity,
                          bias=in_b[:, e:e + 1]).then_inc(freed[b], 1)
                    act.drain()
                    A(tap[:, n % 2, :], up[:, n % 2, 2:L + 2], ACT.Identity, scale=short_w[:, e, 2:3],
                      bias=short_b[:, e:e + 1]).then_inc(s["tap_done"], 1)
                for t in range(0, NT, 2):
                    b = bk.wait(act, ("vrow", t))
                    A(vrow[:, t:t + 2, :], ps[:, b, :].rearrange("p (t n) -> p t n", t=2), ACT.Copy)\
                        .then_inc(s["vrow_done"], 1)
                act.wait_ge(s["mod_picked"], 1)
                for h in range(NHALF):
                    normed(LN_FFN, h, modb[:, 0, 2:4])
                    for n in range(NH1):
                        b = bk.wait(act, ("ffn1", h, n))
                        m = h * NH1 + n
                        if m >= 4:
                            act.wait_ge(s["g_lo_done"], m - 3)
                        A(gfull[:, m % 4, :], ps[:, b, :], ACT.Gelu, scale=alpha1[:, n:n + 1],
                          bias=ffn_b1[:, n:n + 1])
                        A(gT[:, 0, n, h * HALF:(h + 1) * HALF], ps[:, b, :], ACT.Gelu, scale=alpha1[:, n:n + 1],
                          bias=ffn_b1[:, n:n + 1]).then_inc(s["g_hi_done"], 1)
                for h in range(NHALF):
                    normed(LN_ATT, h, modb[:, 1, 0:2])
                    value_rows(0, range(4 * h, 4 * h + 4))
                turn_head(0)
                turn_maxima(0)
                for u in range(HEADS):
                    w = u + 1
                    for j in range(4):
                        exps(u, 0, j)
                    if w < HEADS:
                        turn_head(w)
                    if u >= 2 and u % 2 == 0:
                        turn_outputs(u // 2 - 1)
                    if u % GQ == 2 and u // GQ + 1 < KV:
                        value_rows(u // GQ + 1)
                    for j in range(NT):
                        exps(u, 1, j)
                    if w < HEADS:
                        turn_maxima(w)
                turn_outputs(HEADS // 2 - 1)
                for h in range(NHALF):
                    normed(LN_MOE, h, modb[:, 1, 2:4])
                for k in range(TOPK):
                    act.wait_ge(s[f"expert_loaded{k}"], 16 * 4)
                    for h in range(NHALF):
                        for n in range(ND):
                            b = bk.wait(act, ("moe1", k, h, n))
                            A(geT[:, k * ND + n, h * HALF:(h + 1) * HALF], ps[:, b, :], ACT.Gelu,
                              bias=b1e[:, k, n:n + 1]).then_inc(s["egelu_done"], 1)
                for h in range(NHALF):
                    normed(LN_NEXT, h, modn)
                part_ends(act, "scalar")

        @block.vector
        def _(dve):
            V = nc.vector
            bk = banks["setup"]
            dve.wait_ge(s["loaded_filter"], 16 * 9)
            for layer in range(3):
                if layer:
                    dve.wait_ge(s["filter_sine"], layer)
                for h in range(NHALF):
                    b = bk.wait(dve, ("filter", layer, h))
                    V.tensor_scalar(ang[:, h * HALF:(h + 1) * HALF], ps[0:FILT, b, :], fb[:, layer:layer + 1],
                                    fb[:, 3:4], ALU.add, ALU.mult).then_inc(freed[b], 1)
                dve.drain()
                V.tensor_scalar(turn[:, :], ang[:, :], float(1 / (2 * np.pi)), ROUND, ALU.mult, ALU.add)
                dve.drain()
                V.tensor_scalar(turn[:, :], turn[:, :], ROUND, None, ALU.subtract)
                dve.drain()
                V.scalar_tensor_tensor(out=ang[:, :], in0=turn[:, :], scalar=-TWO_PI_HI, in1=ang[:, :],
                                       op0=ALU.mult, op1=ALU.add)
                dve.drain()
                V.scalar_tensor_tensor(out=ang[:, :], in0=turn[:, :], scalar=-TWO_PI_LO, in1=ang[:, :],
                                       op0=ALU.mult, op1=ALU.add)
                dve.drain()
                V.tensor_scalar(ang[:, :], ang[:, :], PI_DOWN, -PI_DOWN, ALU.min, ALU.max)\
                    .then_inc(s["filter_angle"], 1)
            dve.wait_ge(s["loaded"], 16 * NLOADED)
            for t in range(0, NT, 2):
                b = bk.wait(dve, ("kern", t))
                V.tensor_tensor(kern[:, t:t + 2, :], ps[:, b, :].rearrange("p (t n) -> p t n", t=2),
                                decay[:, t:t + 2, :], ALU.mult).then_inc(s["kern_done"], 1)
            V.reduce_sum(alpha1[:, :], w1rows[:, :, :], AX, apply_absolute_value=True)
            dve.drain()
            V.tensor_scalar(alpha1[:, :], alpha1[:, :], 1.0 / D, None, ALU.mult)
            for layer in range(2):
                b = bk.wait(dve, ("modT", layer))
                V.tensor_copy(modT[:, layer, :, :, :].rearrange("p k t b -> p (k t b)"), ps[:, b, 0:4 * ND * B])\
                    .then_inc(freed[b], 1)
                dve.drain()
                for k in (1, 3):
                    V.tensor_scalar(modT[:, layer, k, :, :], modT[:, layer, k, :, :], 1.0, None, ALU.add)
                b = bk.wait(dve, ("gate", layer))
                V.tensor_copy(grow[:, layer, :], ps[0:B, b, :]).then_inc(freed[b], 1)
                dve.drain()
                V.scalar_tensor_tensor(out=gabs[:, :], in0=grow[:, layer, :], scalar=-1.0, in1=grow[:, layer, :],
                                       op0=ALU.mult, op1=ALU.max)
                V.tensor_scalar(gsgn[:, :], grow[:, layer, :], 0.0, 2.0, ALU.is_ge, ALU.mult)
                dve.drain()
                V.tensor_scalar(gabs[:, :], gabs[:, :], 0.25, None, ALU.max)
                V.tensor_scalar(gsgn[:, :], gsgn[:, :], -1.0, None, ALU.add)
                dve.drain()
                V.tensor_tensor(grow[:, layer, :], gabs[:, :], gsgn[:, :], ALU.mult).then_inc(s["gate_rows"], 1)
                dve.drain()

            def normed(k, h, src):
                four = slice(4 * h, 4 * h + 4)
                for t in range(4 * h, 4 * h + 4):
                    V.bn_stats(stat[:, t, :], src[:, t, :])
                dve.drain()
                for t in range(4 * h, 4 * h + 4):
                    V.bn_aggr(mv[:, t, :], stat[:, t, :])
                dve.drain()
                V.tensor_scalar(var[:, four], mv[:, four, 1], EPS, None, ALU.add).then_inc(s["var_done"], 1)
                dve.wait_ge(s["rstd_done"], k * NHALF + h + 1)
                for t in range(4 * h, 4 * h + 4):
                    V.tensor_scalar(hrow[:, t, :], src[:, t, :], mv[:, t, 0:1], rstd[:, t:t + 1],
                                    ALU.subtract, ALU.mult).then_inc(s["hrow_done"], 1)

            def h_low(k, h):
                for dt in range(ND):
                    n = (k * NHALF + h) * ND + dt
                    cols = slice(h * HALF, (h + 1) * HALF)
                    dve.wait_ge(s["hT_done"], n + 1)
                    V.tensor_tensor(hT[:, 1, dt, cols], hfull[:, n % 2, :], hT[:, 0, dt, cols].bitcast(F32),
                                    ALU.subtract).then_inc(s["h_lo_done"], 1)

            def split(dst, src, done=None):
                V.tensor_copy(dst[0], src)
                dve.drain()
                i = V.tensor_tensor(dst[1], src, dst[0].bitcast(F32), ALU.subtract)
                if done is not None:
                    i.then_inc(done, 1)

            def pick_first(bi):
                V.tensor_copy(modn[:, :, :].rearrange("p k t -> p (k t)"),
                              modT[:, 0, 0:2, :, :].rearrange("p k t b -> p (k t) b")[:, :, bass.ds(bi, 1)]
                              .rearrange("p n b -> p (n b)")).then_inc(s["mod_picked"], 1)

            dve.wait_ge(s["loaded_raw"], 16 * 3)
            split([in_w[:, a, :, :] for a in range(2)], wraw[:, :, 0:INNER], s["raw_used"])
            split([wr[:, a, :, :] for a in range(2)], wr_raw[:, :, :])
            dve.wait_ge(s["loaded_raw"], 16 * 4)
            split([wqkv[:, a, :, :, :].rearrange("p q g n -> p q (g n)") for a in range(2)], wraw[:, :, :])
            dve.drain()
            pick_first(0)
            dve.wait_ge(s["x_loaded"], 16)
            for h in range(NHALF):
                normed(0, h, x)
                h_low(0, h)
            part_ends(dve, "vector")

            bk = banks["batch"]

            def add_to_x(name, h, gate, bias=0):
                if bias:
                    dve.wait_ge(s["bias_added"], NHALF * (bias - 1) + h + 1)
                for t in range(4 * h, 4 * h + 4, 2):
                    b = bk.wait(dve, (name, t))
                    r = (t // 2) % 2
                    V.tensor_tensor(tmp[:, r, :, :], ps[:, b, :].rearrange("p (t n) -> p t n", t=2),
                                    gate.unsqueeze(1).broadcast_to([P, 2, D]), ALU.mult).then_inc(freed[b], 1)
                    dve.drain()
                    V.tensor_tensor(x[:, t:t + 2, :], x[:, t:t + 2, :], tmp[:, r, :, :], ALU.add)
                dve.drain()

            def rotate(g, tiles=range(NT)):
                for t in tiles:
                    b = bk.wait(dve, ("qkv", g, t))
                    r = t % 2
                    n = g * NT + t
                    if n >= 2:
                        dve.wait_ge(s["rot_done"], n - 1)
                    v = ps[:, b, 0:QK].rearrange("p (h e i) -> p h e i", e=2, i=HD // 2)
                    cs = [rope[:, t, q, :].unsqueeze(1).broadcast_to([P, GQ + 1, HD // 2]) for q in range(2)]
                    A4, B4 = rot_buf(r)
                    for e in range(2):
                        V.tensor_tensor(A4[:, :, e, :], v[:, :, e, :], cs[0], ALU.mult)
                    V.tensor_tensor(B4[:, :, 0, :], v[:, :, 1, :], cs[1], ALU.mult)
                    V.tensor_tensor(B4[:, :, 1, :], v[:, :, 0, :], cs[1], ALU.mult).then_inc(s["rot_a"], 1)

            def turn_head(u):
                g = u // GQ
                if u % GQ == 0:
                    for h in range(NHALF):
                        b = bk.wait(dve, ("k", g, h))
                        cols = slice(h * HALF, (h + 1) * HALF)
                        dve.wait_ge(s["k_done"], NHALF * g + h + 1)
                        V.tensor_tensor(khl[HD:P, g % 2, cols], ps[0:HD, b, :], khl[0:HD, g % 2, cols].bitcast(F32),
                                        ALU.subtract).then_inc(s["k_lo_done"], 1)
                for h in range(NHALF):
                    b = bk.wait(dve, ("q", u, h))
                    cols = slice(h * HALF, (h + 1) * HALF)
                    dve.wait_ge(s["q_done"], NHALF * u + h + 1)
                    V.tensor_tensor(q2[0:HD, u % QRING, cols], ps[0:HD, b, :], qhh[0:HD, u % QRING, cols].bitcast(F32),
                                    ALU.subtract).then_inc(s["q_lo_done"], 1)

            def row_maxima(u, i):
                n = (i + 1) * P
                b = bk.wait(dve, ("rows", u, i))
                v = (ps[:, b:b + 2, :].rearrange("p a n -> p (a n)") if n > HALF else ps[:, b, :])[:, 0:n]
                V.tensor_tensor_reduce(out=v, in0=v, in1=mrow[:, L - n:L], scale=1.0, scalar=-3e38, op0=ALU.add,
                                       op1=ALU.max, accum_out=mx[:, u % 2, i:i + 1]).then_inc(freed[b], 1)

            def negate(u):
                dve.drain()
                V.tensor_scalar(nm[:, u % 2, :], mx[:, u % 2, :], -1.0, None, ALU.mult).then_inc(s["nm_done"], 1)

            def normalise(u, c):
                b = bk.wait(dve, ("pv", u, c))
                v = ps[:, b, 0:4 * (HD + 1)].rearrange("p (i n) -> p i n", n=HD + 1)
                V.reciprocal(den[:, c, :], v[:, :, HD])
                dve.drain()
                if u >= 2 and u % 2 == 0:
                    dve.wait_ge(s["oT_done"], u)
                V.tensor_tensor(orow[:, 4 * c:4 * c + 4, (u % 2) * HD:(u % 2 + 1) * HD], v[:, :, 0:HD],
                                den[:, c, :].unsqueeze(2).broadcast_to([P, 4, HD]), ALU.mult)\
                    .then_inc(s["o_done"], 1)

            with dve.Fori(0, B) as bi:
                V.tensor_copy(modb[:, :, :, :].rearrange("p l k t -> p (l k t)"),
                              modT[:, :, :, :, :].rearrange("p l k t b -> p (l k t) b")[:, :, bass.ds(bi, 1)]
                              .rearrange("p n b -> p (n b)")).then_inc(s["mod_picked"], 1)
                for r in range(2):
                    V.memset(up[:, r, 0:2], 0.0)
                dve.drain()
                for n, e in enumerate(E_ORDER):
                    dt = e % ND
                    dst = {0: x0[:, dt, :], 1: x1[:, :], 2: vx[:, dt, :]}[e // ND]
                    dve.wait_ge(s["tap_done"], n + 1)
                    V.scalar_tensor_tensor(out=tap[:, n % 2, :], in0=up[:, n % 2, 1:L + 1], scalar=short_w[:, e, 1:2],
                                           in1=tap[:, n % 2, :], op0=ALU.mult, op1=ALU.add)
                    dve.drain()
                    V.scalar_tensor_tensor(out=dst, in0=up[:, n % 2, 0:L], scalar=short_w[:, e, 0:1],
                                           in1=tap[:, n % 2, :], op0=ALU.mult, op1=ALU.add)\
                        .then_inc(s["conv_done"], 1)
                    if e // ND == 1:
                        dve.drain()
                        V.tensor_tensor(vx[:, dt, :], vx[:, dt, :], x1[:, :], ALU.mult).then_inc(s["vx_done"], 1)
                        dve.drain()
                dve.drain()
                for n, (j, i) in enumerate(PAIRS):
                    b = bk.wait(dve, ("vf", j // 2))
                    if n >= 2 and PAIRS[n - 2] in POOL_PAIRS:
                        dve.wait_ge(s["y_pool"], POOL_PAIRS.index(PAIRS[n - 2]) + 1)
                    v = ps[:, b:b + 2 * ST, j % 2 * D:(j % 2 + 1) * D].rearrange("p (c f) n -> p c f n", c=2)
                    for k in range(2):
                        q = V.tensor_tensor(prod[:, n % 2, k, :, :, :], v,
                                            Kf[:, i - j, k, :, :].unsqueeze(1).broadcast_to([P, 2, ST, D]), ALU.mult)
                    pr = prod[:, n % 2]
                    if (j, i) in POOL_PAIRS:
                        q.then_inc(s["prod_done"], 1)
                        continue
                    if (j, i) == PAIRS[-1]:
                        q.then_inc(freed[b], 1)
                    dve.drain()
                    if j == 0:
                        V.tensor_tensor(Yf[:, i, 0, :, :], pr[:, 0, 0, :, :], pr[:, 1, 1, :, :], ALU.subtract)
                        V.tensor_tensor(Yf[:, i, 1, :, :], pr[:, 0, 1, :, :], pr[:, 1, 0, :, :], ALU.add)\
                            .then_inc(s["y_dve"], 1)
                    else:
                        before = [p for p in POOL_PAIRS if p[1] == i and PAIRS.index(p) < n]
                        dve.wait_ge(s["y_pool"], POOL_PAIRS.index(before[-1]) + 1)
                        for c, (k, w, op) in ((0, (0, 0, ALU.add)), (1, (0, 1, ALU.add)),
                                              (0, (1, 1, ALU.subtract)), (1, (1, 0, ALU.add))):
                            if k == 1 and c == 0:
                                dve.drain()
                            q = V.tensor_tensor(Yf[:, i, c, :, :], Yf[:, i, c, :, :], pr[:, k, w, :, :], op)
                        q.then_inc(s["y_dve"], 1)
                    dve.drain()
                for ip in range(NB // 2):
                    for dt in range(ND):
                        b = bk.wait(dve, ("y", ip, dt))
                        cols = slice(ip * HALF, (ip + 1) * HALF)
                        V.scalar_tensor_tensor(out=vx[:, dt, cols], in0=vx[:, dt, cols], scalar=filt_b[:, dt:dt + 1],
                                               in1=ps[:, b, :], op0=ALU.mult, op1=ALU.add).then_inc(freed[b], 1)
                        dve.drain()
                        V.tensor_tensor(x0[:, dt, cols], vx[:, dt, cols], x0[:, dt, cols], ALU.mult)\
                            .then_inc(s["yv_done"], 1)
                dve.wait_ge(s["gates_mixed"], 1)
                for h in range(NHALF):
                    add_to_x("out0", h, gates[:, 0, :], bias=1)
                    normed(LN_FFN, h, x)
                    if h == 0:
                        h_low(LN_FFN, h)
                for h in range(NHALF):
                    if h:
                        h_low(LN_FFN, h)
                    for n in range(NH1):
                        m = h * NH1 + n
                        cols = slice(h * HALF, (h + 1) * HALF)
                        dve.wait_ge(s["g_hi_done"], m + 1)
                        V.tensor_tensor(gT[:, 1, n, cols], gfull[:, m % 4, :], gT[:, 0, n, cols].bitcast(F32),
                                        ALU.subtract).then_inc(s["g_lo_done"], 1)
                for h in range(NHALF):
                    add_to_x("ffn2", h, escale[:, 0, :], bias=2)
                    normed(LN_ATT, h, x)
                    if h == 0:
                        h_low(LN_ATT, h)
                for h in range(NHALF):
                    if h:
                        h_low(LN_ATT, h)
                    rotate(0, range(4 * h, 4 * h + 4))
                turn_head(0)
                for i in range(NT):
                    row_maxima(0, i)
                negate(0)
                for u in range(HEADS):
                    w = u + 1
                    if w < HEADS:
                        turn_head(w)
                    if u % GQ == 2 and u // GQ + 1 < KV:
                        rotate(u // GQ + 1)
                    normalise(u, 0)
                    if w < HEADS:
                        for i in range(NT):
                            row_maxima(w, i)
                        if w >= 2:
                            dve.wait_ge(s["nmr_done"], w - 1)
                        negate(w)
                    normalise(u, 1)
                add_to_x("out1", 0, gates[:, 2, :])
                normed(LN_MOE, 0, x)
                add_to_x("out1", 1, gates[:, 2, :])
                h_low(LN_MOE, 0)
                b = bk.wait(dve, ("router",))
                V.tensor_tensor(score[:, :], ps[0:1, b, 0:EXPERTS], br[:, :], ALU.add).then_inc(freed[b], 1)
                dve.drain()
                V.max(top[:, :], score[:, :])
                dve.drain()
                V.max_index(topi[:, :], top[:, :], score[:, :]).then_inc(s["top_done"], 1)
                normed(LN_MOE, 1, x)
                h_low(LN_MOE, 1)
                for k in range(TOPK):
                    dve.wait_ge(s[f"expert_loaded{k}"], 16 * 4)
                    split([w1s[:, k, a, :, :] for a in range(2)], w1e[:, k, :, :], s["w1_split"])
                pick_first((bi + 1) % B)
                dve.wait_ge(s["x_next_loaded"], 16)
                dve.wait_ge(s["hT_done"], (LN_MOE + 1) * NHALF * ND)
                for h in range(NHALF):
                    normed(LN_NEXT, h, xn)
                    h_low(LN_NEXT, h)
                for h in range(NHALF):
                    add_to_x("moe2", h, escale[:, 1, :], bias=3)
                dve.drain().then_inc(s["x_done"], 1)
                part_ends(dve, "vector")

        @block.gpsimd
        def _(pool):
            G = nc.gpsimd
            G.memset(ones[:, :], 1.0)
            G.memset(ident[:, :], 0.0)
            G.memset(mrow[:, :], 0.0)
            G.memset(neghalf[:, :], -0.5)
            pool.drain()
            G.affine_select(out=ident[:, :], in_=ident[:, :], compare_op=ALU.not_equal, fill=1.0, base=0,
                            pattern=[[-1, P]], channel_multiplier=1)
            G.affine_select(out=mrow[:, L - P:L], in_=mrow[:, L - P:L], compare_op=ALU.is_ge, fill=MASKED, base=0,
                            pattern=[[-1, P]], channel_multiplier=1)
            pool.drain().then_inc(s["const_made"], 1)

            def normed(k, h):
                four = slice(4 * h, 4 * h + 4)
                pool.wait_ge(s["var_done"], k * NHALF + h + 1)
                G.tensor_tensor(rstd[:, four], var[:, four], neghalf[:, four], ALU.pow).then_inc(s["rstd_done"], 1)

            for h in range(NHALF):
                normed(0, h)
            part_ends(pool, "gpsimd")

            def add_bias(h, n):
                for t in range(4 * h, 4 * h + 4, 2):
                    q = G.tensor_tensor(x[:, t:t + 2, :], x[:, t:t + 2, :],
                                        terms[:, n, :].unsqueeze(1).broadcast_to([P, 2, D]), ALU.add)
                q.then_inc(s["bias_added"], 1)

            def normed_then_bias(k, h, n):
                normed(k, h)
                pool.wait_ge(s["hrow_done"], k * NT + 4 * h + 4)
                add_bias(h, n)

            def mask(u, c, j):
                pool.wait_ge(s["exp_done"], 12 * u + 4 * c + j + 1)
                v = pT[:, (12 * u + 4 * c + j) % PRING, 0:P]
                G.affine_select(out=v, in_=v, compare_op=ALU.is_ge, fill=0.0, base=0, pattern=[[1, P]],
                                channel_multiplier=-1).then_inc(s["masked_done"], 1)

            def rotate(g):
                for t in range(NT):
                    pool.wait_ge(s["rot_a"], g * NT + t + 1)
                    if g and t == 0:
                        pool.wait_ge(s["q_done"], NHALF * GQ * g)
                    A4, B4 = rot_buf(t % 2)
                    R4 = rotated(t).rearrange("p (h e i) -> p h e i", e=2, i=HD // 2)
                    G.tensor_tensor(R4[:, :, 0, :], A4[:, :, 0, :], B4[:, :, 0, :], ALU.subtract)
                    G.tensor_tensor(R4[:, :, 1, :], A4[:, :, 1, :], B4[:, :, 1, :], ALU.add).then_inc(s["rot_done"], 1)

            with pool.Fori(0, B):
                pool.wait_ge(s["gates_loaded"], 16)
                G.tensor_tensor(terms[:, 0, :], rows[:, 0, :], gates[:, 0, :], ALU.mult)
                G.tensor_tensor(terms[:, 1, :], rows[:, 1, :], gates[:, 1, :], ALU.mult)
                G.tensor_tensor(escale[:, 0, :], alpha2[:, :], gates[:, 1, :], ALU.mult)
                G.tensor_scalar(escale[:, 1, :], gates[:, 3, :], 1.0 / TOPK, 0.0, ALU.mult, ALU.add)
                pool.drain().then_inc(s["gates_mixed"], 1)
                pool.wait_ge(s["x_loaded"], 16)
                for h in range(NHALF):
                    add_bias(h, 0)
                for n, (j, i) in enumerate(POOL_PAIRS):
                    pool.wait_ge(s["prod_done"], n + 1)
                    if n < 3:
                        pool.wait_ge(s["y_dve"], DVE_PAIRS.index((0, i)) + 1)
                    pr = prod[:, PAIRS.index((j, i)) % 2]
                    for c, (k, w, op) in ((0, (0, 0, ALU.add)), (1, (0, 1, ALU.add)),
                                          (0, (1, 1, ALU.subtract)), (1, (1, 0, ALU.add))):
                        if k == 1 and c == 0:
                            pool.drain()
                        q = G.tensor_tensor(Yf[:, i, c, :, :], Yf[:, i, c, :, :], pr[:, k, w, :, :], op)
                    q.then_inc(s["y_pool"], 1)
                    pool.drain()
                for h in range(NHALF):
                    normed_then_bias(LN_FFN, h, 1)
                for h in range(NHALF):
                    normed(LN_ATT, h)
                G.memset(v1[:, :, :, HD:HD + 1], 1.0)
                pool.drain()
                G.memset(k2[HD:HD + 1, :, :].bitcast(F32), 1.0)
                pool.drain()
                rotate(0)
                for u in range(HEADS):
                    for j in range(4):
                        mask(u, 0, j)
                    if u % GQ == 2 and u // GQ + 1 < KV:
                        rotate(u // GQ + 1)
                    for j in range(4, NT):
                        mask(u, 1, j)
                for h in range(NHALF):
                    normed(LN_MOE, h)
                for h in range(NHALF):
                    normed(LN_NEXT, h)
                for k in range(TOPK):
                    pool.wait_ge(s[f"expert_loaded{k}"], 16 * 4)
                G.tensor_tensor(b2e[:, 0, :], b2e[:, 0, :], b2e[:, 1, :], ALU.add)
                pool.drain()
                G.tensor_tensor(terms[:, 2, :], b2e[:, 0, :], escale[:, 1, :], ALU.mult)
                pool.drain()
                pool.wait_ge(s["hrow_done"], LN_MOE * NT + NT)
                for h in range(NHALF):
                    add_bias(h, 2)
                part_ends(pool, "gpsimd")

        @block.sync
        def _(sp):
            dma = nc.sync.dma_start
            for dst, src in ((zT[:, :], d["zT"]), (fw1[:, :], d["L0_attn_mlp_w1"]), (fw23[:, 0, :], d["L0_attn_mlp_w2"]),
                             (fw23[:, 1, :], d["L0_attn_mlp_w3"]), (fwo[:, :], d["L0_attn_mlp_wo"]),
                             (fb[:, 0:1], d["L0_attn_mlp_b1"]), (fb[:, 1:2], d["L0_attn_mlp_b2"]),
                             (fb[:, 2:3], d["L0_attn_mlp_b3"]), (fb[:, 3:4], d["L0_attn_freq"])):
                dma(dst, src, allow_slow_non_contiguous=True).then_inc(s["loaded_filter"], 16)
            dma(cT[:, :, :, :], d["cT"], allow_slow_non_contiguous=True).then_inc(s["loaded_c"], 16)
            loads = [(w1rows[:, :, :], d["L0_ffn_w1"]), (x[:, :, :].rearrange("p t n -> p (t n)"), d["w1T"].rearrange("p q n -> p (q n)")), (w2T[:, :, :], d["w2T"]),
                     (decay[:, :, :], d["decay"]), (fwd[:, :, :], d["fwd"][:, 0]), (fwd_old[:, :, :], d["fwd"][:, 1]),
                     (inv[:, :, :], d["inv"]), (out_w[:, :, :], d["out_w"]),
                     (wo[:, :, :], d["wo"]), (rope[:, :, :, :], d["rope"]),
                     (wr_raw[:, :, :], d["wr"]), (br[:, :], d["L1_ffn_br"]), (in_b[:, :], d["in_b"]),
                     (short_w[:, :, :], d["short_w"]), (short_b[:, :], d["short_b"]), (filt_b[:, :], d["filt_b"]),
                     (ffn_b1[:, :], d["ffn_b1"]), (rows[:, 0, :], d["L0_attn_out_b"].partition_broadcast(P)),
                     (rows[:, 1, :], d["L0_ffn_b2"].partition_broadcast(P))]
            assert len(loads) == NLOADED
            for dst, src in loads:
                dma(dst, src, allow_slow_non_contiguous=True).then_inc(s["loaded"], 16)
            dma(wraw[:, :, :], d["wmod0"]).then_inc(s["loaded_raw"], 16)
            sp.wait_ge(s["gate_rows"], 1)
            dma(wraw[:, :, :], d["wmod1"]).then_inc(s["loaded_raw"], 16)
            sp.wait_ge(s["sgn_done"], 1)
            dma(x[:, :, :], d["x"][0].rearrange("(t p) n -> p t n", p=P)).then_inc(s["x_loaded"], 16)
            sp.wait_ge(s["gate_rows"], 2)
            dma(wraw[:, :, 0:INNER], d["in_w"]).then_inc(s["loaded_raw"], 16)
            sp.wait_ge(s["raw_used"], 1)
            dma(wraw[:, :, :], d["wqkv"].rearrange("p q g n -> p q (g n)")).then_inc(s["loaded_raw"], 16)
            dma(gate_scratch, grow[:, :, :].rearrange("b l n -> b (l n)")).then_inc(s["gate_stored"], 16)
            sp.wait_ge(s["kf_done"], 1)
            dma(kf_scratch, Kf[:, :, :, :, :].rearrange("p m c f n -> p (m c f n)")).then_inc(s["gate_stored"], 16)
            flat = {n: t for n, t in (("in_w", in_w[:, :, :, :].rearrange("p a q n -> p (a q n)")),
                                      ("sgn1", sgn1[:, :, :].rearrange("p q n -> p (q n)")),
                                      ("sgn2", sgn2[:, :, :].rearrange("p q n -> p (q n)")))}
            sp.wait_ge(s["sgn_done"], 2)
            for n in flat:
                dma(scratch[n], flat[n].bitcast(F32)).then_inc(s["gate_stored"], 16)
            sp.wait_ge(s["gate_stored"], 16 * 5)

            def clear():
                sp.wait_ge(bar, 4)
                sp.sem_clear(range(nums[0], nums[-1] + 1))
                sp.sem_clear(bar)
                for e in go:
                    sp.sem_inc(go[e], 1)

            clear()
            with sp.Fori(0, B) as bi:
                dma(x[:, :, :], d["x"][bass.ds(bi, 1), :, :].rearrange("a (t p) n -> p (a t) n", p=P))\
                    .then_inc(s["x_loaded"], 16)
                dma(gates[:, :, :].rearrange("p k n -> p (k n)"),
                    gate_scratch[bass.ds(bi, 1), :].broadcast_to([P, 4 * D])).then_inc(s["gates_loaded"], 16)
                for u in range(HEADS):
                    sp.wait_ge(s["nmr_done"], u + 1)
                    if u >= QRING:
                        banks["batch"].wait(sp, ("pv", u - QRING, 1))
                    dma(q2[HD:HD + 1, u % QRING, :].bitcast(F32), nmr[:, u % 2, :].bitcast(F32)).then_inc(m_loaded(u)[0], 16)
                sp.wait_ge(s["top_done"], 1)
                for k in range(TOPK):
                    e = nc.sync.value_load(topi[0:1, k:k + 1], min_val=0, max_val=EXPERTS - 1)
                    one = bass.ds(e, 1)
                    for dst, src in ((w1e[:, k, :, :], d["W1"][one].rearrange("e p q n -> p (e q) n")),
                                     (w2e[:, k, :, :], d["W2"][one].rearrange("e p q n -> p (e q) n")),
                                     (b1e[:, k, :], d["b1"][one].rearrange("e p q -> p (e q)")),
                                     (b2e[:, k, :], d["b2"][one, :].broadcast_to([P, D]))):
                        dma(dst, src, allow_slow_non_contiguous=True).then_inc(s[f"expert_loaded{k}"], 16)
                dma(xn[:, :, :], d["x"][bass.ds((bi + 1) % B, 1), :, :].rearrange("a (t p) n -> p (a t) n", p=P))\
                    .then_inc(s["x_next_loaded"], 16)
                for dst, src in ([(flat[n].bitcast(F32), scratch[n]) for n in flat]
                                 + [(Kf[:, :, :, :, :].rearrange("p m c f n -> p (m c f n)"), kf_scratch),
                                    (out_w[:, :, :], d["out_w"]), (fwd[:, :, :], d["fwd"][:, 0]),
                                    (inv[:, :, :], d["inv"])]):
                    dma(dst, src).then_inc(s["l0_loaded"], 16)
                sp.wait_ge(s["l0_loaded"], 16 * 7)
                sp.wait_ge(s["x_done"], 1)
                dma(out[bass.ds(bi, 1), :, :].rearrange("a (t p) n -> p (a t) n", p=P), x[:, :, :])\
                    .then_inc(s["stored"], 16)
                sp.wait_ge(s["stored"], 16)
                clear()


INPUTS = ["L0_attn_mlp_w1", "L0_attn_mlp_w2", "L0_attn_mlp_w3", "L0_attn_mlp_wo"]


def layouts(v):
    g = {n: np.ascontiguousarray(v[n]) for n in v}
    tiles = lambda a, n: np.ascontiguousarray(a.reshape(n, P, -1).transpose(1, 0, 2))
    cols = lambda a: np.ascontiguousarray(a.reshape(-1, P).T)
    o = {"x": g["L0_attn_u"]}
    for n in INPUTS:
        o[n] = g[n]
    for n in ("L0_attn_mlp_b1", "L0_attn_mlp_b2", "L0_attn_mlp_b3", "L0_attn_freq"):
        o[n] = g[n].reshape(FILT, 1)
    o["L0_ffn_w1"] = tiles(g["L0_ffn_w1"], NH1)
    o["w1T"] = tiles(np.ascontiguousarray(g["L0_ffn_w1"].T), ND)
    o["w2T"] = tiles(np.ascontiguousarray(g["L0_ffn_w2"].T), NH1)
    o["in_w"] = tiles(g["L0_attn_in_w"], ND)
    o["out_w"] = tiles(g["L0_attn_out_w"], ND)
    o["wo"] = tiles(g["L1_attn_Wo"], HEADS * HD // P)
    o["wr"] = tiles(g["L1_ffn_Wr"], ND)
    o["L1_ffn_br"] = g["L1_ffn_br"].reshape(1, EXPERTS)
    o["in_b"] = cols(g["L0_attn_in_b"])
    o["short_w"] = tiles(g["L0_attn_short_w"], INNER // P)
    o["short_b"] = cols(g["L0_attn_short_b"])
    o["filt_b"] = cols(g["L0_attn_filt_bias"])
    o["ffn_b1"] = cols(g["L0_ffn_b1"])
    o["L0_attn_out_b"] = g["L0_attn_out_b"]
    o["L0_ffn_b2"] = g["L0_ffn_b2"]
    halves = lambda w, n: w.reshape(D, n, HD // 2, 2).transpose(0, 1, 3, 2).reshape(D, n, HD)
    q = halves(g["L1_attn_Wq"], HEADS).reshape(D, KV, GQ, HD)
    k = halves(g["L1_attn_Wk"], KV)[:, :, None]
    val = g["L1_attn_Wv"].reshape(D, KV, 1, HD)
    o["wqkv"] = np.ascontiguousarray(np.concatenate([q, k, val], axis=2).reshape(ND, P, KV, GW).transpose(1, 0, 2, 3))
    o["W1"] = np.ascontiguousarray(g["L1_ffn_W1"].reshape(EXPERTS, ND, P, D).transpose(0, 2, 1, 3))
    o["W2"] = np.ascontiguousarray(g["L1_ffn_W2"].reshape(EXPERTS, ND, P, D).transpose(0, 2, 1, 3))
    o["b1"] = np.ascontiguousarray(g["L1_ffn_b1"].reshape(EXPERTS, ND, P).transpose(0, 2, 1))
    o["b2"] = g["L1_ffn_b2"]
    o["cT"] = np.ascontiguousarray(np.stack([g["L0_c"].T, g["L1_c"].T]).reshape(2, ND, P, B).transpose(2, 0, 1, 3))
    o["wmod0"] = tiles(g["L0_wmod"], ND)
    o["wmod1"] = tiles(g["L1_wmod"], ND)
    return o


def kernel(**inputs):
    import concourse.bacc as bacc
    from concourse.bass_utils import run_bass_kernel_spmd

    arrays = layouts({n: np.asarray(a) for n, a in inputs.items()})
    arrays.update(shape_constants())
    nc = bacc.Bacc("TRN2", target_bir_lowering=False, num_devices=1)
    d = {n: nc.dram_tensor(f"in_{n}", a.shape, mybir.dt.from_np(a.dtype), kind="ExternalInput").ap()
         for n, a in arrays.items()}
    out = nc.dram_tensor("out", (B, L, D), F32, kind="ExternalOutput").ap()
    gate_scratch = nc.dram_tensor("gate_scratch", (B, 4 * D), F32, kind="Internal").ap()
    kf_scratch = nc.dram_tensor("kf_scratch", (P, NB * 2 * ST * D), F32, kind="Internal").ap()
    scratch = {n: nc.dram_tensor(f"{n}_scratch", (P, w), F32, kind="Internal").ap()
               for n, w in (("in_w", 2 * ND * INNER), ("sgn1", ND * HID), ("sgn2", NH1 * D))}
    adaln_hyena_binffn_gqa_moe(nc, d, out, gate_scratch, kf_scratch, scratch)
    r = run_bass_kernel_spmd(nc, [{f"in_{n}": a for n, a in arrays.items()}], core_ids=[0])
    return r.results[0]["out"]
```

```python
from contextlib import ExitStack

import numpy as np

import concourse.bass as bass
from concourse import mybir

F32 = mybir.dt.float32
F32R = mybir.dt.float32r
U32 = mybir.dt.uint32
ALU = mybir.AluOpType
ACT = mybir.ActivationFunctionType
AX = mybir.AxisListType.X

P = 128
B, L, D = 4, 1024, 256
NT = L // P
ND = D // P
HALF = 512
NHALF = L // HALF
EPS = 1e-5

S = 256
NB = L // S
ST = S // P
FILT = 64
EMB = 3
INNER = 3 * D

FFN_TURN = 5
FFN_LOW = 4
HID = 1024
NH1 = HID // P

HEADS, KV, HD = 16, 4, 64
GQ = HEADS // KV
GW = (GQ + 2) * HD
QK = (GQ + 1) * HD
SCALE = HD ** -0.5
MASKED = -1e30
QRING = 2
PRING = 8

EXPERTS, TOPK = 8, 2

E_ORDER = (4, 2, 5, 3, 0, 1)
PAIRS = ((0, 0), (0, 1), (1, 1), (0, 2), (0, 3), (1, 2), (1, 3), (2, 2), (2, 3), (3, 3))
POOL_PAIRS = ((1, 1), (1, 2), (2, 2))
DVE_PAIRS = tuple(p for p in PAIRS if p not in POOL_PAIRS)
LN_FFN, LN_ATT, LN_MOE, LN_NEXT = range(4)
NLOADED = 16

PI_DOWN = 3.1415925
TWO_PI_HI = 6.28125
TWO_PI_LO = float(2 * np.pi - 6.28125)
ROUND = float(1.5 * 2 ** 23)


def shape_constants():
    n = np.arange(2 * S)[:, None]
    f = np.arange(S)[None, :] + 0.5
    ang = np.pi * ((n * (2 * f)) % (4 * S)) / (2 * S) * 1.0
    fwd = np.concatenate([np.cos(ang), np.sin(ang)], axis=1)
    fwd = fwd.reshape(2, ST, P, 2 * S).transpose(2, 0, 1, 3)
    inv = np.concatenate([np.cos(ang[S:]), np.sin(ang[S:])], axis=1).T / S
    inv = inv.reshape(2 * ST, P, S).transpose(1, 0, 2)
    t = np.linspace(0.0, 1.0, L, dtype=np.float32)[:, None]
    tr = np.linspace(0.0, L - 1.0, L, dtype=np.float32)[:, None]
    w = (2.0 * np.pi * tr / L).astype(np.float32)
    fr = np.float32(0.0001)
    z = np.concatenate([t, np.cos(fr * w), -np.sin(fr * w)], axis=-1)
    deltas = np.linspace(np.log(0.01) / 1.5, np.log(0.01) / 0.3, D, dtype=np.float32)[None, :]
    decay = np.exp(-t * np.abs(deltas)).reshape(NT, P, D).transpose(1, 0, 2)
    inv_freq = np.float32(1.0) / np.float32(10000.0) ** (np.arange(0, HD, 2, dtype=np.float32) / np.float32(HD))
    freqs = np.arange(L, dtype=np.float32)[:, None] * inv_freq[None, :]
    emb = np.concatenate([freqs, freqs], axis=-1)
    cos, sin = np.cos(emb)[:, 0::2], np.sin(emb)[:, 0::2]
    rope = np.stack([cos, sin], axis=1).reshape(NT, P, 2, HD // 2).transpose(1, 0, 2, 3)
    c = lambda a: np.ascontiguousarray(a, dtype=np.float32)
    return {"fwd": c(fwd), "inv": c(inv), "zT": c(z.T), "decay": c(decay), "rope": c(rope)}


def adaln_hyena_binffn_gqa_moe(nc, d, out, gate_scratch, kf_scratch, scratch):
    es = ExitStack()
    with es:
        def sb(name, shape, dt=F32, stack=es):
            return stack.enter_context(nc.sbuf_tensor(name, shape, dt))

        def sem(name):
            return es.enter_context(nc.semaphore(name))

        x = sb("x", [P, NT, D])
        ident = sb("ident", [P, P])
        wqkv = sb("wqkv", [P, 2, ND, KV, GW], F32R)
        wo = sb("wo", [P, HEADS * HD // P, D])
        rope = sb("rope", [P, NT, 2, HD // 2])
        mrow = sb("mrow", [P, L])
        wr = sb("wr", [P, 2, ND, EXPERTS], F32R)
        br = sb("br", [1, EXPERTS])
        in_b = sb("in_b", [P, INNER // P])
        short_w = sb("short_w", [P, INNER // P, 3])
        short_b = sb("short_b", [P, INNER // P])
        filt_b = sb("filt_b", [P, ND])
        ffn_b1 = sb("ffn_b1", [P, NH1])
        alpha1 = sb("alpha1", [P, NH1])
        rows = sb("rows", [P, 2, D])
        alpha2 = sb("alpha2", [P, D])
        modT = sb("modT", [P, 2, 4, ND, B])
        modb = sb("modb", [P, 2, 4, ND])
        modn = sb("modn", [P, 2, ND])
        gates = sb("gates", [P, 4, D])
        terms = sb("terms", [P, 3, D])
        escale = sb("escale", [P, 2, D])
        neghalf = sb("neghalf", [P, NT])
        stat = sb("stat", [P, NT, 6])
        mv = sb("mv", [P, NT, 2])
        var = sb("var", [P, NT])
        rstd = sb("rstd", [P, NT])
        hT = sb("hT", [P, 2, ND, L], F32R)
        hfull = sb("hfull", [P, 2, HALF])
        hrow = sb("hrow", [P, NT, D])
        tmp = sb("tmp", [P, 2, 2, D])

        with ExitStack() as a:
            in_w = sb("in_w", [P, 2, ND, INNER], F32R, a)
            sgn1 = sb("sgn1", [P, ND, HID], F32R, a)
            sgn2 = sb("sgn2", [P, NH1, D], F32R, a)
            out_w = sb("out_w", [P, ND, D], F32, a)
            fwd = sb("fwd", [P, ST, 2 * S], F32, a)
            inv = sb("inv", [P, 2 * ST, S], F32, a)
            with ExitStack() as ak:
                Kf = sb("Kf", [P, NB, 2, ST, D], F32, ak)
                with ExitStack() as a0:
                    fwd_old = sb("fwd_old", [P, ST, 2 * S], F32, a0)
                    kern = sb("kern", [P, NT, D], F32, a0)
                    decay = sb("decay", [P, NT, D], F32, a0)
                    w2T = sb("w2T", [P, NH1, D], F32, a0)
                    fw1 = sb("fw1", [EMB, FILT], F32, a0)
                    fw23 = sb("fw23", [FILT, 2, FILT], F32, a0)
                    fwo = sb("fwo", [FILT, D], F32, a0)
                    fb = sb("fb", [FILT, 4], F32, a0)
                    ang = sb("ang", [FILT, L], F32, a0)
                    sine = sb("sine", [FILT, L], F32, a0)
                    wraw = sb("wraw", [P, ND, 6 * D], F32, a0)
                    wr_raw = sb("wr_raw", [P, ND, EXPERTS], F32, a0)
                    cT = sb("cT", [P, 2, ND, B], F32, a0)
                    grow = sb("grow", [B, 2, 2 * D], F32, a0)
                    ones = sb("ones", [P, P], F32, a0)
                    with ExitStack() as a01:
                        zT = sb("zT", [EMB, L], F32, a01)
                    with ExitStack() as a02:
                        gabs = sb("gabs", [B, 2 * D], F32, a02)
                        gsgn = sb("gsgn", [B, 2 * D], F32, a02)
                with ExitStack() as a1:
                    x1 = sb("x1", [P, L], F32, a1)
                    x0 = sb("x0", [P, ND, L], F32, a1)
                    vx = sb("vx", [P, ND, L], F32, a1)
                    vrow = sb("vrow", [P, NT, D], F32, a1)
                    Yf = sb("Yf", [P, NB, 2, ST, D], F32, a1)
                    with ExitStack() as a11:
                        up = sb("up", [P, 2, L + 2], F32, a11)
                        tap = sb("tap", [P, 2, L], F32, a11)
                    with ExitStack() as a12:
                        prod = sb("prod", [P, 2, 2, 2, ST, D], F32, a12)
            turn, w1rows = sine, hrow
            with ExitStack() as a2:
                gfull = sb("gfull", [P, 4, HALF], F32, a2)
                gT = sb("gT", [P, 2, NH1, L], F32R, a2)
        with ExitStack() as a:
            with ExitStack() as a3:
                oT = sb("oT", [P, HEADS * HD // P, L], F32, a3)
                qhh = sb("qhh", [P, QRING, L], F32R, a3)
                q2 = sb("q2", [HD + 1, QRING, L], F32R, a3)
                khl = sb("khl", [P, 2, L], F32R, a3)
                k2 = sb("k2", [HD + 1, 2, L], F32R, a3)
                v1 = sb("v1", [P, 2, NT, HD + 1], F32, a3)
                pT = sb("pT", [P, PRING, HALF], F32, a3)
                rprod = sb("rprod", [P, 4, QK], F32, a3)
                rot = sb("rot", [P, NT, QK], F32, a3)
                orow = sb("orow", [P, NT, P], F32, a3)
                mx = sb("mx", [P, 2, NT], F32, a3)
                nm = sb("nm", [P, 2, NT], F32, a3)
                nmr = sb("nmr", [NT, 2, P], F32R, a3)
                den = sb("den", [P, 2, 4], F32, a3)
        with ExitStack() as a:
            skip = sb("skip", [P, 58 * 256], F32, a)
            assert skip.shape[1] * 4 >= 4 * (2 * ND * INNER + ND * HID + NH1 * D + ND * D + ST * 2 * S + 2 * ST * S
                                             + NB * 2 * ST * D)
            w1e = sb("w1e", [P, TOPK, ND, D], F32, a)
            w1s = sb("w1s", [P, TOPK, 2, ND, D], F32R, a)
            w2e = sb("w2e", [P, TOPK, ND, D], F32, a)
            b1e = sb("b1e", [P, TOPK, ND], F32, a)
            b2e = sb("b2e", [P, TOPK, D], F32, a)
            xn = sb("xn", [P, NT, D], F32, a)
            geT = sb("geT", [P, TOPK * ND, L], F32, a)
            score = sb("score", [1, EXPERTS], F32, a)
            top = sb("top", [1, 8], F32, a)
            topi = sb("topi", [1, 8], U32, a)

        def rot_buf(r):
            return [rprod[:, 2 * r + k, :].rearrange("p (h e i) -> p h e i", e=2, i=HD // 2)
                    for k in range(2)]

        def rotated(t):
            return rot[:, t, :]

        ps = es.enter_context(nc.psum_tensor("ps", [P, 8, HALF], F32))

        bar = sem("bar")
        go = {e: sem("go_" + e) for e in ("tensor", "vector", "scalar", "gpsimd")}
        weights_stored = sem("weights_stored")
        stored = sem("stored")
        names = ["loaded", "loaded_filter", "loaded_c", "loaded_windows", "const_made", "filter_angle",
                 "filter_sine", "kern_done", "kf_done", "abs_done", "silu_done", "gate_rows", "gate_stored",
                 "mod_picked", "x_loaded", "x_next_loaded", "gates_loaded", "gates_mixed", "var_done",
                 "rstd_done", "hrow_done", "hT_done", "bias_added", "tap_done", "conv_done", "vx_done",
                 "vrow_done", "prod_done", "y_dve", "y_pool", "yv_done", "gelu_done", "g_lo_done", "h_lo_done",
                 "w1_split", "sgn_done", "raw_used", "loaded_raw", "l0_loaded", "rot_a", "rot_done", "v_done",
                 "q_done", "q_lo_done", "k_done", "k_lo_done", "nm_done", "nmr_done", "m_loaded0", "m_loaded1",
                 "exp_done", "masked_done", "o_done", "oT_done", "top_done", "w1_loaded0", "w1_loaded1",
                 "expert_loaded0", "expert_loaded1", "egelu_done", "x_done"]
        s = {}
        for n in names:
            s[n] = sem(n)
        ready = [sem(f"ready{i}") for i in range(8)]
        freed = [sem(f"freed{i}") for i in range(8)]
        cleared = list(s.values()) + ready + freed
        nums = [q.num for q in cleared]
        assert nums == list(range(nums[0], nums[0] + len(nums)))

        def m_loaded(u):
            return s[f"m_loaded{u % QRING}"], 16 * (u // QRING + 1)

        class Banks:
            def __init__(self):
                self.reset()

            def reset(self):
                self.at, self.uses, self.frees, self.owner, self.chunk = 0, [0] * 8, [0] * 8, [None] * 8, {}

            def take(self, pe, key, n=1, until=None):
                while self.at % n:
                    self.at += 1
                b = self.at % 8
                for q in range(b, b + n):
                    if self.owner[q] is not None:
                        pe.wait_ge(*self.owner[q])
                self.uses[b] += 1
                if until is None:
                    self.frees[b] += 1
                    until = (freed[b], self.frees[b])
                for q in range(b, b + n):
                    self.owner[q] = until
                self.at += n
                self.chunk[key] = (b, self.uses[b])
                return b

            def wait(self, eng, key):
                b, use = self.chunk[key]
                eng.wait_ge(ready[b], use)
                return b

        banks = {"setup": Banks(), "batch": Banks()}

        def part_ends(eng, name):
            eng.drain().then_inc(bar, 1)
            eng.wait_ge(go[name], 1)
            eng.sem_clear(go[name])

        block = es.enter_context(nc.Block())

        @block.tensor
        def _(pe):
            mm, tr = nc.tensor.matmul, nc.tensor.transpose

            def split_mm(o, lhs, rhs, tiles):
                pairs = [(a, c, q) for q in range(tiles) for a, c in ((0, 0), (0, 1), (1, 0))]
                for n, (a, c, q) in enumerate(pairs):
                    i = mm(o, lhs(a, q), rhs(c, q), start=n == 0, stop=n == len(pairs) - 1)
                return i

            def sign_mm(o, lhs, rhs, pairs):
                for n, (a, q) in enumerate(pairs):
                    i = mm(o, lhs(a, q), rhs(a, q), start=n == 0, stop=n == len(pairs) - 1)
                return i
            def modulation(layer):
                pe.wait_ge(s["silu_done"], 1)
                pe.wait_ge(s["loaded_raw"], 16 * (layer + 1))
                b = bk.take(pe, ("modT", layer))
                for n, kind in enumerate((0, 1, 3, 4)):
                    for dt in range(ND):
                        o = (n * ND + dt) * B
                        for q in range(ND):
                            i = mm(ps[:, b, o:o + B], wraw[:, q, kind * D + dt * P:kind * D + (dt + 1) * P],
                                   cT[:, layer, q, :], start=q == 0, stop=q == ND - 1)
                i.then_inc(ready[b], 1)
                b = bk.take(pe, ("gate", layer))
                for n, kind in enumerate((2, 5)):
                    for q in range(ND):
                        i = mm(ps[0:B, b, n * D:(n + 1) * D], cT[:, layer, q, :],
                               wraw[:, q, kind * D:(kind + 1) * D], start=q == 0, stop=q == ND - 1)
                i.then_inc(ready[b], 1)

            bk = banks["setup"]
            pe.wait_ge(s["loaded_filter"], 16 * 9)
            for layer in range(3):
                if layer:
                    pe.wait_ge(s["filter_sine"], layer)
                for h in range(NHALF):
                    b = bk.take(pe, ("filter", layer, h))
                    w = fw1[:, :] if layer == 0 else fw23[:, layer - 1, :]
                    src = zT if layer == 0 else sine
                    mm(ps[0:FILT, b, :], w, src[:, h * HALF:(h + 1) * HALF], start=True, stop=True)\
                        .then_inc(ready[b], 1)
                if layer != 1:
                    modulation(layer // 2)
            pe.wait_ge(s["filter_sine"], 3)
            for t in range(0, NT, 2):
                b = bk.take(pe, ("kern", t), until=(s["kern_done"], t // 2 + 1))
                for u in range(2):
                    i = mm(ps[:, b, u * D:(u + 1) * D], sine[:, (t + u) * P:(t + u + 1) * P], fwo[:, :],
                           start=True, stop=True)
                i.then_inc(ready[b], 1)
            pe.wait_ge(s["loaded_windows"], 16 * 3)
            pe.wait_ge(s["kern_done"], NT // 2)
            for m in range(NB):
                for c in range(2):
                    b = bk.take(pe, ("kf", m, c))
                    for ft in range(ST):
                        col = (c * ST + ft) * P
                        terms_ = [(fwd_old, ST * m + q, q) for q in range(ST)]
                        if m:
                            terms_ += [(fwd, ST * (m - 1) + q, q) for q in range(ST)]
                        for n, (tab, t, q) in enumerate(terms_):
                            i = mm(ps[:, b, ft * D:(ft + 1) * D], tab[:, q, col:col + P], kern[:, t, :],
                                   start=n == 0, stop=n == len(terms_) - 1)
                    i.then_inc(ready[b], 1)
            pe.wait_ge(s["const_made"], 1)
            pe.wait_ge(s["abs_done"], 1)
            b = bk.take(pe, ("alpha2",))
            for q in range(NH1):
                i = mm(ps[:, b, 0:D], ones[:, :], w2T[:, q, :], start=q == 0, stop=q == NH1 - 1)
            i.then_inc(ready[b], 1)
            def normed(k, h):
                for dt in range(ND):
                    b = bk.take(pe, ("ln", k, h, dt), until=(s["hT_done"], (k * NHALF + h) * ND + dt + 1))
                    for u in range(4):
                        t = 4 * h + u
                        if dt == 0:
                            pe.wait_ge(s["hrow_done"], k * NT + t + 1)
                        i = tr(ps[:, b, u * P:(u + 1) * P], hrow[:, t, dt * P:(dt + 1) * P], ident[:, :])
                    i.then_inc(ready[b], 1)

            for h in range(NHALF):
                normed(0, h)
            part_ends(pe, "tensor")

            bk = banks["batch"]

            def h_ready(k, h):
                pe.wait_ge(s["h_lo_done"], (k * NHALF + h + 1) * ND)

            def project(g, tiles=range(NT)):
                for t in tiles:
                    b = bk.take(pe, ("qkv", g, t), until=(s["v_done"], g * NT + t + 1))
                    split_mm(ps[:, b, 0:GW], lambda a, q: hT[:, a, q, t * P:(t + 1) * P],
                             lambda a, q: wqkv[:, a, q, g, :], ND).then_inc(ready[b], 1)

            def turn_rows(h, slot, key, done, n):
                b = bk.take(pe, key + (h,), until=(done, NHALF * n + h + 1))
                for u in range(4):
                    i = tr(ps[0:HD, b, u * P:(u + 1) * P], rotated(4 * h + u)[:, slot * HD:(slot + 1) * HD],
                           ident[:, :])
                i.then_inc(ready[b], 1)

            def turn_head(u):
                g = u // GQ
                for h in range(NHALF):
                    if u % GQ == 0:
                        pe.wait_ge(s["rot_done"], g * NT + 4 * (h + 1))
                        turn_rows(h, GQ, ("k", g), s["k_lo_done"], g)
                    turn_rows(h, u % GQ, ("q", u), s["q_lo_done"], u)

            def score_rows(u, i):
                g, r, n = u // GQ, u % QRING, (i + 1) * P
                b = bk.take(pe, ("rows", u, i), 1 if n <= HALF else 2)
                if i % 4 == 0:
                    pe.wait_ge(s["q_done"], NHALF * u + i // 4 + 1)
                    pe.wait_ge(s["k_lo_done"], NHALF * g + i // 4 + 1)
                for c in range(0, n, HALF):
                    e = min(n, c + HALF)
                    q = mm(ps[:, b + c // HALF, 0:e - c], qhh[:, r, i * P:(i + 1) * P], khl[:, g % 2, c:e],
                           start=True, stop=True)
                q.then_inc(ready[b], 1)

            def turn_maxima(u):
                b = bk.take(pe, ("nm", u), until=(s["nmr_done"], u + 1))
                pe.wait_ge(s["nm_done"], u + 1)
                tr(ps[0:NT, b, 0:P], nm[:, u % 2, :], ident[:, :]).then_inc(ready[b], 1)

            def score_cols(u, c, j):
                g, r = u // GQ, u % QRING
                lo, hi = max(c * HALF, j * P), (c + 1) * HALF
                b = bk.take(pe, ("cols", u, c, j), until=(s["exp_done"], 12 * u + 4 * c + j + 1))
                if c == 0 and j == 0:
                    pe.wait_ge(s["q_lo_done"], NHALF * (u + 1))
                    pe.wait_ge(*m_loaded(u))
                mm(ps[:, b, 0:hi - lo], khl[:, g % 2, j * P:(j + 1) * P], qhh[:, r, lo:hi], start=True, stop=False)
                mm(ps[:, b, 0:hi - lo], k2[:, g % 2, j * P:(j + 1) * P], q2[:, r, lo:hi], start=False, stop=True)\
                    .then_inc(ready[b], 1)

            def values(u, c, i, b):
                g = u // GQ
                if i == 0 and u % GQ == 0:
                    pe.wait_ge(s["v_done"], (g + 1) * NT)
                pe.wait_ge(s["masked_done"], NT * u + i + 1)
                for j in range(i + 1):
                    lo = max(c * HALF, j * P)
                    slot = (12 * u + 4 * c + j) % PRING
                    q = mm(ps[:, b, (i % 4) * (HD + 1):(i % 4 + 1) * (HD + 1)],
                           pT[:, slot, i * P - lo:(i + 1) * P - lo], v1[:, g % 2, j, :],
                           start=j == 0, stop=j == i)
                return q

            def turn_outputs(w):
                for h in range(NHALF):
                    b = bk.take(pe, ("o", w, h), until=(s["oT_done"], NHALF * w + h + 1))
                    pe.wait_ge(s["o_done"], 4 * w + 2 + h + 1)
                    for u in range(4):
                        i = tr(ps[:, b, u * P:(u + 1) * P], orow[:, 4 * h + u, :], ident[:, :])
                    i.then_inc(ready[b], 1)

            def gated_rows(dt):
                pe.wait_ge(s["vx_done"], dt + 1)
                for h in range(NHALF):
                    b = bk.take(pe, ("vrow", dt, h), until=(s["vrow_done"], dt * NHALF + h + 1))
                    for u in range(4):
                        i = tr(ps[:, b, u * P:(u + 1) * P], vx[:, dt, (4 * h + u) * P:(4 * h + u + 1) * P],
                               ident[:, :])
                    i.then_inc(ready[b], 1)

            def inverse(ip):
                for dt in range(ND):
                    b = bk.take(pe, ("y", ip, dt))
                    for u in range(2):
                        blk = 2 * ip + u
                        pe.wait_ge(s["y_dve"], 1 + max(n for n, p in enumerate(DVE_PAIRS) if p[1] == blk))
                        pooled = [n for n, p in enumerate(POOL_PAIRS) if p[1] == blk]
                        if pooled:
                            pe.wait_ge(s["y_pool"], 1 + pooled[-1])
                        for q in range(2 * ST):
                            i = mm(ps[:, b, u * S:(u + 1) * S], Yf[:, blk, q // ST, q % ST, dt * P:(dt + 1) * P],
                                   inv[:, q, :], start=q == 0, stop=q == 2 * ST - 1)
                    i.then_inc(ready[b], 1)

            def long_out(h):
                pe.wait_ge(s["yv_done"], ND * (h + 1))
                for t in range(4 * h, 4 * h + 4, 2):
                    b = bk.take(pe, ("out0", t))
                    for u in range(2):
                        for q in range(ND):
                            i = mm(ps[:, b, u * D:(u + 1) * D], x0[:, q, (t + u) * P:(t + u + 1) * P], out_w[:, q, :],
                                   start=q == 0, stop=q == ND - 1)
                    i.then_inc(ready[b], 1)

            def route():
                h_ready(LN_MOE, 0)
                b = bk.take(pe, ("router",))
                split_mm(ps[0:1, b, 0:EXPERTS], lambda a, q: hT[:, a, q, 0:1], lambda a, q: wr[:, a, q, :], ND)\
                    .then_inc(ready[b], 1)

            with pe.Fori(0, B):
                bk.reset()
                for n, e in enumerate(E_ORDER):
                    if n == 4:
                        gated_rows(0)
                    for h in range(NHALF):
                        b = bk.take(pe, ("up", n, h))
                        split_mm(ps[:, b, :], lambda a, q: in_w[:, a, q, e * P:(e + 1) * P],
                                 lambda a, q: hT[:, a, q, h * HALF:(h + 1) * HALF], ND).then_inc(ready[b], 1)
                gated_rows(1)
                vblocks = vrow[:, :, :].rearrange("p (j q) n -> p j q n", q=ST)
                for jp in range(NB // 2):
                    pe.wait_ge(s["vrow_done"], NHALF * (ND - 1) + jp + 1)
                    b = bk.take(pe, ("vf", jp), 4)
                    for c in range(2 * ST):
                        for q in range(ST):
                            i = mm(ps[:, b + c, :], fwd[:, q, c * P:(c + 1) * P], vblocks[:, 2 * jp:2 * jp + 2, q, :],
                                   start=q == 0, stop=q == ST - 1)
                    i.then_inc(ready[b], 1)
                inverse(0)
                long_out(0)
                inverse(1)
                normed(LN_FFN, 0)
                long_out(1)
                for h in range(NHALF):
                    h_ready(LN_FFN, h)
                    for n in range(NH1):
                        if (h, n) == (0, FFN_TURN):
                            normed(LN_FFN, 1)
                        b = bk.take(pe, ("ffn1", h, n), until=(s["gelu_done"], h * NH1 + n + 1))
                        sign_mm(ps[:, b, :], lambda a, q: sgn1[:, q, n * P:(n + 1) * P],
                                lambda a, q: hT[:, a, q, h * HALF:(h + 1) * HALF],
                                [(a, q) for q in range(ND) for a in range(2)]).then_inc(ready[b], 1)
                for t in range(0, NT, 2):
                    b = bk.take(pe, ("ffn2", t))
                    for u in range(2):
                        if u == 0 and t % 4 == 0:
                            pe.wait_ge(s["g_lo_done"], NH1 * (t // 4 + 1))
                        i = sign_mm(ps[:, b, u * D:(u + 1) * D],
                                    lambda a, q: gT[:, a, q, (t + u) * P:(t + u + 1) * P],
                                    lambda a, q: sgn2[:, q, :], [(a, q) for q in range(NH1) for a in range(2)])
                    i.then_inc(ready[b], 1)
                for h in range(NHALF):
                    normed(LN_ATT, h)
                    h_ready(LN_ATT, h)
                    project(0, range(4 * h, 4 * h + 4))
                turn_head(0)
                for i in range(NT):
                    score_rows(0, i)
                turn_maxima(0)
                for u in range(HEADS):
                    w = u + 1
                    for j in range(4):
                        score_cols(u, 0, j)
                    if w < HEADS:
                        turn_head(w)
                    if u >= 2 and u % 2 == 0:
                        turn_outputs(u // 2 - 1)
                    if u % GQ == 2 and u // GQ + 1 < KV:
                        project(u // GQ + 1)
                    for j in range(4):
                        score_cols(u, 1, j)
                    b = bk.take(pe, ("pv", u, 0), until=(s["o_done"], 2 * u + 1))
                    for i in range(4):
                        if i == 3 and w < HEADS:
                            for k in range(3):
                                score_rows(w, k)
                        q = values(u, 0, i, b)
                    q.then_inc(ready[b], 1)
                    if w < HEADS:
                        for k in range(3, 4):
                            score_rows(w, k)
                    for j in range(4, NT):
                        score_cols(u, 1, j)
                        if w < HEADS:
                            score_rows(w, j)
                    b = bk.take(pe, ("pv", u, 1), until=(s["o_done"], 2 * u + 2))
                    for i in range(4, NT):
                        if i == 6 and w < HEADS:
                            turn_maxima(w)
                        q = values(u, 1, i, b)
                    q.then_inc(ready[b], 1)
                turn_outputs(HEADS // 2 - 1)
                for t in range(0, NT, 2):
                    b = bk.take(pe, ("out1", t))
                    pe.wait_ge(s["oT_done"], HEADS - 1 + t // 4)
                    for u in range(2):
                        if (t, u) == (NT - 2, 1):
                            route()
                        for q in range(HEADS // 2):
                            i = mm(ps[:, b, u * D:(u + 1) * D], oT[:, q, (t + u) * P:(t + u + 1) * P], wo[:, q, :],
                                   start=q == 0, stop=q == HEADS // 2 - 1)
                    i.then_inc(ready[b], 1)
                    if t == NT - 4:
                        normed(LN_MOE, 0)
                normed(LN_MOE, 1)
                for k in range(TOPK):
                    pe.wait_ge(s["w1_split"], k + 1)
                    for h in range(NHALF):
                        if k == 0 and h:
                            h_ready(LN_MOE, h)
                        for n in range(ND):
                            b = bk.take(pe, ("moe1", k, h, n), until=(s["egelu_done"], (k * NHALF + h) * ND + n + 1))
                            split_mm(ps[:, b, :], lambda a, q: w1s[:, k, a, q, n * P:(n + 1) * P],
                                     lambda a, q: hT[:, a, q, h * HALF:(h + 1) * HALF], ND).then_inc(ready[b], 1)
                for h in range(NHALF):
                    normed(LN_NEXT, h)
                for t in range(0, NT, 2):
                    b = bk.take(pe, ("moe2", t))
                    pe.wait_ge(s["egelu_done"], ND * NHALF + ND * (t // 4 + 1))
                    for u in range(2):
                        for n in range(TOPK * ND):
                            i = mm(ps[:, b, u * D:(u + 1) * D], geT[:, n, (t + u) * P:(t + u + 1) * P],
                                   w2e[:, n // ND, n % ND, :], start=n == 0, stop=n == TOPK * ND - 1)
                    i.then_inc(ready[b], 1)
                part_ends(pe, "tensor")

        @block.scalar
        def _(act):
            A = nc.scalar.activation
            bk = banks["setup"]

            act.wait_ge(s["loaded_c"], 16)
            A(cT[:, :, :, :], cT[:, :, :, :], ACT.Silu).then_inc(s["silu_done"], 1)
            for layer in range(3):
                act.wait_ge(s["filter_angle"], layer + 1)
                A(sine[:, :], ang[:, :], ACT.Sin).then_inc(s["filter_sine"], 1)
            act.wait_ge(s["loaded"], 16 * NLOADED)
            A(sgn1[:, :, :], x[:, :, :].rearrange("p t n -> p (t n)").rearrange("p (q n) -> p q n", q=ND), ACT.Sign)\
                .then_inc(s["sgn_done"], 1)
            A(sgn2[:, :, :], w2T[:, :, :], ACT.Sign).then_inc(s["sgn_done"], 1)
            act.drain()
            A(w2T[:, :, :], w2T[:, :, :], ACT.Abs).then_inc(s["abs_done"], 1)
            for m in range(NB):
                for c in range(2):
                    b = bk.wait(act, ("kf", m, c))
                    A(Kf[:, m, c, :, :], ps[:, b, :].rearrange("p (f n) -> p f n", f=ST), ACT.Copy)\
                        .then_inc(freed[b], 1)
            act.drain().then_inc(s["kf_done"], 1)
            b = bk.wait(act, ("alpha2",))
            A(alpha2[:, :], ps[:, b, 0:D], ACT.Copy, scale=1.0 / HID).then_inc(freed[b], 1)

            def normed(k, h, mod):
                for dt in range(ND):
                    n = (k * NHALF + h) * ND + dt
                    b = bk.wait(act, ("ln", k, h, dt))
                    if n >= 2:
                        act.wait_ge(s["h_lo_done"], n - 1)
                    args = {"bias": mod[:, 0, dt:dt + 1], "scale": mod[:, 1, dt:dt + 1]}
                    A(hfull[:, n % 2, :], ps[:, b, :], ACT.Identity, **args)
                    A(hT[:, 0, dt, h * HALF:(h + 1) * HALF], ps[:, b, :], ACT.Identity, **args)\
                        .then_inc(s["hT_done"], 1)

            act.wait_ge(s["mod_picked"], 1)
            for h in range(NHALF):
                normed(0, h, modn)
            part_ends(act, "scalar")

            bk = banks["batch"]

            def turn_head(u):
                g = u // GQ
                if u >= QRING:
                    bk.wait(act, ("pv", u - QRING, 1))
                for h in range(NHALF):
                    if u % GQ == 0:
                        b = bk.wait(act, ("k", g, h))
                        cols = slice(h * HALF, (h + 1) * HALF)
                        A(khl[0:HD, g % 2, cols], ps[0:HD, b, :], ACT.Copy)
                        A(k2[0:HD, g % 2, cols], ps[0:HD, b, :], ACT.Copy).then_inc(s["k_done"], 1)
                    b = bk.wait(act, ("q", u, h))
                    for half in (HD, 0):
                        i = A(qhh[half:half + HD, u % QRING, h * HALF:(h + 1) * HALF], ps[0:HD, b, :], ACT.Copy)
                    i.then_inc(s["q_done"], 1)

            def turn_maxima(u):
                b = bk.wait(act, ("nm", u))
                if u >= 2:
                    act.wait_ge(*m_loaded(u - 2))
                A(nmr[:, u % 2, :], ps[0:NT, b, 0:P], ACT.Copy).then_inc(s["nmr_done"], 1)

            def exps(u, c, j):
                n = 12 * u + 4 * c + j
                lo = max(c * HALF, j * P)
                b = bk.wait(act, ("cols", u, c, j))
                if (c, j) == (0, 0) and u:
                    bk.wait(act, ("pv", u - 1, 1))
                if (c, j) == (1, PRING - 4):
                    bk.wait(act, ("pv", u, 0))
                A(pT[:, n % PRING, 0:(c + 1) * HALF - lo], ps[:, b, 0:(c + 1) * HALF - lo], ACT.Exp, scale=SCALE)\
                    .then_inc(s["exp_done"], 1)

            def value_rows(g, tiles=range(NT)):
                for t in tiles:
                    b = bk.wait(act, ("qkv", g, t))
                    act.wait_ge(s["rot_a"], g * NT + t + 1)
                    A(v1[:, g % 2, t, 0:HD], ps[:, b, QK:GW], ACT.Copy).then_inc(s["v_done"], 1)

            def turn_outputs(w):
                for h in range(NHALF):
                    b = bk.wait(act, ("o", w, h))
                    A(oT[:, w, h * HALF:(h + 1) * HALF], ps[:, b, :], ACT.Copy).then_inc(s["oT_done"], 1)

            def gated_rows(dt):
                for h in range(NHALF):
                    b = bk.wait(act, ("vrow", dt, h))
                    A(vrow[:, 4 * h:4 * h + 4, dt * P:(dt + 1) * P],
                      ps[:, b, :].rearrange("p (t n) -> p t n", t=4), ACT.Copy).then_inc(s["vrow_done"], 1)

            with act.Fori(0, B):
                for n, e in enumerate(E_ORDER):
                    if n >= 2:
                        act.wait_ge(s["conv_done"], n - 1)
                    for h in range(NHALF):
                        if (n, h) == (4, 0):
                            gated_rows(0)
                        b = bk.wait(act, ("up", n, h))
                        A(up[:, n % 2, 2 + h * HALF:2 + (h + 1) * HALF], ps[:, b, :], ACT.Identity,
                          bias=in_b[:, e:e + 1]).then_inc(freed[b], 1)
                    act.drain()
                    if n == len(E_ORDER) - 1:
                        gated_rows(1)
                    A(tap[:, n % 2, :], up[:, n % 2, 2:L + 2], ACT.Identity, scale=short_w[:, e, 2:3],
                      bias=short_b[:, e:e + 1]).then_inc(s["tap_done"], 1)
                act.wait_ge(s["mod_picked"], 1)
                act.wait_ge(weights_stored, 16 * 4)
                normed(LN_FFN, 0, modb[:, 0, 2:4])
                for h in range(NHALF):
                    for n in range(NH1):
                        if (h, n) == (0, FFN_TURN):
                            normed(LN_FFN, 1, modb[:, 0, 2:4])
                        b = bk.wait(act, ("ffn1", h, n))
                        m = h * NH1 + n
                        if m >= 4:
                            act.wait_ge(s["g_lo_done"], m - 3)
                        A(gfull[:, m % 4, :], ps[:, b, :], ACT.Gelu, scale=alpha1[:, n:n + 1],
                          bias=ffn_b1[:, n:n + 1]).then_inc(s["gelu_done"], 1)
                for h in range(NHALF):
                    normed(LN_ATT, h, modb[:, 1, 0:2])
                value_rows(0)
                turn_head(0)
                turn_maxima(0)
                for u in range(HEADS):
                    w = u + 1
                    for j in range(4):
                        exps(u, 0, j)
                    if w < HEADS:
                        turn_head(w)
                    if u >= 2 and u % 2 == 0:
                        turn_outputs(u // 2 - 1)
                    if u % GQ == 2 and u // GQ + 1 < KV:
                        value_rows(u // GQ + 1)
                    for j in range(NT):
                        exps(u, 1, j)
                    if w < HEADS:
                        turn_maxima(w)
                turn_outputs(HEADS // 2 - 1)
                for h in range(NHALF):
                    normed(LN_MOE, h, modb[:, 1, 2:4])
                for k in range(TOPK):
                    act.wait_ge(s[f"expert_loaded{k}"], 16 * 3)
                    for h in range(NHALF):
                        for n in range(ND):
                            b = bk.wait(act, ("moe1", k, h, n))
                            A(geT[:, k * ND + n, h * HALF:(h + 1) * HALF], ps[:, b, :], ACT.Gelu,
                              bias=b1e[:, k, n:n + 1]).then_inc(s["egelu_done"], 1)
                for h in range(NHALF):
                    normed(LN_NEXT, h, modn)
                part_ends(act, "scalar")

        @block.vector
        def _(dve):
            V = nc.vector
            bk = banks["setup"]
            def modulation(layer):
                b = bk.wait(dve, ("modT", layer))
                V.tensor_copy(modT[:, layer, :, :, :].rearrange("p k t b -> p (k t b)"), ps[:, b, 0:4 * ND * B])\
                    .then_inc(freed[b], 1)
                dve.drain()
                for k in (1, 3):
                    V.tensor_scalar(modT[:, layer, k, :, :], modT[:, layer, k, :, :], 1.0, None, ALU.add)
                b = bk.wait(dve, ("gate", layer))
                V.tensor_copy(grow[:, layer, :], ps[0:B, b, :]).then_inc(freed[b], 1)
                dve.drain()
                V.scalar_tensor_tensor(out=gabs[:, :], in0=grow[:, layer, :], scalar=-1.0, in1=grow[:, layer, :],
                                       op0=ALU.mult, op1=ALU.max)
                V.tensor_scalar(gsgn[:, :], grow[:, layer, :], 0.0, 2.0, ALU.is_ge, ALU.mult)
                dve.drain()
                V.tensor_scalar(gabs[:, :], gabs[:, :], 0.25, None, ALU.max)
                V.tensor_scalar(gsgn[:, :], gsgn[:, :], -1.0, None, ALU.add)
                dve.drain()
                V.tensor_tensor(grow[:, layer, :], gabs[:, :], gsgn[:, :], ALU.mult).then_inc(s["gate_rows"], 1)
                dve.drain()

            dve.wait_ge(s["loaded_filter"], 16 * 9)
            for layer in range(3):
                if layer:
                    dve.wait_ge(s["filter_sine"], layer)
                for h in range(NHALF):
                    b = bk.wait(dve, ("filter", layer, h))
                    V.tensor_scalar(ang[:, h * HALF:(h + 1) * HALF], ps[0:FILT, b, :], fb[:, layer:layer + 1],
                                    fb[:, 3:4], ALU.add, ALU.mult).then_inc(freed[b], 1)
                dve.drain()
                V.tensor_scalar(turn[:, :], ang[:, :], float(1 / (2 * np.pi)), ROUND, ALU.mult, ALU.add)
                dve.drain()
                V.tensor_scalar(turn[:, :], turn[:, :], ROUND, None, ALU.subtract)
                dve.drain()
                V.scalar_tensor_tensor(out=ang[:, :], in0=turn[:, :], scalar=-TWO_PI_HI, in1=ang[:, :],
                                       op0=ALU.mult, op1=ALU.add)
                dve.drain()
                V.scalar_tensor_tensor(out=ang[:, :], in0=turn[:, :], scalar=-TWO_PI_LO, in1=ang[:, :],
                                       op0=ALU.mult, op1=ALU.add)
                dve.drain()
                V.tensor_scalar(ang[:, :], ang[:, :], PI_DOWN, -PI_DOWN, ALU.min, ALU.max)\
                    .then_inc(s["filter_angle"], 1)
                if layer == 0:
                    modulation(0)
            dve.wait_ge(s["loaded_windows"], 16 * 3)
            for t in range(0, NT, 2):
                b = bk.wait(dve, ("kern", t))
                V.tensor_tensor(kern[:, t:t + 2, :], ps[:, b, :].rearrange("p (t n) -> p t n", t=2),
                                decay[:, t:t + 2, :], ALU.mult).then_inc(s["kern_done"], 1)
            modulation(1)
            dve.wait_ge(s["loaded"], 16 * NLOADED)
            V.reduce_sum(alpha1[:, :], w1rows[:, :, :], AX, apply_absolute_value=True)
            dve.drain()
            V.tensor_scalar(alpha1[:, :], alpha1[:, :], 1.0 / D, None, ALU.mult)
            def stats(src, tiles):
                for t in tiles:
                    V.bn_stats(stat[:, t, :], src[:, t, :])

            def normed(k, h, src):
                four = slice(4 * h, 4 * h + 4)
                dve.drain()
                for t in range(4 * h, 4 * h + 4):
                    V.bn_aggr(mv[:, t, :], stat[:, t, :])
                dve.drain()
                V.tensor_scalar(var[:, four], mv[:, four, 1], EPS, None, ALU.add).then_inc(s["var_done"], 1)
                dve.wait_ge(s["rstd_done"], k * NHALF + h + 1)
                for t in range(4 * h, 4 * h + 4):
                    V.tensor_scalar(hrow[:, t, :], src[:, t, :], mv[:, t, 0:1], rstd[:, t:t + 1],
                                    ALU.subtract, ALU.mult).then_inc(s["hrow_done"], 1)

            def h_low(k, h):
                for dt in range(ND):
                    n = (k * NHALF + h) * ND + dt
                    cols = slice(h * HALF, (h + 1) * HALF)
                    dve.wait_ge(s["hT_done"], n + 1)
                    V.tensor_tensor(hT[:, 1, dt, cols], hfull[:, n % 2, :], hT[:, 0, dt, cols].bitcast(F32),
                                    ALU.subtract).then_inc(s["h_lo_done"], 1)

            def split(dst, src, done=None):
                V.tensor_copy(dst[0], src)
                dve.drain()
                i = V.tensor_tensor(dst[1], src, dst[0].bitcast(F32), ALU.subtract)
                if done is not None:
                    i.then_inc(done, 1)

            def pick_first(bi):
                V.tensor_copy(modn[:, :, :].rearrange("p k t -> p (k t)"),
                              modT[:, 0, 0:2, :, :].rearrange("p k t b -> p (k t) b")[:, :, bass.ds(bi, 1)]
                              .rearrange("p n b -> p (n b)")).then_inc(s["mod_picked"], 1)

            dve.wait_ge(s["loaded_raw"], 16 * 3)
            split([in_w[:, a, :, :] for a in range(2)], wraw[:, :, 0:INNER], s["raw_used"])
            split([wr[:, a, :, :] for a in range(2)], wr_raw[:, :, :])
            dve.wait_ge(s["loaded_raw"], 16 * 4)
            split([wqkv[:, a, :, :, :].rearrange("p q g n -> p q (g n)") for a in range(2)], wraw[:, :, :])
            dve.drain()
            pick_first(0)
            dve.wait_ge(s["x_loaded"], 16)
            for h in range(NHALF):
                stats(x, range(4 * h, 4 * h + 4))
                normed(0, h, x)
            for h in range(NHALF):
                h_low(0, h)
            part_ends(dve, "vector")

            bk = banks["batch"]

            def add_to_x(name, h, gate, bias=0, norm_follows=True):
                if bias:
                    dve.wait_ge(s["bias_added"], NHALF * (bias - 1) + h + 1)
                for t in range(4 * h, 4 * h + 4, 2):
                    b = bk.wait(dve, (name, t))
                    r = (t // 2) % 2
                    V.tensor_tensor(tmp[:, r, :, :], ps[:, b, :].rearrange("p (t n) -> p t n", t=2),
                                    gate.unsqueeze(1).broadcast_to([P, 2, D]), ALU.mult).then_inc(freed[b], 1)
                    dve.drain()
                    V.tensor_tensor(x[:, t:t + 2, :], x[:, t:t + 2, :], tmp[:, r, :, :], ALU.add)
                    if norm_follows:
                        dve.drain()
                        stats(x, (t, t + 1))
                dve.drain()

            def rotate(g, tiles=range(NT)):
                for t in tiles:
                    b = bk.wait(dve, ("qkv", g, t))
                    r = t % 2
                    n = g * NT + t
                    if n >= 2:
                        dve.wait_ge(s["rot_done"], n - 1)
                    v = ps[:, b, 0:QK].rearrange("p (h e i) -> p h e i", e=2, i=HD // 2)
                    cs = [rope[:, t, q, :].unsqueeze(1).broadcast_to([P, GQ + 1, HD // 2]) for q in range(2)]
                    A4, B4 = rot_buf(r)
                    for e in range(2):
                        V.tensor_tensor(A4[:, :, e, :], v[:, :, e, :], cs[0], ALU.mult)
                    V.tensor_tensor(B4[:, :, 0, :], v[:, :, 1, :], cs[1], ALU.mult)
                    V.tensor_tensor(B4[:, :, 1, :], v[:, :, 0, :], cs[1], ALU.mult).then_inc(s["rot_a"], 1)

            def turn_head(u):
                g = u // GQ
                for h in range(NHALF):
                    cols = slice(h * HALF, (h + 1) * HALF)
                    if u % GQ == 0:
                        b = bk.wait(dve, ("k", g, h))
                        dve.wait_ge(s["k_done"], NHALF * g + h + 1)
                        V.tensor_tensor(khl[HD:P, g % 2, cols], ps[0:HD, b, :], khl[0:HD, g % 2, cols].bitcast(F32),
                                        ALU.subtract).then_inc(s["k_lo_done"], 1)
                    b = bk.wait(dve, ("q", u, h))
                    dve.wait_ge(s["q_done"], NHALF * u + h + 1)
                    V.tensor_tensor(q2[0:HD, u % QRING, cols], ps[0:HD, b, :], qhh[0:HD, u % QRING, cols].bitcast(F32),
                                    ALU.subtract).then_inc(s["q_lo_done"], 1)

            def row_maxima(u, i):
                n = (i + 1) * P
                b = bk.wait(dve, ("rows", u, i))
                v = (ps[:, b:b + 2, :].rearrange("p a n -> p (a n)") if n > HALF else ps[:, b, :])[:, 0:n]
                V.tensor_tensor_reduce(out=v, in0=v, in1=mrow[:, L - n:L], scale=1.0, scalar=-3e38, op0=ALU.add,
                                       op1=ALU.max, accum_out=mx[:, u % 2, i:i + 1]).then_inc(freed[b], 1)

            def negate(u):
                dve.drain()
                V.tensor_scalar(nm[:, u % 2, :], mx[:, u % 2, :], -1.0, None, ALU.mult).then_inc(s["nm_done"], 1)

            def normalise(u, c):
                b = bk.wait(dve, ("pv", u, c))
                v = ps[:, b, 0:4 * (HD + 1)].rearrange("p (i n) -> p i n", n=HD + 1)
                V.reciprocal(den[:, c, :], v[:, :, HD])
                dve.drain()
                if u >= 2 and u % 2 == 0:
                    dve.wait_ge(s["oT_done"], u)
                V.tensor_tensor(orow[:, 4 * c:4 * c + 4, (u % 2) * HD:(u % 2 + 1) * HD], v[:, :, 0:HD],
                                den[:, c, :].unsqueeze(2).broadcast_to([P, 4, HD]), ALU.mult)\
                    .then_inc(s["o_done"], 1)

            def skip_and_gate(ip):
                for dt in range(ND):
                    b = bk.wait(dve, ("y", ip, dt))
                    cols = slice(ip * HALF, (ip + 1) * HALF)
                    V.scalar_tensor_tensor(out=vx[:, dt, cols], in0=vx[:, dt, cols], scalar=filt_b[:, dt:dt + 1],
                                           in1=ps[:, b, :], op0=ALU.mult, op1=ALU.add).then_inc(freed[b], 1)
                    dve.drain()
                    V.tensor_tensor(x0[:, dt, cols], vx[:, dt, cols], x0[:, dt, cols], ALU.mult)\
                        .then_inc(s["yv_done"], 1)

            with dve.Fori(0, B) as bi:
                V.tensor_copy(modb[:, :, :, :].rearrange("p l k t -> p (l k t)"),
                              modT[:, :, :, :, :].rearrange("p l k t b -> p (l k t) b")[:, :, bass.ds(bi, 1)]
                              .rearrange("p n b -> p (n b)")).then_inc(s["mod_picked"], 1)
                for r in range(2):
                    V.memset(up[:, r, 0:2], 0.0)
                dve.drain()
                for n, e in enumerate(E_ORDER):
                    dt = e % ND
                    dst = {0: x0[:, dt, :], 1: x1[:, :], 2: vx[:, dt, :]}[e // ND]
                    dve.wait_ge(s["tap_done"], n + 1)
                    V.scalar_tensor_tensor(out=tap[:, n % 2, :], in0=up[:, n % 2, 1:L + 1], scalar=short_w[:, e, 1:2],
                                           in1=tap[:, n % 2, :], op0=ALU.mult, op1=ALU.add)
                    dve.drain()
                    V.scalar_tensor_tensor(out=dst, in0=up[:, n % 2, 0:L], scalar=short_w[:, e, 0:1],
                                           in1=tap[:, n % 2, :], op0=ALU.mult, op1=ALU.add)\
                        .then_inc(s["conv_done"], 1)
                    if e // ND == 1:
                        dve.drain()
                        V.tensor_tensor(vx[:, dt, :], vx[:, dt, :], x1[:, :], ALU.mult).then_inc(s["vx_done"], 1)
                        dve.drain()
                dve.drain()
                for n, (j, i) in enumerate(PAIRS):
                    if n == len(PAIRS) - 1:
                        skip_and_gate(0)
                    b = bk.wait(dve, ("vf", j // 2))
                    slot = int((j, i) in POOL_PAIRS)
                    if slot and POOL_PAIRS.index((j, i)):
                        dve.wait_ge(s["y_pool"], POOL_PAIRS.index((j, i)))
                    v = ps[:, b:b + 2 * ST, j % 2 * D:(j % 2 + 1) * D].rearrange("p (c f) n -> p c f n", c=2)
                    for k in range(2):
                        q = V.tensor_tensor(prod[:, slot, k, :, :, :], v,
                                            Kf[:, i - j, k, :, :].unsqueeze(1).broadcast_to([P, 2, ST, D]), ALU.mult)
                    pr = prod[:, slot]
                    if (j, i) in POOL_PAIRS:
                        q.then_inc(s["prod_done"], 1)
                        continue
                    if i == NB - 1 and j % 2:
                        q.then_inc(freed[b], 1)
                    dve.drain()
                    if j == 0:
                        V.tensor_tensor(Yf[:, i, 0, :, :], pr[:, 0, 0, :, :], pr[:, 1, 1, :, :], ALU.subtract)
                        V.tensor_tensor(Yf[:, i, 1, :, :], pr[:, 0, 1, :, :], pr[:, 1, 0, :, :], ALU.add)\
                            .then_inc(s["y_dve"], 1)
                    else:
                        before = [p for p in POOL_PAIRS if p[1] == i and PAIRS.index(p) < n]
                        if before:
                            dve.wait_ge(s["y_pool"], POOL_PAIRS.index(before[-1]) + 1)
                        for c, (k, w, op) in ((0, (0, 0, ALU.add)), (1, (0, 1, ALU.add)),
                                              (0, (1, 1, ALU.subtract)), (1, (1, 0, ALU.add))):
                            if k == 1 and c == 0:
                                dve.drain()
                            q = V.tensor_tensor(Yf[:, i, c, :, :], Yf[:, i, c, :, :], pr[:, k, w, :, :], op)
                        q.then_inc(s["y_dve"], 1)
                    dve.drain()
                dve.wait_ge(s["gates_mixed"], 1)
                add_to_x("out0", 0, gates[:, 0, :], bias=1)
                normed(LN_FFN, 0, x)
                skip_and_gate(1)
                h_low(LN_FFN, 0)
                add_to_x("out0", 1, gates[:, 0, :], bias=1)
                normed(LN_FFN, 1, x)
                for h in range(NHALF):
                    for n in range(NH1):
                        if (h, n) == (0, FFN_LOW):
                            h_low(LN_FFN, 1)
                        m = h * NH1 + n
                        cols = slice(h * HALF, (h + 1) * HALF)
                        dve.wait_ge(s["gelu_done"], m + 1)
                        V.tensor_copy(gT[:, 0, n, cols], gfull[:, m % 4, :])
                        dve.drain()
                        V.tensor_tensor(gT[:, 1, n, cols], gfull[:, m % 4, :], gT[:, 0, n, cols].bitcast(F32),
                                        ALU.subtract).then_inc(s["g_lo_done"], 1)
                for h in range(NHALF):
                    add_to_x("ffn2", h, escale[:, 0, :], bias=2)
                    if h:
                        h_low(LN_ATT, 0)
                    normed(LN_ATT, h, x)
                rotate(0, range(2))
                h_low(LN_ATT, 1)
                rotate(0, range(2, NT))
                turn_head(0)
                for i in range(NT):
                    row_maxima(0, i)
                negate(0)
                for u in range(HEADS):
                    w = u + 1
                    if w < HEADS:
                        turn_head(w)
                    if u % GQ == 2 and u // GQ + 1 < KV:
                        rotate(u // GQ + 1)
                    if w < HEADS:
                        for i in range(3):
                            row_maxima(w, i)
                    normalise(u, 0)
                    if w < HEADS:
                        for i in range(3, NT):
                            row_maxima(w, i)
                        if w >= 2:
                            dve.wait_ge(s["nmr_done"], w - 1)
                        negate(w)
                    normalise(u, 1)
                add_to_x("out1", 0, gates[:, 2, :])
                normed(LN_MOE, 0, x)
                h_low(LN_MOE, 0)
                b = bk.wait(dve, ("router",))
                V.tensor_tensor(score[:, :], ps[0:1, b, 0:EXPERTS], br[:, :], ALU.add).then_inc(freed[b], 1)
                dve.drain()
                V.max(top[:, :], score[:, :])
                dve.drain()
                V.max_index(topi[:, :], top[:, :], score[:, :]).then_inc(s["top_done"], 1)
                add_to_x("out1", 1, gates[:, 2, :])
                normed(LN_MOE, 1, x)
                for k in range(TOPK):
                    dve.wait_ge(s[f"w1_loaded{k}"], 16)
                    split([w1s[:, k, a, :, :] for a in range(2)], w1e[:, k, :, :], s["w1_split"])
                    if k == 0:
                        h_low(LN_MOE, 1)
                pick_first((bi + 1) % B)
                dve.wait_ge(s["x_next_loaded"], 16)
                dve.wait_ge(s["hT_done"], (LN_MOE + 1) * NHALF * ND)
                for h in range(NHALF):
                    stats(xn, range(4 * h, 4 * h + 4))
                    normed(LN_NEXT, h, xn)
                for h in range(NHALF):
                    h_low(LN_NEXT, h)
                for h in range(NHALF):
                    add_to_x("moe2", h, escale[:, 1, :], bias=3, norm_follows=False)
                dve.drain().then_inc(s["x_done"], 1)
                part_ends(dve, "vector")

        @block.gpsimd
        def _(pool):
            G = nc.gpsimd
            G.memset(ones[:, :], 1.0)
            G.memset(ident[:, :], 0.0)
            G.memset(mrow[:, :], 0.0)
            G.memset(neghalf[:, :], -0.5)
            pool.drain()
            G.affine_select(out=ident[:, :], in_=ident[:, :], compare_op=ALU.not_equal, fill=1.0, base=0,
                            pattern=[[-1, P]], channel_multiplier=1)
            G.affine_select(out=mrow[:, L - P:L], in_=mrow[:, L - P:L], compare_op=ALU.is_ge, fill=MASKED, base=0,
                            pattern=[[-1, P]], channel_multiplier=1)
            pool.drain().then_inc(s["const_made"], 1)

            def normed(k, h):
                four = slice(4 * h, 4 * h + 4)
                pool.wait_ge(s["var_done"], k * NHALF + h + 1)
                G.tensor_tensor(rstd[:, four], var[:, four], neghalf[:, four], ALU.pow).then_inc(s["rstd_done"], 1)

            for h in range(NHALF):
                normed(0, h)
            part_ends(pool, "gpsimd")

            def add_bias(h, n):
                for t in range(4 * h, 4 * h + 4, 2):
                    q = G.tensor_tensor(x[:, t:t + 2, :], x[:, t:t + 2, :],
                                        terms[:, n, :].unsqueeze(1).broadcast_to([P, 2, D]), ALU.add)
                q.then_inc(s["bias_added"], 1)

            def normed_then_bias(k, h, n):
                normed(k, h)
                pool.wait_ge(s["hrow_done"], k * NT + 4 * h + 4)
                add_bias(h, n)

            def mask(u, c, j):
                pool.wait_ge(s["exp_done"], 12 * u + 4 * c + j + 1)
                v = pT[:, (12 * u + 4 * c + j) % PRING, 0:P]
                G.affine_select(out=v, in_=v, compare_op=ALU.is_ge, fill=0.0, base=0, pattern=[[1, P]],
                                channel_multiplier=-1).then_inc(s["masked_done"], 1)

            def rotate(g):
                for t in range(NT):
                    pool.wait_ge(s["rot_a"], g * NT + t + 1)
                    if g and t == 0:
                        pool.wait_ge(s["q_done"], NHALF * GQ * g)
                    A4, B4 = rot_buf(t % 2)
                    R4 = rotated(t).rearrange("p (h e i) -> p h e i", e=2, i=HD // 2)
                    G.tensor_tensor(R4[:, :, 0, :], A4[:, :, 0, :], B4[:, :, 0, :], ALU.subtract)
                    G.tensor_tensor(R4[:, :, 1, :], A4[:, :, 1, :], B4[:, :, 1, :], ALU.add).then_inc(s["rot_done"], 1)

            with pool.Fori(0, B):
                pool.wait_ge(s["gates_loaded"], 16)
                G.tensor_tensor(terms[:, 0, :], rows[:, 0, :], gates[:, 0, :], ALU.mult)
                G.tensor_tensor(terms[:, 1, :], rows[:, 1, :], gates[:, 1, :], ALU.mult)
                G.tensor_tensor(escale[:, 0, :], alpha2[:, :], gates[:, 1, :], ALU.mult)
                G.tensor_scalar(escale[:, 1, :], gates[:, 3, :], 1.0 / TOPK, 0.0, ALU.mult, ALU.add)
                pool.drain().then_inc(s["gates_mixed"], 1)
                pool.wait_ge(s["x_loaded"], 16)
                for h in range(NHALF):
                    add_bias(h, 0)
                for n, (j, i) in enumerate(POOL_PAIRS):
                    pool.wait_ge(s["prod_done"], n + 1)
                    pool.wait_ge(s["y_dve"], DVE_PAIRS.index((0, i)) + 1)
                    pr = prod[:, 1]
                    for c, (k, w, op) in ((0, (0, 0, ALU.add)), (1, (0, 1, ALU.add)),
                                          (0, (1, 1, ALU.subtract)), (1, (1, 0, ALU.add))):
                        if k == 1 and c == 0:
                            pool.drain()
                        q = G.tensor_tensor(Yf[:, i, c, :, :], Yf[:, i, c, :, :], pr[:, k, w, :, :], op)
                    q.then_inc(s["y_pool"], 1)
                    pool.drain()
                for h in range(NHALF):
                    normed_then_bias(LN_FFN, h, 1)
                for h in range(NHALF):
                    normed(LN_ATT, h)
                G.memset(v1[:, :, :, HD:HD + 1], 1.0)
                pool.drain()
                G.memset(k2[HD:HD + 1, :, :].bitcast(F32), 1.0)
                pool.drain()
                rotate(0)
                for u in range(HEADS):
                    for j in range(4):
                        mask(u, 0, j)
                    if u % GQ == 2 and u // GQ + 1 < KV:
                        rotate(u // GQ + 1)
                    for j in range(4, NT):
                        mask(u, 1, j)
                for h in range(NHALF):
                    normed(LN_MOE, h)
                for h in range(NHALF):
                    normed(LN_NEXT, h)
                for k in range(TOPK):
                    pool.wait_ge(s[f"expert_loaded{k}"], 16 * 3)
                G.tensor_tensor(b2e[:, 0, :], b2e[:, 0, :], b2e[:, 1, :], ALU.add)
                pool.drain()
                G.tensor_tensor(terms[:, 2, :], b2e[:, 0, :], escale[:, 1, :], ALU.mult)
                pool.drain()
                pool.wait_ge(s["hrow_done"], LN_MOE * NT + NT)
                for h in range(NHALF):
                    add_bias(h, 2)
                part_ends(pool, "gpsimd")

        @block.sync
        def _(sp):
            dma = nc.sync.dma_start
            for dst, src in ((zT[:, :], d["zT"]), (fw1[:, :], d["L0_attn_mlp_w1"]), (fw23[:, 0, :], d["L0_attn_mlp_w2"]),
                             (fw23[:, 1, :], d["L0_attn_mlp_w3"]), (fwo[:, :], d["L0_attn_mlp_wo"]),
                             (fb[:, 0:1], d["L0_attn_mlp_b1"]), (fb[:, 1:2], d["L0_attn_mlp_b2"]),
                             (fb[:, 2:3], d["L0_attn_mlp_b3"]), (fb[:, 3:4], d["L0_attn_freq"])):
                dma(dst, src, allow_slow_non_contiguous=True).then_inc(s["loaded_filter"], 16)
            dma(cT[:, :, :, :], d["cT"], allow_slow_non_contiguous=True).then_inc(s["loaded_c"], 16)
            dma(wraw[:, :, :], d["wmod0"]).then_inc(s["loaded_raw"], 16)
            for dst, src in ((decay[:, :, :], d["decay"]), (fwd[:, :, :], d["fwd"][:, 0]),
                             (fwd_old[:, :, :], d["fwd"][:, 1])):
                dma(dst, src).then_inc(s["loaded_windows"], 16)
            banks["setup"].wait(sp, ("gate", 0))
            dma(wraw[:, :, :], d["wmod1"]).then_inc(s["loaded_raw"], 16)
            w1T = x[:, :, :].rearrange("p t n -> p (t n)")
            loads = [(w1T, d["w1T"].rearrange("p q n -> p (q n)")), (w2T[:, :, :], d["w2T"]),
                     (w1rows[:, :, :], d["L0_ffn_w1"]), (wr_raw[:, :, :], d["wr"]),
                     (inv[:, :, :], d["inv"]), (out_w[:, :, :], d["out_w"]),
                     (wo[:, :, :], d["wo"]), (rope[:, :, :, :], d["rope"]),
                     (br[:, :], d["L1_ffn_br"]), (in_b[:, :], d["in_b"]),
                     (short_w[:, :, :], d["short_w"]), (short_b[:, :], d["short_b"]), (filt_b[:, :], d["filt_b"]),
                     (ffn_b1[:, :], d["ffn_b1"]), (rows[:, 0, :], d["L0_attn_out_b"].partition_broadcast(P)),
                     (rows[:, 1, :], d["L0_ffn_b2"].partition_broadcast(P))]
            assert len(loads) == NLOADED
            for dst, src in loads:
                dma(dst, src, allow_slow_non_contiguous=True).then_inc(s["loaded"], 16)
            banks["setup"].wait(sp, ("gate", 1))
            dma(wraw[:, :, 0:INNER], d["in_w"]).then_inc(s["loaded_raw"], 16)
            sp.wait_ge(s["gate_rows"], 2)
            dma(gate_scratch, grow[:, :, :].rearrange("b l n -> b (l n)")).then_inc(s["gate_stored"], 16)
            sp.wait_ge(s["sgn_done"], 1)
            dma(x[:, :, :], d["x"][0].rearrange("(t p) n -> p t n", p=P)).then_inc(s["x_loaded"], 16)
            sp.wait_ge(s["raw_used"], 1)
            dma(wraw[:, :, :], d["wqkv"].rearrange("p q g n -> p q (g n)")).then_inc(s["loaded_raw"], 16)
            flat = {n: t for n, t in (("in_w", in_w[:, :, :, :].rearrange("p a q n -> p (a q n)")),
                                      ("sgn1", sgn1[:, :, :].rearrange("p q n -> p (q n)")),
                                      ("sgn2", sgn2[:, :, :].rearrange("p q n -> p (q n)")))}
            sp.wait_ge(s["sgn_done"], 2)
            for n in flat:
                dma(scratch[n], flat[n].bitcast(F32)).then_inc(weights_stored, 16)
            sp.wait_ge(s["kf_done"], 1)
            dma(kf_scratch, Kf[:, :, :, :, :].rearrange("p m c f n -> p (m c f n)")).then_inc(weights_stored, 16)
            sp.wait_ge(s["gate_stored"], 16)

            def clear():
                sp.wait_ge(bar, 4)
                sp.sem_clear(range(nums[0], nums[-1] + 1))
                sp.sem_clear(bar)
                for e in go:
                    sp.sem_inc(go[e], 1)

            clear()
            sp.sem_inc(stored, 16)
            with sp.Fori(0, B) as bi:
                sp.wait_ge(stored, 16)
                sp.sem_clear(stored)
                dma(x[:, :, :], d["x"][bass.ds(bi, 1), :, :].rearrange("a (t p) n -> p (a t) n", p=P))\
                    .then_inc(s["x_loaded"], 16)
                dma(gates[:, :, :].rearrange("p k n -> p (k n)"),
                    gate_scratch[bass.ds(bi, 1), :].broadcast_to([P, 4 * D])).then_inc(s["gates_loaded"], 16)
                for u in range(HEADS):
                    sp.wait_ge(s["nmr_done"], u + 1)
                    if u >= QRING:
                        banks["batch"].wait(sp, ("pv", u - QRING, 1))
                    dma(q2[HD:HD + 1, u % QRING, :].bitcast(F32), nmr[:, u % 2, :].bitcast(F32))\
                        .then_inc(m_loaded(u)[0], 16)
                sp.wait_ge(s["top_done"], 1)
                chosen = [bass.ds(nc.sync.value_load(topi[0:1, k:k + 1], min_val=0, max_val=EXPERTS - 1), 1)
                          for k in range(TOPK)]
                for k, one in enumerate(chosen):
                    dma(w1e[:, k, :, :], d["W1"][one].rearrange("e p q n -> p (e q) n")).then_inc(s[f"w1_loaded{k}"], 16)
                for k, one in enumerate(chosen):
                    for dst, src in ((w2e[:, k, :, :], d["W2"][one].rearrange("e p q n -> p (e q) n")),
                                     (b1e[:, k, :], d["b1"][one].rearrange("e p q -> p (e q)")),
                                     (b2e[:, k, :], d["b2"][one, :].broadcast_to([P, D]))):
                        dma(dst, src, allow_slow_non_contiguous=True).then_inc(s[f"expert_loaded{k}"], 16)
                dma(xn[:, :, :], d["x"][bass.ds((bi + 1) % B, 1), :, :].rearrange("a (t p) n -> p (a t) n", p=P))\
                    .then_inc(s["x_next_loaded"], 16)
                banks["batch"].wait(sp, ("out1", NT - 2))
                sp.wait_ge(weights_stored, 16 * 4)
                for dst, src in ([(flat[n].bitcast(F32), scratch[n]) for n in flat]
                                 + [(Kf[:, :, :, :, :].rearrange("p m c f n -> p (m c f n)"), kf_scratch),
                                    (out_w[:, :, :], d["out_w"]), (fwd[:, :, :], d["fwd"][:, 0]),
                                    (inv[:, :, :], d["inv"])]):
                    dma(dst, src).then_inc(s["l0_loaded"], 16)
                sp.wait_ge(s["l0_loaded"], 16 * 7)
                sp.wait_ge(s["x_done"], 1)
                dma(out[bass.ds(bi, 1), :, :].rearrange("a (t p) n -> p (a t) n", p=P), x[:, :, :])\
                    .then_inc(stored, 16)
                clear()
            sp.wait_ge(stored, 16)


INPUTS = ["L0_attn_mlp_w1", "L0_attn_mlp_w2", "L0_attn_mlp_w3", "L0_attn_mlp_wo"]


def layouts(v):
    g = {n: np.ascontiguousarray(v[n]) for n in v}
    tiles = lambda a, n: np.ascontiguousarray(a.reshape(n, P, -1).transpose(1, 0, 2))
    cols = lambda a: np.ascontiguousarray(a.reshape(-1, P).T)
    o = {"x": g["L0_attn_u"]}
    for n in INPUTS:
        o[n] = g[n]
    for n in ("L0_attn_mlp_b1", "L0_attn_mlp_b2", "L0_attn_mlp_b3", "L0_attn_freq"):
        o[n] = g[n].reshape(FILT, 1)
    o["L0_ffn_w1"] = tiles(g["L0_ffn_w1"], NH1)
    o["w1T"] = tiles(np.ascontiguousarray(g["L0_ffn_w1"].T), ND)
    o["w2T"] = tiles(np.ascontiguousarray(g["L0_ffn_w2"].T), NH1)
    o["in_w"] = tiles(g["L0_attn_in_w"], ND)
    o["out_w"] = tiles(g["L0_attn_out_w"], ND)
    o["wo"] = tiles(g["L1_attn_Wo"], HEADS * HD // P)
    o["wr"] = tiles(g["L1_ffn_Wr"], ND)
    o["L1_ffn_br"] = g["L1_ffn_br"].reshape(1, EXPERTS)
    o["in_b"] = cols(g["L0_attn_in_b"])
    o["short_w"] = tiles(g["L0_attn_short_w"], INNER // P)
    o["short_b"] = cols(g["L0_attn_short_b"])
    o["filt_b"] = cols(g["L0_attn_filt_bias"])
    o["ffn_b1"] = cols(g["L0_ffn_b1"])
    o["L0_attn_out_b"] = g["L0_attn_out_b"]
    o["L0_ffn_b2"] = g["L0_ffn_b2"]
    halves = lambda w, n: w.reshape(D, n, HD // 2, 2).transpose(0, 1, 3, 2).reshape(D, n, HD)
    q = halves(g["L1_attn_Wq"], HEADS).reshape(D, KV, GQ, HD)
    k = halves(g["L1_attn_Wk"], KV)[:, :, None]
    val = g["L1_attn_Wv"].reshape(D, KV, 1, HD)
    o["wqkv"] = np.ascontiguousarray(np.concatenate([q, k, val], axis=2).reshape(ND, P, KV, GW).transpose(1, 0, 2, 3))
    o["W1"] = np.ascontiguousarray(g["L1_ffn_W1"].reshape(EXPERTS, ND, P, D).transpose(0, 2, 1, 3))
    o["W2"] = np.ascontiguousarray(g["L1_ffn_W2"].reshape(EXPERTS, ND, P, D).transpose(0, 2, 1, 3))
    o["b1"] = np.ascontiguousarray(g["L1_ffn_b1"].reshape(EXPERTS, ND, P).transpose(0, 2, 1))
    o["b2"] = g["L1_ffn_b2"]
    o["cT"] = np.ascontiguousarray(np.stack([g["L0_c"].T, g["L1_c"].T]).reshape(2, ND, P, B).transpose(2, 0, 1, 3))
    o["wmod0"] = tiles(g["L0_wmod"], ND)
    o["wmod1"] = tiles(g["L1_wmod"], ND)
    return o


def kernel(**inputs):
    import concourse.bacc as bacc
    from concourse.bass_utils import run_bass_kernel_spmd

    arrays = layouts({n: np.asarray(a) for n, a in inputs.items()})
    arrays.update(shape_constants())
    nc = bacc.Bacc("TRN2", target_bir_lowering=False, num_devices=1)
    d = {n: nc.dram_tensor(f"in_{n}", a.shape, mybir.dt.from_np(a.dtype), kind="ExternalInput").ap()
         for n, a in arrays.items()}
    out = nc.dram_tensor("out", (B, L, D), F32, kind="ExternalOutput").ap()
    gate_scratch = nc.dram_tensor("gate_scratch", (B, 4 * D), F32, kind="Internal").ap()
    kf_scratch = nc.dram_tensor("kf_scratch", (P, NB * 2 * ST * D), F32, kind="Internal").ap()
    scratch = {n: nc.dram_tensor(f"{n}_scratch", (P, w), F32, kind="Internal").ap()
               for n, w in (("in_w", 2 * ND * INNER), ("sgn1", ND * HID), ("sgn2", NH1 * D))}
    adaln_hyena_binffn_gqa_moe(nc, d, out, gate_scratch, kf_scratch, scratch)
    r = run_bass_kernel_spmd(nc, [{f"in_{n}": a for n, a in arrays.items()}], core_ids=[0])
    return r.results[0]["out"]
```
